# Optimizing a Trainium2 kernel written in Bass

```python
import numpy as np
import jax
import jax.numpy as jnp

def _softmax(x, axis=-1):
    return jax.nn.softmax(x, axis=axis)

def _gelu(x):
    return jax.nn.gelu(x, approximate=True)

def _silu(x):
    return jax.nn.silu(x)

def _sigmoid(x):
    return jax.nn.sigmoid(x)

def _layernorm(x, axis=-1, eps=1e-05):
    m = jnp.mean(x, axis=axis, keepdims=True)
    v = jnp.var(x, axis=axis, keepdims=True)
    return (x - m) / jnp.sqrt(v + eps)

def _scatter_add(tgt, idx, src, axis=0):
    return tgt.at[idx].add(src)

def _segment_sum(src, seg, n):
    return jax.ops.segment_sum(src, seg, n)
kernel_name = 'mk_adaln_d1_jaxref_r8_9fcaeb'

def setup_inputs(seed: int=0):
    np.random.seed(seed)
    _w = jnp.asarray

    def _L0_attn_setup():
        import jax, jax.numpy as jnp
        import numpy as np
        from jax import lax
        DIM = 128
        EXPAND = 2
        D_STATE = 16
        D_CONV = 4
        DT_RANK = 64
        DIM_INNER = DIM * EXPAND
        B_SZ, SEQ = (2, 128)

        def _mamba_forward(x, W_in, conv_w, conv_b, W_x, W_dt, b_dt, A_log, D, W_out):
            b, l, d = x.shape
            di = W_out.shape[0]
            n = A_log.shape[1]
            dt_rank = W_dt.shape[0]
            x_and_res = x @ W_in
            u, res = jnp.split(x_and_res, 2, axis=-1)
            pad = conv_w.shape[1] - 1
            up = jnp.pad(u, ((0, 0), (pad, 0), (0, 0)))
            kernel = conv_w.T[:, None, :]
            u = lax.conv_general_dilated(up, kernel, window_strides=(1,), padding='VALID', dimension_numbers=('NWC', 'WIO', 'NWC'), feature_group_count=di) + conv_b
            u = jax.nn.silu(u)
            x_dbl = u @ W_x
            delta_r, Bm, Cm = jnp.split(x_dbl, [dt_rank, dt_rank + n], axis=-1)
            delta = jax.nn.softplus(delta_r @ W_dt + b_dt)
            A = -jnp.exp(A_log)
            deltaA = jnp.exp(jnp.einsum('bld,dn->bldn', delta, A))
            deltaB_u = jnp.einsum('bld,bln,bld->bldn', delta, Bm, u)

            def step(h, inp):
                dA_t, dBu_t, c_t = inp
                h = dA_t * h + dBu_t
                y_t = jnp.einsum('bdn,bn->bd', h, c_t)
                return (h, y_t)
            h0 = jnp.zeros((b, di, n), dtype=u.dtype)
            xs = (jnp.moveaxis(deltaA, 1, 0), jnp.moveaxis(deltaB_u, 1, 0), jnp.moveaxis(Cm, 1, 0))
            _, ys = lax.scan(step, h0, xs)
            y = jnp.moveaxis(ys, 0, 1)
            y = y + u * D
            y = y * jax.nn.silu(res)
            return y @ W_out
        key = jax.random.key(seed)
        ks = jax.random.split(key, 8)
        s = lambda fan_in: 1.0 / np.sqrt(fan_in)
        x = jax.random.normal(ks[0], (B_SZ, SEQ, DIM), dtype=jnp.float32)
        W_in = jax.random.normal(ks[1], (DIM, 2 * DIM_INNER), dtype=jnp.float32) * s(DIM)
        conv_w = jax.random.normal(ks[2], (DIM_INNER, D_CONV), dtype=jnp.float32) * s(D_CONV)
        conv_b = jax.random.normal(ks[3], (DIM_INNER,), dtype=jnp.float32) * s(D_CONV)
        W_x = jax.random.normal(ks[4], (DIM_INNER, DT_RANK + 2 * D_STATE), dtype=jnp.float32) * s(DIM_INNER)
        W_dt = jax.random.normal(ks[5], (DT_RANK, DIM_INNER), dtype=jnp.float32) * s(DT_RANK)
        b_dt = jax.random.normal(ks[6], (DIM_INNER,), dtype=jnp.float32) * s(DT_RANK)
        A_log = jnp.broadcast_to(jnp.log(jnp.arange(1, D_STATE + 1, dtype=jnp.float32)), (DIM_INNER, D_STATE))
        D = jnp.ones((DIM_INNER,), dtype=jnp.float32)
        W_out = jax.random.normal(ks[7], (DIM_INNER, DIM), dtype=jnp.float32) * s(DIM_INNER)
        return {'x': x, 'W_in': W_in, 'conv_w': conv_w, 'conv_b': conv_b, 'W_x': W_x, 'W_dt': W_dt, 'b_dt': b_dt, 'A_log': A_log, 'D': D, 'W_out': W_out}
    _L0_attn_in = _L0_attn_setup()

    def _L0_ffn_setup():
        import jax, jax.numpy as jnp
        import numpy as np
        DIM = 128
        DEPTH = 2
        HEADS = 8
        DIM_HEAD = 64
        WINDOW = 64
        INNER = HEADS * DIM_HEAD
        HID = int(DIM * 4 * 2 / 3)
        B, N = (2, 1024)
        QK_SCALE = 8.0

        def shift_token(t):
            t1, t2 = jnp.split(t, 2, axis=-1)
            t2 = jnp.pad(t2, ((0, 0), (1, 0), (0, 0)))[:, :-1]
            return jnp.concatenate([t1, t2], axis=-1)

        def l2norm(t):
            return t / jnp.clip(jnp.linalg.norm(t, axis=-1, keepdims=True), 1e-12)

        def rotate_half(x):
            x1, x2 = jnp.split(x, 2, axis=-1)
            return jnp.concatenate([-x2, x1], axis=-1)

        def rotary_xpos(q, k):
            n = q.shape[-2]
            half_idx = jnp.arange(0, DIM_HEAD, 2, dtype=jnp.float32)
            inv_freq = 1.0 / 10000.0 ** (half_idx / DIM_HEAD)
            t = jnp.arange(n, dtype=jnp.float32)
            freqs = t[:, None] * inv_freq[None, :]
            freqs = jnp.concatenate([freqs, freqs], axis=-1)
            base = (half_idx + 0.4 * DIM_HEAD) / (1.4 * DIM_HEAD)
            power = (t - n // 2) / float(WINDOW // 2)
            scale = base[None, :] ** power[:, None]
            scale = jnp.concatenate([scale, scale], axis=-1)
            cos, sin = (jnp.cos(freqs), jnp.sin(freqs))
            q = q * cos * scale + rotate_half(q) * sin * scale
            k = k * cos / scale + rotate_half(k) * sin / scale
            return (q, k)

        def local_attention(q, k, v):
            b, h, n, d = q.shape
            w = n // WINDOW
            bq = q.reshape(b, h, w, WINDOW, d) * QK_SCALE
            bk = k.reshape(b, h, w, WINDOW, d)
            bv = v.reshape(b, h, w, WINDOW, d)

            def look_around(t):
                p = jnp.pad(t, ((0, 0), (0, 0), (1, 0), (0, 0), (0, 0)))
                return jnp.concatenate([p[:, :, :w], p[:, :, 1:]], axis=3)
            bk, bv = (look_around(bk), look_around(bv))
            bt = jnp.arange(n).reshape(w, WINDOW)
            btp = jnp.pad(bt, ((1, 0), (0, 0)), constant_values=-1)
            btk = jnp.concatenate([btp[:w], btp[1:]], axis=1)
            sim = jnp.einsum('bhwid,bhwjd->bhwij', bq, bk)
            i = bt[:, :, None]
            j = btk[:, None, :]
            mask = (i < j) | (i > j + WINDOW) | (j == -1)
            sim = jnp.where(mask, -jnp.finfo(sim.dtype).max, sim)
            attn = jax.nn.softmax(sim, axis=-1)
            out = jnp.einsum('bhwij,bhwjd->bhwid', attn, bv)
            return out.reshape(b, h, n, d)

        def _layer(x, wqkv, qs, ksc, wo, lg, lb, w1, b1, w2, b2):
            b, n, _ = x.shape
            h = shift_token(x)
            qkv = h @ wqkv
            q, k, v = jnp.split(qkv, 3, axis=-1)
            to_heads = lambda t: t.reshape(b, n, HEADS, DIM_HEAD).transpose(0, 2, 1, 3)
            q, k, v = (to_heads(q), to_heads(k), to_heads(v))
            q = l2norm(q) * qs
            k = l2norm(k) * ksc
            q, k = rotary_xpos(q, k)
            o = local_attention(q, k, v)
            o = o.transpose(0, 2, 1, 3).reshape(b, n, INNER)
            x = x + o @ wo
            h = shift_token(x)
            mu = h.mean(-1, keepdims=True)
            var = h.var(-1, keepdims=True)
            h = (h - mu) / jnp.sqrt(var + 1e-05) * lg + lb
            h = h @ w1 + b1
            a, g = jnp.split(h, 2, axis=-1)
            h = a * jax.nn.gelu(g, approximate=False)
            x = x + h @ w2 + b2
            return x
        key = jax.random.key(seed)
        ks = jax.random.split(key, 6)
        return {'x': jax.random.normal(ks[0], (B, N, DIM), jnp.float32), 'wqkv': jax.random.normal(ks[1], (DEPTH, DIM, 3 * INNER), jnp.float32) * 0.02, 'q_scale': jnp.ones((DEPTH, DIM_HEAD), jnp.float32), 'k_scale': jnp.ones((DEPTH, DIM_HEAD), jnp.float32), 'wo': jax.random.normal(ks[2], (DEPTH, INNER, DIM), jnp.float32) * 0.02, 'ln_g': jnp.ones((DEPTH, DIM), jnp.float32), 'ln_b': jnp.zeros((DEPTH, DIM), jnp.float32), 'w1': jax.random.normal(ks[3], (DEPTH, DIM, 2 * HID), jnp.float32) * 0.02, 'b1': jnp.zeros((DEPTH, 2 * HID), jnp.float32), 'w2': jax.random.normal(ks[4], (DEPTH, HID, DIM), jnp.float32) * 0.02, 'b2': jnp.zeros((DEPTH, DIM), jnp.float32)}
    _L0_ffn_in = _L0_ffn_setup()
    _L0_c = _w((lambda *s: np.random.randn(*s).astype(np.float32) * 0.05)(32, 128))
    _L0_wmod = _w((lambda *s: np.random.randn(*s).astype(np.float32) * 0.05)(128, 6 * 128) * 128 ** (-0.5))
    _d = {'L0_attn_x': _L0_attn_in['x'], 'L0_attn_W_in': _L0_attn_in['W_in'], 'L0_attn_conv_w': _L0_attn_in['conv_w'], 'L0_attn_conv_b': _L0_attn_in['conv_b'], 'L0_attn_W_x': _L0_attn_in['W_x'], 'L0_attn_W_dt': _L0_attn_in['W_dt'], 'L0_attn_b_dt': _L0_attn_in['b_dt'], 'L0_attn_A_log': _L0_attn_in['A_log'], 'L0_attn_D': _L0_attn_in['D'], 'L0_attn_W_out': _L0_attn_in['W_out'], 'L0_ffn_wqkv': _L0_ffn_in['wqkv'], 'L0_ffn_q_scale': _L0_ffn_in['q_scale'], 'L0_ffn_k_scale': _L0_ffn_in['k_scale'], 'L0_ffn_wo': _L0_ffn_in['wo'], 'L0_ffn_ln_g': _L0_ffn_in['ln_g'], 'L0_ffn_ln_b': _L0_ffn_in['ln_b'], 'L0_ffn_w1': _L0_ffn_in['w1'], 'L0_ffn_b1': _L0_ffn_in['b1'], 'L0_ffn_w2': _L0_ffn_in['w2'], 'L0_ffn_b2': _L0_ffn_in['b2'], 'L0_c': _L0_c, 'L0_wmod': _L0_wmod}
    _x0 = _d['L0_attn_x']
    _d['L0_attn_x'] = jax.random.normal(jax.random.fold_in(jax.random.key(seed), 1), (32, 256, 128), dtype=_x0.dtype)
    del _x0
    return _d

def reference(L0_attn_x, L0_attn_W_in, L0_attn_conv_w, L0_attn_conv_b, L0_attn_W_x, L0_attn_W_dt, L0_attn_b_dt, L0_attn_A_log, L0_attn_D, L0_attn_W_out, L0_ffn_wqkv, L0_ffn_q_scale, L0_ffn_k_scale, L0_ffn_wo, L0_ffn_ln_g, L0_ffn_ln_b, L0_ffn_w1, L0_ffn_b1, L0_ffn_w2, L0_ffn_b2, L0_c, L0_wmod):

    def _L0_attn_ref(x, W_in, conv_w, conv_b, W_x, W_dt, b_dt, A_log, D, W_out):
        import jax, jax.numpy as jnp
        import numpy as np
        from jax import lax
        DIM = 128
        EXPAND = 2
        D_STATE = 16
        D_CONV = 4
        DT_RANK = 64
        DIM_INNER = DIM * EXPAND
        B_SZ, SEQ = (2, 128)

        def _mamba_forward(x, W_in, conv_w, conv_b, W_x, W_dt, b_dt, A_log, D, W_out):
            b, l, d = x.shape
            di = W_out.shape[0]
            n = A_log.shape[1]
            dt_rank = W_dt.shape[0]
            x_and_res = x @ W_in
            u, res = jnp.split(x_and_res, 2, axis=-1)
            pad = conv_w.shape[1] - 1
            up = jnp.pad(u, ((0, 0), (pad, 0), (0, 0)))
            kernel = conv_w.T[:, None, :]
            u = lax.conv_general_dilated(up, kernel, window_strides=(1,), padding='VALID', dimension_numbers=('NWC', 'WIO', 'NWC'), feature_group_count=di) + conv_b
            u = jax.nn.silu(u)
            x_dbl = u @ W_x
            delta_r, Bm, Cm = jnp.split(x_dbl, [dt_rank, dt_rank + n], axis=-1)
            delta = jax.nn.softplus(delta_r @ W_dt + b_dt)
            A = -jnp.exp(A_log)
            deltaA = jnp.exp(jnp.einsum('bld,dn->bldn', delta, A))
            deltaB_u = jnp.einsum('bld,bln,bld->bldn', delta, Bm, u)

            def step(h, inp):
                dA_t, dBu_t, c_t = inp
                h = dA_t * h + dBu_t
                y_t = jnp.einsum('bdn,bn->bd', h, c_t)
                return (h, y_t)
            h0 = jnp.zeros((b, di, n), dtype=u.dtype)
            xs = (jnp.moveaxis(deltaA, 1, 0), jnp.moveaxis(deltaB_u, 1, 0), jnp.moveaxis(Cm, 1, 0))
            _, ys = lax.scan(step, h0, xs)
            y = jnp.moveaxis(ys, 0, 1)
            y = y + u * D
            y = y * jax.nn.silu(res)
            return y @ W_out
        return _mamba_forward(x, W_in, conv_w, conv_b, W_x, W_dt, b_dt, A_log, D, W_out)

    def _L0_ffn_ref(x, wqkv, q_scale, k_scale, wo, ln_g, ln_b, w1, b1, w2, b2):
        import jax, jax.numpy as jnp
        import numpy as np
        DIM = 128
        DEPTH = 2
        HEADS = 8
        DIM_HEAD = 64
        WINDOW = 64
        INNER = HEADS * DIM_HEAD
        HID = int(DIM * 4 * 2 / 3)
        B, N = (2, 1024)
        QK_SCALE = 8.0

        def shift_token(t):
            t1, t2 = jnp.split(t, 2, axis=-1)
            t2 = jnp.pad(t2, ((0, 0), (1, 0), (0, 0)))[:, :-1]
            return jnp.concatenate([t1, t2], axis=-1)

        def l2norm(t):
            return t / jnp.clip(jnp.linalg.norm(t, axis=-1, keepdims=True), 1e-12)

        def rotate_half(x):
            x1, x2 = jnp.split(x, 2, axis=-1)
            return jnp.concatenate([-x2, x1], axis=-1)

        def rotary_xpos(q, k):
            n = q.shape[-2]
            half_idx = jnp.arange(0, DIM_HEAD, 2, dtype=jnp.float32)
            inv_freq = 1.0 / 10000.0 ** (half_idx / DIM_HEAD)
            t = jnp.arange(n, dtype=jnp.float32)
            freqs = t[:, None] * inv_freq[None, :]
            freqs = jnp.concatenate([freqs, freqs], axis=-1)
            base = (half_idx + 0.4 * DIM_HEAD) / (1.4 * DIM_HEAD)
            power = (t - n // 2) / float(WINDOW // 2)
            scale = base[None, :] ** power[:, None]
            scale = jnp.concatenate([scale, scale], axis=-1)
            cos, sin = (jnp.cos(freqs), jnp.sin(freqs))
            q = q * cos * scale + rotate_half(q) * sin * scale
            k = k * cos / scale + rotate_half(k) * sin / scale
            return (q, k)

        def local_attention(q, k, v):
            b, h, n, d = q.shape
            w = n // WINDOW
            bq = q.reshape(b, h, w, WINDOW, d) * QK_SCALE
            bk = k.reshape(b, h, w, WINDOW, d)
            bv = v.reshape(b, h, w, WINDOW, d)

            def look_around(t):
                p = jnp.pad(t, ((0, 0), (0, 0), (1, 0), (0, 0), (0, 0)))
                return jnp.concatenate([p[:, :, :w], p[:, :, 1:]], axis=3)
            bk, bv = (look_around(bk), look_around(bv))
            bt = jnp.arange(n).reshape(w, WINDOW)
            btp = jnp.pad(bt, ((1, 0), (0, 0)), constant_values=-1)
            btk = jnp.concatenate([btp[:w], btp[1:]], axis=1)
            sim = jnp.einsum('bhwid,bhwjd->bhwij', bq, bk)
            i = bt[:, :, None]
            j = btk[:, None, :]
            mask = (i < j) | (i > j + WINDOW) | (j == -1)
            sim = jnp.where(mask, -jnp.finfo(sim.dtype).max, sim)
            attn = jax.nn.softmax(sim, axis=-1)
            out = jnp.einsum('bhwij,bhwjd->bhwid', attn, bv)
            return out.reshape(b, h, n, d)

        def _layer(x, wqkv, qs, ksc, wo, lg, lb, w1, b1, w2, b2):
            b, n, _ = x.shape
            h = shift_token(x)
            qkv = h @ wqkv
            q, k, v = jnp.split(qkv, 3, axis=-1)
            to_heads = lambda t: t.reshape(b, n, HEADS, DIM_HEAD).transpose(0, 2, 1, 3)
            q, k, v = (to_heads(q), to_heads(k), to_heads(v))
            q = l2norm(q) * qs
            k = l2norm(k) * ksc
            q, k = rotary_xpos(q, k)
            o = local_attention(q, k, v)
            o = o.transpose(0, 2, 1, 3).reshape(b, n, INNER)
            x = x + o @ wo
            h = shift_token(x)
            mu = h.mean(-1, keepdims=True)
            var = h.var(-1, keepdims=True)
            h = (h - mu) / jnp.sqrt(var + 1e-05) * lg + lb
            h = h @ w1 + b1
            a, g = jnp.split(h, 2, axis=-1)
            h = a * jax.nn.gelu(g, approximate=False)
            x = x + h @ w2 + b2
            return x
        for l in range(DEPTH):
            x = _layer(x, wqkv[l], q_scale[l], k_scale[l], wo[l], ln_g[l], ln_b[l], w1[l], b1[l], w2[l], b2[l])
        return x
    x = L0_attn_x
    mod = (_silu(L0_c) @ L0_wmod).reshape(L0_c.shape[0], 6, 1, -1)
    sa, ca, ga, sb, cb, gb = (mod[:, 0], mod[:, 1], mod[:, 2], mod[:, 3], mod[:, 4], mod[:, 5])
    ga = (2 * (ga >= 0) - 1) * jnp.maximum(jnp.abs(ga), 0.25)
    gb = (2 * (gb >= 0) - 1) * jnp.maximum(jnp.abs(gb), 0.25)
    h = _layernorm(x, axis=-1) * (1 + ca) + sa
    x = x + ga * _L0_attn_ref(h, L0_attn_W_in, L0_attn_conv_w, L0_attn_conv_b, L0_attn_W_x, L0_attn_W_dt, L0_attn_b_dt, L0_attn_A_log, L0_attn_D, L0_attn_W_out)
    h = _layernorm(x, axis=-1) * (1 + cb) + sb
    x = x + gb * _L0_ffn_ref(h, L0_ffn_wqkv, L0_ffn_q_scale, L0_ffn_k_scale, L0_ffn_wo, L0_ffn_ln_g, L0_ffn_ln_b, L0_ffn_w1, L0_ffn_b1, L0_ffn_w2, L0_ffn_b2)
    return x

_drawn_inputs = setup_inputs


def setup_inputs(seed=0):
    import zlib

    import numpy as np

    out = dict(_drawn_inputs(seed))
    spreads = {'L0_attn_D': (1.0, 0.6),
     'L0_ffn_q_scale': (1.0, 0.6),
     'L0_ffn_k_scale': (1.0, 0.6),
     'L0_ffn_ln_g': (1.0, 0.6),
     'L0_ffn_ln_b': (0.0, 0.8),
     'L0_ffn_b1': (0.0, 0.8),
     'L0_ffn_b2': (0.0, 0.762)}
    factors = {'L0_attn_b_dt': 3.866,
     'L0_ffn_wqkv': 7.083,
     'L0_ffn_wo': 7.089,
     'L0_ffn_w1': 8.0,
     'L0_ffn_w2': 8.0}
    for name, (base, spread) in spreads.items():
        noise = np.random.default_rng([zlib.crc32(name.encode()), seed]).standard_normal(out[name].shape)
        drawn = base * np.exp(spread * noise) if base else spread * noise
        out[name] = jnp.asarray(drawn.astype(out[name].dtype))
    for name, factor in factors.items():
        out[name] = (out[name] * factor).astype(out[name].dtype)
    return out
```

```python
import concourse.bass as bass
import numpy as np
from concourse import mybir
from contextlib import ExitStack

FP32 = mybir.dt.float32
BF16 = mybir.dt.bfloat16
ALU = mybir.AluOpType
ACT = mybir.ActivationFunctionType
AX = mybir.AxisListType

BATCH, SEQ, DIM = 32, 256, 128
INNER = 256
HALVES = INNER // 128
STATE = 16
TAPS = 4
RING = 4
RANK = 64
DEPTH = 2
HEADS, DH = 8, 64
WINDOW = 64
QKV = HEADS * DH
HID = 341
HID_BLOCKS = [(0, 128), (128, 128), (256, HID - 256)]
TOK = 512
PAIRS = BATCH // 2
QK_SCALE = 8.0
MASKED = -1.0e30
EPS = 1e-5

CREDIT = 4


def shape_constants():
    ident = np.eye(128, dtype=np.float32)
    center = (ident - np.float32(1.0 / 128)).astype(np.float32)
    sel = np.zeros((96, 32, 128), np.float32)
    for n in range(32):
        for part in range(3):
            sel[32 * part + n, n, :] = 1.0
    i = np.arange(128)[:, None]
    j = np.arange(128)[None, :]
    near = i - j
    far = WINDOW + (i % WINDOW) - j
    mask = np.stack([np.where((d >= 0) & (d <= WINDOW), 0.0, MASKED) for d in (near, far)], 1)
    half = np.arange(0, DH, 2, dtype=np.float32)
    inv = (np.float32(1.0) / np.float32(10000.0) ** (half / np.float32(DH))).astype(np.float32)
    t = np.arange(SEQ, dtype=np.float32)
    freqs = t[:, None] * inv[None, :]
    freqs = np.concatenate([freqs, freqs], -1).astype(np.float32)
    base = ((half + np.float32(0.4 * DH)) / np.float32(1.4 * DH)).astype(np.float32)
    power = ((t - SEQ // 2) / np.float32(WINDOW // 2)).astype(np.float32)
    scale = (base[None, :] ** power[:, None]).astype(np.float32)
    scale = np.concatenate([scale, scale], -1)
    sign = np.where(np.arange(DH) < DH // 2, -1.0, 1.0).astype(np.float32)
    cos, sin = np.cos(freqs), np.sin(freqs) * sign
    rope = np.stack([cos * scale, sin * scale, cos / scale, sin / scale], 1).astype(np.float32)
    rope = rope.reshape(2, 128, 4, DH).transpose(1, 0, 2, 3)
    return {
        "c_ident": ident, "c_center": center, "c_sel": sel.reshape(96, 32 * 128),
        "c_mask": mask.astype(np.float32).reshape(128, 256),
        "c_rope": np.ascontiguousarray(rope).reshape(128, 2 * 4 * DH),
    }


def ev(count):
    return count + CREDIT


def block_kernel(nc, a, out):
    ctx = ExitStack()
    with ctx:
        def sb(name, shape, dt=FP32):
            return ctx.enter_context(nc.sbuf_tensor(name, shape, dt))

        def sem(name):
            return ctx.enter_context(nc.semaphore(name))

        loop_sems = []

        def event(name):
            loop_sems.append(sem(name))
            return loop_sems[-1]

        ident = sb("ident", [128, 128])
        identb = sb("identb", [128, 128], BF16)
        center = sb("center", [128, 128])
        mean_w = sb("mean_w", [128, 128])
        sel = sb("sel", [96, 32, 128], BF16)
        mask = sb("mask", [128, 2, 128], BF16)
        tables = sb("tables", [128, DEPTH, 2, 4, DH])
        w_in = sb("w_in", [128, 2 * INNER])
        conv_w = sb("conv_w", [128, HALVES, TAPS])
        conv_b = sb("conv_b", [128, HALVES])
        w_x = sb("w_x", [128, HALVES, RANK + 2 * STATE])
        w_dt = sb("w_dt", [RANK, INNER])
        b_dt = sb("b_dt", [128, HALVES])
        a_neg = sb("a_neg", [128, HALVES, STATE])
        skip_d = sb("skip_d", [128, HALVES])
        w_out = sb("w_out", [128, HALVES, DIM])
        wqkv = sb("wqkv", [128, DEPTH, 3 * QKV])
        wo = sb("wo", [128, DEPTH, 4, DIM])
        ln_g = sb("ln_g", [128, DEPTH])
        ln_b = sb("ln_b", [128, DEPTH])
        w1 = sb("w1", [128, DEPTH, 2 * HID])
        b1 = sb("b1", [128, DEPTH, 2, 3])
        w2 = sb("w2", [128, DEPTH, 3, DIM])
        b2 = sb("b2", [128, DEPTH])
        eps = sb("eps", [128, 1])
        power = sb("power", [128, 2 * HEADS])
        mod = sb("mod", [128, 6, BATCH])

        x1 = sb("x1", [128, BATCH * SEQ])
        xf = sb("xf", [128, BATCH * SEQ])

        psum = [ctx.enter_context(nc.psum_tensor(f"bank{i}", [128, 512], FP32)) for i in range(8)]

        s_w = sem("s_w")
        s_cast = sem("s_cast")
        s_mod = sem("s_mod")
        s_set_act = sem("s_set_act")
        s_set_dve = sem("s_set_dve")
        s_set_pool = sem("s_set_pool")
        s_x = [event("s_x0"), event("s_x1")]
        s_out = [event("s_out0"), event("s_out1")]

        SET_DVE = 10
        x_rows = a["x"].rearrange("b s d -> (b s) d")
        out_rows = out.rearrange("b s d -> (b s) d")

        with ExitStack() as s_ctx:
            def ssb(name, shape):
                return s_ctx.enter_context(nc.sbuf_tensor(name, shape, FP32))

            rope = ssb("rope", [128, 2, 4, DH])
            qks = ssb("qks", [128, DEPTH, 2, DH])
            cond = ssb("cond", [32, DIM])
            wmod = ssb("wmod", [128, 6 * DIM])
            condT = ssb("condT", [128, BATCH])
            gate_abs = ssb("gate_abs", [128, 2, BATCH])
            gate_sign = ssb("gate_sign", [128, 2, BATCH])
        m_ctx = ExitStack()

        def msb(name, shape, dt=FP32):
            return m_ctx.enter_context(nc.sbuf_tensor(name, shape, dt))

        us = [msb(f"us{i}", [128, HALVES, TOK]) for i in range(2)]
        sr = [msb(f"sr{i}", [128, HALVES, TOK]) for i in range(2)]
        xin = [msb(f"xin{i}", [128, 4, DIM]) for i in range(2)]
        xs = [msb(f"xs{i}", [128, TOK]) for i in range(2)]
        sq = msb("sq", [128, TOK])
        rstd = msb("rstd", [128, TOK])
        hn = msb("hn", [128, TOK])
        h_mod = msb("h_mod", [128, TOK])
        ub = msb("ub", [128, HALVES, 2, TAPS - 1 + SEQ])
        cv = msb("cv", [128, HALVES, 2, SEQ])
        dr_rest = msb("dr_rest", [96, TOK])
        dr, rest = dr_rest[0:RANK, :], dr_rest[64:96, :]
        parts = [msb(f"parts{i}", [96, TOK], BF16) for i in range(2)]
        sp_abs = msb("sp_abs", [128, TOK])
        sp_ln = msb("sp_ln", [128, HALVES, TOK])
        delta = [msb(f"delta{i}", [128, HALVES, TOK]) for i in range(2)]
        du = [msb(f"du{i}", [128, HALVES, TOK]) for i in range(2)]
        dA = [msb(f"dA{i}", [128, HALVES, 2, SEQ]) for i in range(2)]
        hst = [msb(f"hst{i}", [128, HALVES, TOK]) for i in range(RING)]
        cs = [msb(f"cs{i}", [128, TOK]) for i in range(2)]
        z = msb("z", [128, HALVES, TOK])

        WLOADS = [
            (ident[:, :], a["c_ident"]), (center[:, :], a["c_center"]),
            (rope[:, :, :, :], a["c_rope"].rearrange("p (b k d) -> p b k d", b=2, k=4)),
            (w_in[:, :], a["W_in"]),
            (conv_w[:, :, :], a["conv_w"].rearrange("(h p) k -> p h k", p=128)),
            (conv_b[:, :], a["conv_b"].rearrange("(h p) -> p h", p=128)),
            (w_x[:, :, :], a["W_x"].rearrange("(h p) k -> p h k", p=128)),
            (w_dt[:, :], a["W_dt"]),
            (b_dt[:, :], a["b_dt"].rearrange("(h p) -> p h", p=128)),
            (a_neg[:, :, :], a["A_log"].rearrange("(h p) k -> p h k", p=128)),
            (skip_d[:, :], a["D"].rearrange("(h p) -> p h", p=128)),
            (w_out[:, :, :], a["W_out"].rearrange("(h p) k -> p h k", p=128)),
            (wqkv[:, :, :], a["wqkv"].rearrange("l p n -> p l n")),
            (wo[:, :, :, :], a["wo"].rearrange("l (k p) n -> p l k n", p=128)),
            (ln_g[:, :], a["ln_g"].rearrange("l p -> p l")),
            (ln_b[:, :], a["ln_b"].rearrange("l p -> p l")),
            (w1[:, :, :], a["w1"].rearrange("l p n -> p l n")),
            (b2[:, :], a["b2"].rearrange("l p -> p l")),
            (qks[:, :, 0, :], a["q_scale"].partition_broadcast(128)),
            (qks[:, :, 1, :], a["k_scale"].partition_broadcast(128)),
            (w2[:, 0, 0:2, :], a["w2"][0, 0:256, :].rearrange("(k p) n -> p k n", p=128)),
            (w2[:, 1, 0:2, :], a["w2"][1, 0:256, :].rearrange("(k p) n -> p k n", p=128)),
            (w2[0:HID - 256, :, 2, :], a["w2"][:, 256:HID, :].rearrange("l p n -> p l n")),
            (cond[:, :], a["c"]), (wmod[:, :], a["wmod"]),
        ]
        for s in range(2):
            for layer in range(DEPTH):
                at = s * HID
                WLOADS.append((b1[:, layer, s, 0:2],
                               a["b1"][layer, at:at + 256].rearrange("(j p) -> p j", p=128)))
                WLOADS.append((b1[0:HID - 256, layer, s, 2:3],
                               a["b1"][layer, at + 256:at + HID].rearrange("(p j) -> p j", j=1)))
        CASTS = [(sel[:, :, :], a["c_sel"].rearrange("p (n m) -> p n m", n=32)),
                 (mask[:, :, :], a["c_mask"].rearrange("p (t m) -> p t m", t=2)),
                 (identb[:, :], a["c_ident"])]
        ALL_W = 16 * len(WLOADS)
        pA, pB = psum[0], psum[1]
        bB, bC, yp = psum[2:4], psum[4:6], psum[6:8]

        (xT_done, xs_done, cen_done, sq_done, var_done, ln_done, rstd_done, hn_done, h_done,
         u_done, ub_done, res_done, sr_done, conv_step, cv_done, us_done, xdbl_done, dr_done,
         hi_done, rest_done, mid_done, split_done, dt_done, abs_done, exp_done, spl_done, pos_done,
         delta_done, du_done, bcB_done, bcC_done, dA_done, dBu_done, scan_done, cs_done, hc_done,
         y_done, yd_done, z_done, out_done, xn_done, x1_done, cen2_done, sq2_done, var2_done,
         ln2_done, rstd2_done, hn2_done, xf_done) = [event(n) for n in (
             "xT xs cen sq var ln rstd hn h u ub res sr conv cv us xdbl dr hi rest mid split dt abs "
             "exp spl pos delta du bcB bcC dA dBu scan cs hc y yd z out xn x1 cen2 sq2 var2 ln2 "
             "rstd2 hn2 xf").split()]

        block = ctx.enter_context(nc.Block())

        m_ctx.close()
        hf = sb("hf", [128, BATCH * SEQ])
        a_ctx = ExitStack()

        def asb(name, shape, dt=FP32):
            return a_ctx.enter_context(nc.sbuf_tensor(name, shape, dt))

        hT = [asb(f"hT{i}", [128, SEQ]) for i in range(2)]
        sqk = asb("sqk", [128, 2 * QKV])
        ss = asb("ss", [128, 2 * HEADS])
        ssm = asb("ssm", [128, 2 * HEADS])
        rn = [asb(f"rn{i}", [128, 2 * HEADS]) for i in range(2)]
        rq8 = [asb(f"rq8{i}", [128, HEADS]) for i in range(2)]
        rot_a = asb("rot_a", [128, 2, QKV])
        rot_b = asb("rot_b", [128, 2, QKV])
        qkr = asb("qkr", [128, 2, QKV])
        kn = asb("kn", [128, QKV])
        qT = asb("qT", [128, 4, SEQ])
        kT = asb("kT", [128, 4, SEQ])
        vs = asb("vs", [128, 3, HEADS, DH + 1])
        mx = [asb(f"mx{i}", [128, 4]) for i in range(2)]
        nb = [asb(f"nb{i}", [128, 4]) for i in range(2)]
        pr = [asb(f"pr{i}", [128, 4, 128]) for i in range(2)]
        pT = [asb(f"pT{i}", [128, 4, 128]) for i in range(2)]
        rd = [asb(f"rd{i}", [128, 4]) for i in range(2)]
        on = asb("on", [128, QKV])
        oT = asb("oT", [128, 4, SEQ])
        hs = asb("hs", [128, SEQ])
        a_sq = asb("a_sq", [128, SEQ])
        a_ln = asb("a_ln", [128, SEQ])
        a_rstd = asb("a_rstd", [128, SEQ])
        a_hn = asb("a_hn", [128, SEQ])
        front, tb, sc, op = psum[0:2], psum[2:4], psum[4:6], psum[6:8]
        (ht_done, qk_done, sqk_done, ss_done, ssm_done, rn_done, rot_done, add_done, kn_done,
         tq_done, qT_done, kT_done, v_done, vs_done, s_done, mx_done, nb_done, p_done, tp_done,
         pT_done, o_done, rd_done, on_done, to_done, oT_done, wo_done, xr_done, hs_done, ac_done,
         asq_done, avar_done, aln_done, arstd_done, ahn_done, hf_done, rq8_done) = [
             event("a_" + n) for n in (
                 "ht qk sqk ss ssm rn rot add kn tq qT kT v vs s mx nb p tp pT o rd on to oT wo xr "
                 "hs ac asq avar aln arstd ahn hf rq8").split()]
        a_ctx.close()

        f_ctx = ExitStack()

        def fsb(name, shape, dt=FP32):
            return f_ctx.enter_context(nc.sbuf_tensor(name, shape, dt))

        ge = [fsb(f"ge{i}", [128, TOK]) for i in range(2)]
        mid = [fsb(f"mid{i}", [128, TOK]) for i in range(3)]
        fo = fsb("fo", [128, TOK])
        so = [fsb(f"so{i}", [128, 4, DIM]) for i in range(2)]
        gp, ap_, rp, tp = psum[0:2], psum[2:4], psum[4], psum[5]
        (g_done, ge_done, mid_done_f, w2_done, xo_done, fo_done, fT_done, so_done) = [
            event("f_" + n) for n in "g ge mid w2 xo fo fT so".split()]
        f_ctx.close()

        def tokens(buf, pair):
            return buf[:, bass.ds(pair * TOK, TOK)]

        def seqs(buf):
            return buf.rearrange("p (b s) -> p b s", b=2)

        @block.sync
        def _(sp):
            for s in loop_sems:
                sp.sem_inc(s, CREDIT)
            with nc.allow_non_contiguous_dma(reason="short vectors put one element on a partition, once"):
                for dst, src in WLOADS:
                    sp.dma_start(dst, src).then_inc(s_w, 16)
            with sp.Fori(0, PAIRS // 2) as i:
                for par in range(2):
                    pair = 2 * i + par
                    sp.wait_ge(xT_done, ev(pair - 1))
                    sp.dma_start(xin[par][:, :, :],
                                 x_rows[bass.ds(pair * TOK, TOK), :].rearrange("(t p) d -> p t d", p=128)
                                 ).then_inc(s_x[par], 16)
            with sp.Fori(0, PAIRS // 2) as i:
                for par in range(2):
                    pair = 2 * i + par
                    sp.wait_ge(so_done, ev(pair + 1))
                    sp.dma_start(out_rows[bass.ds(pair * TOK, TOK), :].rearrange("(t p) d -> p t d", p=128),
                                 so[par][:, :, :]).then_inc(s_out[par], 16)
            for par in range(2):
                sp.wait_ge(s_out[par], ev(16 * (PAIRS // 2)))

        @block.gpsimd
        def _(pool):
            for dst, src in CASTS:
                pool.dma_start(dst, src).then_inc(s_cast, 16)
            pool.memset(mean_w[:, :], 1.0 / DIM)
            pool.memset(eps[:, :], EPS)
            pool.memset(power[:, :], -0.5)
            pool.memset(ub[:, :, :, :], 0.0)
            pool.memset(dA[0][:, :, :, :], 0.0)
            pool.memset(dA[1][:, :, :, :], 0.0).then_inc(s_set_pool, 1)
            with pool.Fori(0, PAIRS // 2) as i:
                for par in range(2):
                    for n in range(STATE):
                        g = (2 * i + par) * STATE + n
                        r = n % 2
                        pool.wait_ge(scan_done, ev(g + 1))
                        pool.wait_ge(cs_done, ev(g + 1))
                        pool.tensor_tensor(hst[n % RING][:, :, :], hst[n % RING][:, :, :],
                                           cs[r][:, :].unsqueeze(1).broadcast_to([128, HALVES, TOK]),
                                           ALU.mult).then_inc(hc_done, 1)
            pool.wait_ge(xf_done, ev(PAIRS))
            for i in range(2):
                pool.memset(hT[i][:, :], 0.0)
            pool.memset(hs[:, :], 0.0)
            pool.memset(vs[:, :, :, :], 1.0).then_inc(s_set_pool, 1)
            for layer in range(DEPTH):
                if layer:
                    pool.wait_ge(xo_done, ev(PAIRS))
                    pool.memset(hT[0][:, :], 0.0)
                    pool.memset(hT[1][:, :], 0.0)
                    pool.memset(hs[:, :], 0.0)
                    pool.memset(vs[:, :, :, :], 1.0).then_inc(s_set_pool, 1)
                with pool.Fori(0, BATCH) as i:
                    b = i + layer * BATCH
                    for t in range(2):
                        e = b * 2 + t
                        pool.wait_ge(ssm_done, ev(e + 1))
                        pool.wait_ge(s_done, ev(b * 4 - 2 + 2 * t))
                        pool.tensor_tensor(rn[t][:, :], ssm[:, :], power[:, :], ALU.pow).then_inc(rn_done, 1)
                        pool.wait_ge(rot_done, ev(e + 1))
                        pool.wait_ge(tq_done, ev(2 * e))
                        pool.tensor_tensor(qkr[:, :, :], rot_a[:, :, :], rot_b[:, :, :],
                                           ALU.add).then_inc(add_done, 1)
                        pool.wait_ge(add_done, ev(e + 1))
                        pool.wait_ge(rn_done, ev(e + 1))
                        pool.tensor_tensor(kn[:, :].rearrange("p (h d) -> p h d", h=HEADS),
                                           qkr[:, 1, :].rearrange("p (h d) -> p h d", h=HEADS),
                                           rn[t][:, HEADS:].unsqueeze(2).broadcast_to([128, HEADS, DH]),
                                           ALU.mult).then_inc(kn_done, 1)

        @block.scalar
        def _(act):
            act.wait_ge(s_w, ALL_W)
            act.wait_ge(s_mod, 1)
            act.activation(condT[:, :], psum[0][:, 0:BATCH], ACT.Silu).then_inc(s_set_act, 1)
            act.activation(a_neg[:, :, :], a_neg[:, :, :], ACT.Exp).then_inc(s_set_act, 1)
            act.preload_act_table_set("natural_log_exp_and_others")
            act.wait_ge(s_set_pool, 1)
            act.wait_ge(s_set_dve, SET_DVE)
            with act.Fori(0, PAIRS // 2) as i:
                for par in range(2):
                    pair = 2 * i + par
                    act.wait_ge(xT_done, ev(pair + 1))
                    act.wait_ge(x1_done, ev(pair - 1))
                    act.wait_ge(cen2_done, ev(pair - 1))
                    act.activation(xs[par][:, :], pA[:, :], ACT.Copy).then_inc(xs_done, 1)
                    act.wait_ge(cen_done, ev(pair + 1))
                    act.activation(sq[:, :], pB[:, :], ACT.Square).then_inc(sq_done, 1)
                    act.wait_ge(var_done, ev(pair + 1))
                    act.wait_ge(hn2_done, ev(pair))
                    act.activation(rstd[:, :], pA[:, :], ACT.Ln, bias=eps[:, 0:1]).then_inc(ln_done, 1)
                    act.wait_ge(ln_done, ev(pair + 1))
                    act.activation(rstd[:, :], rstd[:, :], ACT.Exp, scale=-0.5).then_inc(rstd_done, 1)
                    for k in range(HALVES):
                        act.wait_ge(u_done, ev(pair * 2 + k + 1))
                        act.wait_ge(cv_done, ev(pair * 2 - 1 + k))
                        act.activation(ub[:, k, :, TAPS - 1:], seqs((pA, pB)[k][:, :]),
                                       ACT.Copy).then_inc(ub_done, 1)
                    for k in range(HALVES):
                        act.wait_ge(res_done, ev(pair * 2 + k + 1))
                        act.wait_ge(z_done, ev(pair - 1))
                        act.activation(sr[par][:, k, :], (pA, pB)[k][:, :], ACT.Silu).then_inc(sr_done, 1)
                    for k in range(HALVES):
                        act.wait_ge(cv_done, ev(pair * 2 + k + 1))
                        act.wait_ge(yd_done, ev(pair - 1))
                        act.activation(us[par][:, k, :], cv[:, k, :, :].rearrange("p b s -> p (b s)"),
                                       ACT.Silu).then_inc(us_done, 1)
                    act.wait_ge(xdbl_done, ev(pair + 1))
                    act.activation(dr, pA[0:RANK, :], ACT.Copy).then_inc(dr_done, 1)
                    act.preload_act_table_set("natural_log_exp_and_others")
                    for k in range(HALVES):
                        e = pair * 2 + k
                        act.wait_ge(dt_done, ev(e + 1))
                        act.wait_ge(spl_done, ev(e))
                        act.activation(sp_abs[:, :], (pB, pA)[k][:, :], ACT.Abs,
                                       bias=b_dt[:, k:k + 1]).then_inc(abs_done, 1)
                        act.wait_ge(abs_done, ev(e + 1))
                        act.activation(sp_abs[:, :], sp_abs[:, :], ACT.Exp, scale=-1.0).then_inc(exp_done, 1)
                        act.wait_ge(exp_done, ev(e + 1))
                        act.activation(sp_ln[:, k, :], sp_abs[:, :], ACT.Ln, bias=1.0).then_inc(spl_done, 1)
                    act.wait_ge(delta_done, ev(pair + 1))
                    for n in range(STATE):
                        g = pair * STATE + n
                        r = n % 2
                        act.wait_ge(scan_done, ev(g - 1))
                        for k in range(HALVES):
                            last = act.activation(dA[r][:, k, :, 1:], seqs(delta[par][:, k, :])[:, :, 1:],
                                                  ACT.Exp, scale=a_neg[:, k, n:n + 1])
                        last.then_inc(dA_done, 1)
                        act.wait_ge(bcC_done, ev(g + 1))
                        act.wait_ge(hc_done, ev(g - 1))
                        act.activation(cs[r][:, :], bC[r][:, :], ACT.Copy).then_inc(cs_done, 1)
                    act.wait_ge(cen2_done, ev(pair + 1))
                    act.activation(sq[:, :], pA[:, :], ACT.Square).then_inc(sq2_done, 1)
                    act.wait_ge(var2_done, ev(pair + 1))
                    act.wait_ge(hn_done, ev(pair + 1))
                    act.activation(rstd[:, :], pB[:, :], ACT.Ln, bias=eps[:, 0:1]).then_inc(ln2_done, 1)
                    act.wait_ge(ln2_done, ev(pair + 1))
                    act.activation(rstd[:, :], rstd[:, :], ACT.Exp, scale=-0.5).then_inc(rstd2_done, 1)
            for layer in range(DEPTH):
                act.wait_ge(s_set_pool, 2 + layer)
                with act.Fori(0, BATCH) as i:
                    b = i + layer * BATCH
                    for t in range(2):
                        e = b * 2 + t
                        act.wait_ge(qk_done, ev(e + 1))
                        act.wait_ge(ss_done, ev(e))
                        for c in range(2):
                            last = act.activation(sqk[:, c * QKV:(c + 1) * QKV], front[c][:, :], ACT.Square)
                        last.then_inc(sqk_done, 1)
                        act.wait_ge(tq_done, ev(2 * e + 1))
                        act.activation(qT[:, :, t * 128:(t + 1) * 128],
                                       tb[0][:, :].rearrange("p (k c) -> p k c", k=4), ACT.Copy).then_inc(qT_done, 1)
                        act.wait_ge(tq_done, ev(2 * e + 2))
                        act.activation(kT[:, :, t * 128:(t + 1) * 128],
                                       tb[1][:, :].rearrange("p (k c) -> p k c", k=4), ACT.Copy).then_inc(kT_done, 1)
                    for j in range(3):
                        act.wait_ge(v_done, ev(b * 3 + j + 1))
                        act.activation(vs[:, j, :, 0:DH],
                                       front[j % 2][:, :].rearrange("p (h d) -> p h d", h=HEADS),
                                       ACT.Copy).then_inc(vs_done, 1)
                    for t in range(2):
                        for hp in range(2):
                            e = b * 4 + 2 * t + hp
                            act.wait_ge(nb_done, ev(e + 1))
                            act.wait_ge(tp_done, ev(e - 1))
                            for k in range(4):
                                last = act.activation(pr[hp][:, k, :], sc[hp][:, k * 128:(k + 1) * 128],
                                                      ACT.Exp, scale=rq8[t][:, 2 * k + hp:2 * k + hp + 1],
                                                      bias=nb[hp][:, k:k + 1])
                            last.then_inc(p_done, 1)
                        act.wait_ge(to_done, ev(b * 2 + t + 1))
                        act.activation(oT[:, :, t * 128:(t + 1) * 128],
                                       tb[t][:, :].rearrange("p (k c) -> p k c", k=4), ACT.Copy).then_inc(oT_done, 1)
                    act.wait_ge(ac_done, ev(b + 1))
                    act.activation(a_sq[:, :], front[1][:, 0:SEQ], ACT.Square).then_inc(asq_done, 1)
                    act.wait_ge(avar_done, ev(b + 1))
                    act.activation(a_ln[:, :], front[0][:, 0:SEQ], ACT.Ln, bias=eps[:, 0:1]).then_inc(aln_done, 1)
                    act.wait_ge(aln_done, ev(b + 1))
                    act.activation(a_rstd[:, :], a_ln[:, :], ACT.Exp, scale=-0.5).then_inc(arstd_done, 1)
                with act.Fori(0, PAIRS // 2) as i:
                    for par in range(2):
                        pair = 2 * i + par + layer * PAIRS
                        for j, (_, m) in enumerate(HID_BLOCKS):
                            e = pair * 3 + j
                            act.wait_ge(g_done, ev(e + 1))
                            act.wait_ge(mid_done_f, ev(e - 1))
                            act.activation(ge[j % 2][0:m, :], gp[j % 2][0:m, :], ACT.Gelu,
                                           bias=b1[0:m, layer, 1, j:j + 1]).then_inc(ge_done, 1)
                        if layer == DEPTH - 1:
                            q = 2 * i + par
                            act.wait_ge(fT_done, ev(q + 1))
                            act.wait_ge(s_out[par], ev(16 * i))
                            act.activation(so[par][:, :, :].rearrange("p t d -> p (t d)"), tp[:, :],
                                           ACT.Copy).then_inc(so_done, 1)
                act.preload_act_table_set("natural_log_exp_and_others")

        @block.vector
        def _(dve):
            dve.wait_ge(s_w, ALL_W)
            half = DH // 2
            for layer in range(DEPTH):
                for c in range(2):
                    scale_of = qks[:, layer, c, :]
                    dve.tensor_tensor(tables[:, layer, :, 2 * c, :], rope[:, :, 2 * c, :],
                                      scale_of.unsqueeze(1).broadcast_to([128, 2, DH]), ALU.mult)
                    for s in range(2):
                        o = 1 - s
                        dve.tensor_tensor(tables[:, layer, :, 2 * c + 1, s * half:(s + 1) * half],
                                          rope[:, :, 2 * c + 1, s * half:(s + 1) * half],
                                          scale_of[:, o * half:(o + 1) * half].unsqueeze(1)
                                          .broadcast_to([128, 2, half]), ALU.mult)
            dve.wait_ge(s_mod, 2)
            dve.tensor_copy(mod[:, :, :], psum[1][:, 0:6 * BATCH].rearrange("p (k b) -> p k b", k=6)
                            ).then_inc(s_set_dve, 1)
            dve.wait_ge(s_set_dve, 1)
            dve.wait_ge(s_set_act, 2)
            for n, k in enumerate((1, 4)):
                dve.tensor_scalar(mod[:, k, :], mod[:, k, :], 1.0, None, ALU.add).then_inc(s_set_dve, 1)
            for n, k in enumerate((2, 5)):
                dve.tensor_scalar(gate_abs[:, n, :], mod[:, k, :], -1.0, None, ALU.mult).then_inc(s_set_dve, 1)
                dve.tensor_scalar(gate_sign[:, n, :], mod[:, k, :], 0.0, 2.0, ALU.is_ge, ALU.mult)
            dve.wait_ge(s_set_dve, 5)
            for n, k in enumerate((2, 5)):
                dve.tensor_tensor(gate_abs[:, n, :], gate_abs[:, n, :], mod[:, k, :], ALU.max).then_inc(s_set_dve, 1)
            dve.wait_ge(s_set_dve, 7)
            dve.tensor_scalar(gate_abs[:, :, :], gate_abs[:, :, :], 0.25, None, ALU.max).then_inc(s_set_dve, 1)
            dve.wait_ge(s_set_dve, 8)
            dve.scalar_tensor_tensor(mod[:, 2:6:3, :], gate_sign[:, :, :], -1.0, gate_abs[:, :, :],
                                     ALU.add, ALU.mult).then_inc(s_set_dve, 1)
            dve.tensor_scalar(a_neg[:, :, :], a_neg[:, :, :], -1.0, None, ALU.mult).then_inc(s_set_dve, 1)
            dve.wait_ge(s_set_dve, SET_DVE)
            dve.wait_ge(s_set_pool, 1)

            def scalar_of(k, pair, j):
                return mod[:, k, bass.ds(pair * 2 + j, 1)]

            with dve.Fori(0, PAIRS // 2) as i:
                for par in range(2):
                    pair = 2 * i + par
                    dve.wait_ge(rstd_done, ev(pair + 1))
                    dve.wait_ge(xf_done, ev(pair))
                    dve.tensor_tensor(hn[:, :], pB[:, :], rstd[:, :], ALU.mult).then_inc(hn_done, 1)
                    dve.wait_ge(hn_done, ev(pair + 1))
                    dve.wait_ge(res_done, ev(2 * pair))
                    for j in range(2):
                        cols = slice(j * SEQ, (j + 1) * SEQ)
                        last = dve.tensor_scalar(h_mod[:, cols], hn[:, cols], scalar_of(1, pair, j),
                                                 scalar_of(0, pair, j), ALU.mult, ALU.add)
                    last.then_inc(h_done, 1)
                    for k in range(HALVES):
                        dve.wait_ge(ub_done, ev(pair * 2 + k + 1))
                        dve.wait_ge(us_done, ev(pair * 2 - 1 + k))
                        dve.tensor_scalar(cv[:, k, :, :], ub[:, k, :, 0:SEQ], conv_w[:, k, 0:1],
                                          conv_b[:, k:k + 1], ALU.mult, ALU.add).then_inc(conv_step, 1)
                        for tap in range(1, TAPS):
                            dve.wait_ge(conv_step, ev((pair * 2 + k) * (TAPS - 1) + tap))
                            last = dve.scalar_tensor_tensor(cv[:, k, :, :], ub[:, k, :, tap:tap + SEQ],
                                                            conv_w[:, k, tap:tap + 1], cv[:, k, :, :],
                                                            ALU.mult, ALU.add)
                            last.then_inc(cv_done if tap == TAPS - 1 else conv_step, 1)
                    dve.wait_ge(xdbl_done, ev(pair + 1))
                    dve.wait_ge(bcC_done, ev(pair * STATE))
                    dve.wait_ge(split_done, ev(pair))
                    bc = pA[RANK:RANK + 2 * STATE, :]
                    dve.tensor_copy(parts[par][0:32, :], bc).then_inc(hi_done, 1)
                    dve.wait_ge(hi_done, ev(pair + 1))
                    dve.tensor_tensor(rest, bc, parts[par][0:32, :], ALU.subtract).then_inc(rest_done, 1)
                    dve.wait_ge(rest_done, ev(pair + 1))
                    dve.tensor_copy(parts[par][64:96, :], rest).then_inc(mid_done, 1)
                    dve.wait_ge(mid_done, ev(pair + 1))
                    dve.tensor_tensor(parts[par][32:64, :], rest, parts[par][64:96, :],
                                      ALU.subtract).then_inc(split_done, 1)
                    for k in range(HALVES):
                        dve.wait_ge(abs_done, ev(pair * 2 + k + 1))
                        dve.tensor_scalar(delta[par][:, k, :], (pB, pA)[k][:, :], b_dt[:, k:k + 1], 0.0,
                                          ALU.add, ALU.max).then_inc(pos_done, 1)
                    dve.wait_ge(pos_done, ev(pair * 2 + 2))
                    dve.wait_ge(spl_done, ev(pair * 2 + 2))
                    dve.tensor_tensor(delta[par][:, :, :], delta[par][:, :, :], sp_ln[:, :, :],
                                      ALU.add).then_inc(delta_done, 1)
                    dve.wait_ge(delta_done, ev(pair + 1))
                    dve.tensor_tensor(du[par][:, :, :], delta[par][:, :, :], us[par][:, :, :],
                                      ALU.mult).then_inc(du_done, 1)
                    dve.wait_ge(du_done, ev(pair + 1))
                    for n in range(STATE):
                        g = pair * STATE + n
                        r = n % 2
                        dve.wait_ge(bcB_done, ev(g + 1))
                        dve.wait_ge(y_done, ev(g + 1 - RING))
                        dve.tensor_tensor(hst[n % RING][:, :, :], du[par][:, :, :],
                                          bB[r][:, :].unsqueeze(1).broadcast_to([128, HALVES, TOK]),
                                          ALU.mult).then_inc(dBu_done, 1)
                        dve.wait_ge(dBu_done, ev(g + 1))
                        dve.wait_ge(dA_done, ev(g + 1))
                        dve.tensor_tensor_scan(hst[n % RING][:, :, :].rearrange("p k s -> p (k s)"),
                                               dA[r][:, :, :, :].rearrange("p k b s -> p (k b s)"),
                                               hst[n % RING][:, :, :].rearrange("p k s -> p (k s)"), 0.0,
                                               ALU.mult, ALU.add).then_inc(scan_done, 1)
                    dve.wait_ge(y_done, ev(pair * STATE + STATE))
                    dve.wait_ge(out_done, ev(pair))
                    for k in range(HALVES):
                        last = dve.scalar_tensor_tensor(z[:, k, :], us[par][:, k, :], skip_d[:, k:k + 1],
                                                        yp[k][:, :], ALU.mult, ALU.add)
                    last.then_inc(yd_done, 1)
                    dve.wait_ge(yd_done, ev(pair + 1))
                    dve.tensor_tensor(z[:, :, :], z[:, :, :], sr[par][:, :, :], ALU.mult).then_inc(z_done, 1)
                    dve.wait_ge(out_done, ev(pair + 1))
                    for j in range(2):
                        cols = slice(j * SEQ, (j + 1) * SEQ)
                        last = dve.scalar_tensor_tensor(xs[par][:, cols], pB[:, cols], scalar_of(2, pair, j),
                                                        xs[par][:, cols], ALU.mult, ALU.add)
                    last.then_inc(xn_done, 1)
                    dve.wait_ge(xn_done, ev(pair + 1))
                    dve.tensor_scalar(tokens(x1, pair), xs[par][:, :], 1.0, None, ALU.mult).then_inc(x1_done, 1)
                    dve.wait_ge(rstd2_done, ev(pair + 1))
                    dve.wait_ge(h_done, ev(pair + 1))
                    dve.tensor_tensor(hn[:, :], pA[:, :], rstd[:, :], ALU.mult).then_inc(hn2_done, 1)
                    dve.wait_ge(hn2_done, ev(pair + 1))
                    for j in range(2):
                        last = dve.tensor_scalar(xf[:, bass.ds(pair * TOK + j * SEQ, SEQ)],
                                                 hn[:, j * SEQ:(j + 1) * SEQ], scalar_of(4, pair, j),
                                                 scalar_of(3, pair, j), ALU.mult, ALU.add)
                    last.then_inc(xf_done, 1)

            def shifted(dst, b):
                dve.tensor_scalar(dst[0:64, :], xf[0:64, bass.ds(b * SEQ, SEQ)], 1.0, None, ALU.mult)
                return dve.tensor_scalar(dst[64:128, 1:SEQ], xf[64:128, bass.ds(b * SEQ, SEQ - 1)],
                                         1.0, None, ALU.mult)

            dve.wait_ge(xf_done, ev(PAIRS))
            for layer in range(DEPTH):
                dve.wait_ge(s_set_pool, 2 + layer)
                if layer:
                    dve.wait_ge(xo_done, ev(PAIRS))
                with dve.Fori(0, BATCH) as i:
                    b = i + layer * BATCH
                    dve.wait_ge(v_done, ev(b * 3))
                    shifted(hT[0], i).then_inc(ht_done, 1)
                    for t in range(2):
                        e = b * 2 + t
                        dve.wait_ge(sqk_done, ev(e + 1))
                        dve.wait_ge(add_done, ev(e))
                        for c in range(2):
                            src = front[c][:, :].rearrange("p (h d) -> p h d", h=HEADS)
                            table = tables[:, layer, t, 2 * c, :].unsqueeze(1).broadcast_to([128, HEADS, DH])
                            dve.tensor_tensor(rot_a[:, c, :].rearrange("p (h d) -> p h d", h=HEADS),
                                              src, table, ALU.mult)
                            for s in range(2):
                                o = 1 - s
                                table = tables[:, layer, t, 2 * c + 1, s * half:(s + 1) * half]
                                last = dve.tensor_tensor(
                                    rot_b[:, c, :].rearrange("p (h d) -> p h d", h=HEADS)[:, :, s * half:(s + 1) * half],
                                    src[:, :, o * half:(o + 1) * half],
                                    table.unsqueeze(1).broadcast_to([128, HEADS, half]), ALU.mult)
                        last.then_inc(rot_done, 1)
                        dve.tensor_reduce(ss[:, :], sqk[:, :].rearrange("p (h d) -> p h d", d=DH),
                                          AX.X, ALU.add).then_inc(ss_done, 1)
                        dve.wait_ge(ss_done, ev(e + 1))
                        dve.wait_ge(rn_done, ev(e))
                        dve.tensor_scalar(ssm[:, :], ss[:, :], 1e-24, None, ALU.max).then_inc(ssm_done, 1)
                        dve.wait_ge(rn_done, ev(e + 1))
                        dve.wait_ge(p_done, ev(b * 4 - 2 + 2 * t))
                        dve.tensor_scalar(rq8[t][:, :], rn[t][:, 0:HEADS], QK_SCALE, None,
                                          ALU.mult).then_inc(rq8_done, 1)
                    for t in range(2):
                        for hp in range(2):
                            e = b * 4 + 2 * t + hp
                            dve.wait_ge(s_done, ev(e + 1))
                            dve.tensor_reduce(mx[hp][:, :], sc[hp][:, :].rearrange("p (k j) -> p k j", k=4),
                                              AX.X, ALU.max).then_inc(mx_done, 1)
                            dve.wait_ge(mx_done, ev(e + 1))
                            dve.wait_ge(p_done, ev(e - 1))
                            dve.wait_ge(rq8_done, ev(b * 2 + t + 1))
                            dve.scalar_tensor_tensor(nb[hp][:, :], mx[hp][:, :], -1.0,
                                                     rq8[t][:, hp:HEADS:2], ALU.mult, ALU.mult).then_inc(nb_done, 1)
                        for hp in range(2):
                            e = b * 4 + 2 * t + hp
                            dve.wait_ge(tp_done, ev(e + 1))
                            dve.wait_ge(o_done, ev(e - 1))
                            dve.tensor_copy(pT[hp][:, :, :].rearrange("p k j -> p (k j)"),
                                            tb[hp if t == 0 else 1 - hp][:, :]).then_inc(pT_done, 1)
                        for hp in range(2):
                            e = b * 4 + 2 * t + hp
                            o4 = op[hp][:, 0:4 * (DH + 1)].rearrange("p (k d) -> p k d", k=4)
                            dve.wait_ge(o_done, ev(e + 1))
                            dve.wait_ge(on_done, ev(e - 1))
                            dve.reciprocal(rd[hp][:, :], o4[:, :, DH]).then_inc(rd_done, 1)
                            dve.wait_ge(rd_done, ev(e + 1))
                            dve.wait_ge(to_done, ev(b * 2 + t))
                            dve.tensor_tensor(
                                on[:, :].rearrange("p (k s d) -> p k s d", k=4, s=2)[:, :, hp, :],
                                o4[:, :, 0:DH], rd[hp][:, :].unsqueeze(2).broadcast_to([128, 4, DH]),
                                ALU.mult).then_inc(on_done, 1)
                    dve.wait_ge(wo_done, ev(b + 1))
                    cur = xf[:, bass.ds(i * SEQ, SEQ)]
                    dve.tensor_tensor(cur, front[0][:, 0:SEQ], cur, ALU.add).then_inc(xr_done, 1)
                    dve.wait_ge(xr_done, ev(b + 1))
                    shifted(hs, i).then_inc(hs_done, 1)
                    dve.wait_ge(arstd_done, ev(b + 1))
                    dve.tensor_tensor(a_hn[:, :], front[1][:, 0:SEQ], a_rstd[:, :], ALU.mult).then_inc(ahn_done, 1)
                    dve.wait_ge(ahn_done, ev(b + 1))
                    dve.tensor_scalar(hf[:, bass.ds(i * SEQ, SEQ)], a_hn[:, :], ln_g[:, layer:layer + 1],
                                      ln_b[:, layer:layer + 1], ALU.mult, ALU.add).then_inc(hf_done, 1)
                with dve.Fori(0, PAIRS // 2) as i:
                    for par in range(2):
                        q = 2 * i + par
                        pair = q + layer * PAIRS
                        for j, (_, m) in enumerate(HID_BLOCKS):
                            e = pair * 3 + j
                            dve.wait_ge(ge_done, ev(e + 1))
                            dve.wait_ge(w2_done, ev(pair))
                            dve.scalar_tensor_tensor(mid[j][0:m, :], ap_[j % 2][0:m, :],
                                                     b1[0:m, layer, 0, j:j + 1], ge[j % 2][0:m, :],
                                                     ALU.add, ALU.mult).then_inc(mid_done_f, 1)
                        dve.wait_ge(w2_done, ev(pair + 1))
                        dve.scalar_tensor_tensor(tokens(xf, q), rp[:, :], b2[:, layer:layer + 1],
                                                 tokens(xf, q), ALU.add, ALU.add).then_inc(xo_done, 1)
                        if layer == DEPTH - 1:
                            dve.wait_ge(xo_done, ev(pair + 1))
                            dve.wait_ge(fT_done, ev(q))
                            for j in range(2):
                                at = bass.ds(q * TOK + j * SEQ, SEQ)
                                last = dve.scalar_tensor_tensor(fo[:, j * SEQ:(j + 1) * SEQ], xf[:, at],
                                                                scalar_of(5, q, j), x1[:, at],
                                                                ALU.mult, ALU.add)
                            last.then_inc(fo_done, 1)

        @block.tensor
        def _(pe):
            pe.wait_ge(s_w, ALL_W)
            pe.wait_ge(s_cast, 16 * len(CASTS))
            pe.transpose(psum[0][:, 0:BATCH], cond[:, :], ident[0:32, 0:32]).then_inc(s_mod, 1)
            pe.wait_ge(s_set_act, 1)
            for k in range(6):
                last = pe.matmul(psum[1][:, k * BATCH:(k + 1) * BATCH], wmod[:, k * DIM:(k + 1) * DIM],
                                 condT[:, :], start=True, stop=True)
            last.then_inc(s_mod, 1)
            pe.wait_ge(s_set_dve, SET_DVE)
            pe.wait_ge(s_set_pool, 1)

            with pe.Fori(0, PAIRS // 2) as i:
                for par in range(2):
                    pair = 2 * i + par
                    pe.wait_ge(s_x[par], ev(16 * (i + 1)))
                    pe.wait_ge(hn2_done, ev(pair))
                    for t in range(4):
                        last = pe.transpose(pA[:, t * 128:(t + 1) * 128], xin[par][:, t, :], ident[:, :])
                    last.then_inc(xT_done, 1)
                    pe.wait_ge(xs_done, ev(pair + 1))
                    pe.wait_ge(ln2_done, ev(pair))
                    pe.matmul(pB[:, :], center[:, :], xs[par][:, :], start=True, stop=True).then_inc(cen_done, 1)
                    pe.wait_ge(sq_done, ev(pair + 1))
                    pe.matmul(pA[:, :], mean_w[:, :], sq[:, :], start=True, stop=True).then_inc(var_done, 1)
                    pe.wait_ge(h_done, ev(pair + 1))
                    for k in range(HALVES):
                        pe.matmul((pA, pB)[k][:, :], w_in[:, k * 128:(k + 1) * 128], h_mod[:, :],
                                  start=True, stop=True).then_inc(u_done, 1)
                    for k in range(HALVES):
                        pe.wait_ge(ub_done, ev(pair * 2 + k + 1))
                        pe.matmul((pA, pB)[k][:, :], w_in[:, INNER + k * 128:INNER + (k + 1) * 128],
                                  h_mod[:, :], start=True, stop=True).then_inc(res_done, 1)
                    pe.wait_ge(us_done, ev(pair * 2 + 2))
                    for k in range(HALVES):
                        last = pe.matmul(pA[0:RANK + 2 * STATE, :], w_x[:, k, :], us[par][:, k, :],
                                         start=(k == 0), stop=(k == HALVES - 1))
                    last.then_inc(xdbl_done, 1)
                    pe.wait_ge(dr_done, ev(pair + 1))
                    pe.matmul(pB[:, :], w_dt[:, 0:128], dr, start=True, stop=True).then_inc(dt_done, 1)
                    pe.wait_ge(rest_done, ev(pair + 1))
                    pe.matmul(pA[:, :], w_dt[:, 128:256], dr, start=True, stop=True).then_inc(dt_done, 1)
                    pe.wait_ge(split_done, ev(pair + 1))
                    pe.wait_ge(yd_done, ev(pair))

                    def reduce_state(g, r, n):
                        pe.wait_ge(hc_done, ev(g + 1))
                        for k in range(HALVES):
                            last = pe.matmul(yp[k][:, :], ident[:, :], hst[n % RING][:, k, :],
                                             start=(n == 0), stop=(n == STATE - 1))
                        last.then_inc(y_done, 1)

                    for n in range(STATE):
                        g = pair * STATE + n
                        r = n % 2
                        pe.wait_ge(dBu_done, ev(g - 1))
                        pe.matmul(bB[r][:, :], sel[:, n, :], parts[par][:, :], start=True,
                                  stop=True).then_inc(bcB_done, 1)
                        pe.wait_ge(cs_done, ev(g - 1))
                        pe.matmul(bC[r][:, :], sel[:, STATE + n, :], parts[par][:, :], start=True,
                                  stop=True).then_inc(bcC_done, 1)
                        if n:
                            reduce_state(g - 1, 1 - r, n - 1)
                    reduce_state(pair * STATE + STATE - 1, (STATE - 1) % 2, STATE - 1)
                    pe.wait_ge(z_done, ev(pair + 1))
                    for k in range(HALVES):
                        last = pe.matmul(pB[:, :], w_out[:, k, :], z[:, k, :], start=(k == 0),
                                         stop=(k == HALVES - 1))
                    last.then_inc(out_done, 1)
                    pe.wait_ge(xn_done, ev(pair + 1))
                    pe.matmul(pA[:, :], center[:, :], xs[par][:, :], start=True, stop=True).then_inc(cen2_done, 1)
                    pe.wait_ge(sq2_done, ev(pair + 1))
                    pe.matmul(pB[:, :], mean_w[:, :], sq[:, :], start=True, stop=True).then_inc(var2_done, 1)

            for layer in range(DEPTH):
                pe.wait_ge(s_set_pool, 2 + layer)
                with pe.Fori(0, BATCH) as i:
                    b = i + layer * BATCH
                    pe.wait_ge(ht_done, ev(b + 1))
                    pe.wait_ge(ahn_done, ev(b))
                    for t in range(2):
                        e = b * 2 + t
                        tok = hT[0][:, t * 128:(t + 1) * 128]
                        pe.wait_ge(rot_done, ev(e))
                        pe.wait_ge(sqk_done, ev(e))
                        for c in range(2):
                            last = pe.matmul(front[c][:, :], tok, wqkv[:, layer, c * QKV:(c + 1) * QKV],
                                             start=True, stop=True)
                        last.then_inc(qk_done, 1)
                        pe.wait_ge(add_done, ev(e + 1))
                        pe.wait_ge(kT_done, ev(e))
                        pe.wait_ge(oT_done, ev(2 * b))
                        pe.wait_ge(pT_done, ev(4 * b))
                        for k in range(4):
                            last = pe.transpose(tb[0][:, k * 128:(k + 1) * 128],
                                                qkr[:, 0, k * 128:(k + 1) * 128], ident[:, :])
                        last.then_inc(tq_done, 1)
                        pe.wait_ge(kn_done, ev(e + 1))
                        for k in range(4):
                            last = pe.transpose(tb[1][:, k * 128:(k + 1) * 128],
                                                kn[:, k * 128:(k + 1) * 128], ident[:, :])
                        last.then_inc(tq_done, 1)
                    pe.wait_ge(rot_done, ev(b * 2 + 2))
                    pe.wait_ge(sqk_done, ev(b * 2 + 2))
                    for j in range(3):
                        if j == 2:
                            pe.wait_ge(vs_done, ev(b * 3 + 1))
                        pe.matmul(front[j % 2][:, :], hT[0][:, j * 64:j * 64 + 128],
                                  wqkv[:, layer, 2 * QKV:3 * QKV], start=True, stop=True).then_inc(v_done, 1)
                    pe.wait_ge(kT_done, ev(b * 2 + 2))
                    pe.wait_ge(vs_done, ev(b * 3 + 3))
                    for t in range(2):
                        for hp in range(2):
                            e = b * 4 + 2 * t + hp
                            rows = slice(64 * hp, 64 * hp + 64)
                            pe.wait_ge(p_done, ev(e - 1))
                            pe.matmul(sc[hp][:, :], identb[:, :],
                                      mask[:, t, :].unsqueeze(1).broadcast_to([128, 4, 128]),
                                      start=True, stop=False, skip_group_check=True)
                            for k in range(4):
                                cols = slice(k * 128, (k + 1) * 128)
                                if t == 0:
                                    last = pe.matmul(sc[hp][:, cols], qT[rows, k, 0:128], kT[rows, k, 0:128],
                                                     start=False, stop=True, skip_group_check=True)
                                else:
                                    for w in range(2):
                                        last = pe.matmul(sc[hp][64 * w:64 * w + 64, cols],
                                                         qT[rows, k, 128 + 64 * w:192 + 64 * w],
                                                         kT[rows, k, 64 + 64 * w:192 + 64 * w],
                                                         start=False, stop=True, skip_group_check=True)
                            last.then_inc(s_done, 1)
                        for hp in range(2):
                            e = b * 4 + 2 * t + hp
                            pe.wait_ge(p_done, ev(e + 1))
                            pe.wait_ge(oT_done, ev(b * 2 + t))
                            pe.wait_ge(pT_done, ev(e - 1))
                            bank = tb[hp if t == 0 else 1 - hp]
                            for k in range(4):
                                last = pe.transpose(bank[:, k * 128:(k + 1) * 128], pr[hp][:, k, :], ident[:, :])
                            last.then_inc(tp_done, 1)
                        for hp in range(2):
                            e = b * 4 + 2 * t + hp
                            pe.wait_ge(pT_done, ev(e + 1))
                            pe.wait_ge(on_done, ev(e - 1))
                            for k in range(4):
                                h = 2 * k + hp
                                cols = slice(k * (DH + 1), (k + 1) * (DH + 1))
                                if t == 0:
                                    last = pe.matmul(op[hp][:, cols], pT[hp][:, k, :], vs[:, 0, h, :],
                                                     start=True, stop=True)
                                else:
                                    for w in range(2):
                                        last = pe.matmul(op[hp][64 * w:64 * w + 64, cols],
                                                         pT[hp][:, k, 64 * w:64 * w + 64],
                                                         vs[:, 1 + w, h, :], start=True, stop=True)
                            last.then_inc(o_done, 1)
                        pe.wait_ge(on_done, ev(b * 4 + 2 * t + 2))
                        for k in range(4):
                            last = pe.transpose(tb[t][:, k * 128:(k + 1) * 128],
                                                on[:, k * 128:(k + 1) * 128], ident[:, :])
                        last.then_inc(to_done, 1)
                    pe.wait_ge(oT_done, ev(b * 2 + 2))
                    for k in range(4):
                        last = pe.matmul(front[0][:, 0:SEQ], wo[:, layer, k, :], oT[:, k, :],
                                         start=(k == 0), stop=(k == 3))
                    last.then_inc(wo_done, 1)
                    pe.wait_ge(hs_done, ev(b + 1))
                    pe.matmul(front[1][:, 0:SEQ], center[:, :], hs[:, :], start=True, stop=True).then_inc(ac_done, 1)
                    pe.wait_ge(asq_done, ev(b + 1))
                    pe.matmul(front[0][:, 0:SEQ], mean_w[:, :], a_sq[:, :], start=True, stop=True).then_inc(avar_done, 1)
                pe.wait_ge(hf_done, ev((layer + 1) * BATCH))
                with pe.Fori(0, PAIRS // 2) as i:
                    for par in range(2):
                        q = 2 * i + par
                        pair = q + layer * PAIRS
                        for j, (at, m) in enumerate(HID_BLOCKS):
                            e = pair * 3 + j
                            pe.wait_ge(mid_done_f, ev(e - 1))
                            pe.matmul(gp[j % 2][0:m, :], w1[:, layer, HID + at:HID + at + m],
                                      tokens(hf, q), start=True, stop=True)
                            pe.matmul(ap_[j % 2][0:m, :], w1[:, layer, at:at + m], tokens(hf, q),
                                      start=True, stop=True).then_inc(g_done, 1)
                        pe.wait_ge(xo_done, ev(pair))
                        for j, (at, m) in enumerate(HID_BLOCKS):
                            pe.wait_ge(mid_done_f, ev(pair * 3 + j + 1))
                            last = pe.matmul(rp[:, :], w2[0:m, layer, j, :], mid[j][0:m, :],
                                             start=(j == 0), stop=(j == 2))
                        last.then_inc(w2_done, 1)
                        if layer == DEPTH - 1:
                            pe.wait_ge(fo_done, ev(q + 1))
                            pe.wait_ge(so_done, ev(q))
                            for t in range(4):
                                last = pe.transpose(tp[:, t * 128:(t + 1) * 128],
                                                    fo[:, t * 128:(t + 1) * 128], ident[:, :])
                            last.then_inc(fT_done, 1)


_NAMES = {
    "L0_attn_x": "x", "L0_attn_W_in": "W_in", "L0_attn_conv_w": "conv_w", "L0_attn_conv_b": "conv_b",
    "L0_attn_W_x": "W_x", "L0_attn_W_dt": "W_dt", "L0_attn_b_dt": "b_dt", "L0_attn_A_log": "A_log",
    "L0_attn_D": "D", "L0_attn_W_out": "W_out", "L0_ffn_wqkv": "wqkv", "L0_ffn_q_scale": "q_scale",
    "L0_ffn_k_scale": "k_scale", "L0_ffn_wo": "wo", "L0_ffn_ln_g": "ln_g", "L0_ffn_ln_b": "ln_b",
    "L0_ffn_w1": "w1", "L0_ffn_b1": "b1", "L0_ffn_w2": "w2", "L0_ffn_b2": "b2", "L0_c": "c",
    "L0_wmod": "wmod",
}


def kernel(**inputs):
    import numpy as _np
    import concourse.bacc as _bacc
    from concourse import mybir as _mybir
    from concourse.bass_utils import run_bass_kernel_spmd as _run

    nc = _bacc.Bacc("TRN2", target_bir_lowering=False, num_devices=1)
    arrays, args = {}, {}
    given = {short: _np.ascontiguousarray(inputs[name]) for name, short in _NAMES.items()}
    given.update(shape_constants())
    for short, a in given.items():
        arrays[f"in_{short}"] = a
        args[short] = nc.dram_tensor(f"in_{short}", a.shape, _mybir.dt.from_np(a.dtype),
                                     kind="ExternalInput").ap()
    out = nc.dram_tensor("out_0", (BATCH, SEQ, DIM), _mybir.dt.float32, kind="ExternalOutput").ap()
    block_kernel(nc, args, out)
    r = _run(nc, [arrays], core_ids=[0])
    return r.results[0]["out_0"]
```

```python
import math

import concourse.bass as bass
import numpy as np
from concourse import mybir
from contextlib import ExitStack

FP32 = mybir.dt.float32
BF16 = mybir.dt.bfloat16
ALU = mybir.AluOpType
ACT = mybir.ActivationFunctionType
AX = mybir.AxisListType

BATCH, SEQ, DIM = 32, 256, 128
INNER = 256
HALVES = INNER // 128
STATE = 16
TAPS = 4
RING = 4
LAG = 2
RANK = 64
DEPTH = 2
HEADS, DH = 8, 64
WINDOW = 64
QKV = HEADS * DH
HID = 341
HID_BLOCKS = [(0, 128), (128, 128), (256, HID - 256)]
TOK = 512
PAIRS = BATCH // 2
QK_SCALE = 8.0
MASKED = -1.0e30
EPS = 1e-5
SS_BITS = 18

CREDIT = 8


def shape_constants():
    ident = np.eye(128, dtype=np.float32)
    center = (ident - np.float32(1.0 / 128)).astype(np.float32)
    sel = np.zeros((96, 32, 128), np.float32)
    for n in range(32):
        for part in range(3):
            sel[32 * part + n, n, :] = 1.0
    i = np.arange(128)[:, None]
    j = np.arange(128)[None, :]
    near = i - j
    far = WINDOW + (i % WINDOW) - j
    mask = np.stack([np.where((d >= 0) & (d <= WINDOW), 0.0, MASKED) for d in (near, far)], 1)
    half = np.arange(0, DH, 2, dtype=np.float32)
    inv = (np.float32(1.0) / np.float32(10000.0) ** (half / np.float32(DH))).astype(np.float32)
    t = np.arange(SEQ, dtype=np.float32)
    freqs = t[:, None] * inv[None, :]
    freqs = np.concatenate([freqs, freqs], -1).astype(np.float32)
    base = ((half + np.float32(0.4 * DH)) / np.float32(1.4 * DH)).astype(np.float32)
    power = ((t - SEQ // 2) / np.float32(WINDOW // 2)).astype(np.float32)
    scale = (base[None, :] ** power[:, None]).astype(np.float32)
    scale = np.concatenate([scale, scale], -1)
    sign = np.where(np.arange(DH) < DH // 2, -1.0, 1.0).astype(np.float32)
    cos, sin = np.cos(freqs), np.sin(freqs) * sign
    rope = np.stack([cos * scale, sin * scale, cos / scale, sin / scale], 1).astype(np.float32)
    rope = rope.reshape(2, 128, 4, DH).transpose(1, 0, 2, 3)
    return {
        "c_ident": ident, "c_center": center, "c_sel": sel.reshape(96, 32 * 128),
        "c_mask": mask.astype(np.float32).reshape(128, 256),
        "c_rope": np.ascontiguousarray(rope).reshape(128, 2 * 4 * DH),
    }


def ev(count):
    return count + CREDIT


def after(eng, sem, count):
    if not isinstance(count, int) or count > 0:
        eng.wait_ge(sem, ev(count))


def block_kernel(nc, a, out):
    ctx = ExitStack()
    with ctx:
        def sb(name, shape, dt=FP32):
            return ctx.enter_context(nc.sbuf_tensor(name, shape, dt))

        def sem(name):
            return ctx.enter_context(nc.semaphore(name))

        loop_sems = []

        def event(name):
            loop_sems.append(sem(name))
            return loop_sems[-1]

        ident = sb("ident", [128, 128])
        identb = sb("identb", [128, 128], BF16)
        center = sb("center", [128, 128])
        mean_w = sb("mean_w", [128, 128])
        mask = sb("mask", [128, 2, 128], BF16)
        tables = sb("tables", [128, DEPTH, 2, 4, DH])
        conv_w = sb("conv_w", [128, HALVES, TAPS])
        conv_b = sb("conv_b", [128, HALVES])
        b_dt = sb("b_dt", [128, HALVES])
        a_neg = sb("a_neg", [128, HALVES, STATE])
        skip_d = sb("skip_d", [128, HALVES])
        wqkv = sb("wqkv", [128, DEPTH, 3 * QKV])
        wo = sb("wo", [128, DEPTH, 4, DIM])
        ln_g = sb("ln_g", [128, DEPTH])
        ln_b = sb("ln_b", [128, DEPTH])
        w1 = sb("w1", [128, DEPTH, 2 * HID])
        b1 = sb("b1", [128, DEPTH, 2, 3])
        w2 = sb("w2", [128, DEPTH, 3, DIM])
        b2 = sb("b2", [128, DEPTH])
        eps = sb("eps", [128, 1])
        rn_shift = sb("rn_shift", [128, 1])
        newton_a = sb("newton_a", [128, 2 * HEADS])
        newton_b = sb("newton_b", [128, 2 * HEADS])
        mod = sb("mod", [128, 6, BATCH])

        x1 = sb("x1", [128, BATCH * SEQ])
        xf = sb("xf", [128, BATCH * SEQ])

        psum = [ctx.enter_context(nc.psum_tensor(f"bank{i}", [128, 512], FP32)) for i in range(8)]

        s_w = sem("s_w")
        s_cast = sem("s_cast")
        s_mod = sem("s_mod")
        s_set_act = sem("s_set_act")
        s_set_dve = sem("s_set_dve")
        s_set_pool = sem("s_set_pool")
        s_x = [event("s_x0"), event("s_x1")]
        s_out = [event("s_out0"), event("s_out1")]

        SET_DVE = 10
        x_rows = a["x"].rearrange("b s d -> (b s) d")
        out_rows = out.rearrange("b s d -> (b s) d")

        with ExitStack() as s_ctx:
            def ssb(name, shape):
                return s_ctx.enter_context(nc.sbuf_tensor(name, shape, FP32))

            rope = ssb("rope", [128, 2, 4, DH])
            qks = ssb("qks", [128, DEPTH, 2, DH])
            cond = ssb("cond", [32, DIM])
            wmod = ssb("wmod", [128, 6 * DIM])
            condT = ssb("condT", [128, BATCH])
            gate_abs = ssb("gate_abs", [128, 2, BATCH])
            gate_sign = ssb("gate_sign", [128, 2, BATCH])
        m_ctx = ExitStack()

        def msb(name, shape, dt=FP32):
            return m_ctx.enter_context(nc.sbuf_tensor(name, shape, dt))

        us = [msb(f"us{i}", [128, HALVES, TOK]) for i in range(2)]
        sr = [msb(f"sr{i}", [128, HALVES, TOK]) for i in range(2)]
        xin = [msb(f"xin{i}", [128, 4, DIM]) for i in range(2)]
        xs = msb("xs", [128, TOK])
        sq, sq2 = msb("sq", [128, TOK]), msb("sq2", [128, TOK])
        rstd, rstd2 = msb("rstd", [128, TOK]), msb("rstd2", [128, TOK])
        h_mod = msb("h_mod", [128, TOK])
        sel = msb("sel", [96, 32, 128], BF16)
        w_in = msb("w_in", [128, 2 * INNER])
        w_x = msb("w_x", [128, HALVES, RANK + 2 * STATE])
        w_dt = msb("w_dt", [RANK, INNER])
        w_out = msb("w_out", [128, HALVES, DIM])
        ub = msb("ub", [128, HALVES, 2, TAPS - 1 + SEQ])
        cv = msb("cv", [128, HALVES, 2, SEQ])
        dr_rest = msb("dr_rest", [96, TOK])
        dr, rest = dr_rest[0:RANK, :], dr_rest[64:96, :]
        parts = [msb(f"parts{i}", [96, TOK], BF16) for i in range(2)]
        sp_abs = msb("sp_abs", [128, TOK])
        sp_ln = msb("sp_ln", [128, HALVES, TOK])
        delta = [msb(f"delta{i}", [128, HALVES, TOK]) for i in range(2)]
        du = [msb(f"du{i}", [128, HALVES, TOK]) for i in range(2)]
        dA = [msb(f"dA{i}", [128, HALVES, 2, SEQ]) for i in range(2)]
        hst = [msb(f"hst{i}", [128, HALVES, TOK]) for i in range(RING)]
        cs = [msb(f"cs{i}", [128, TOK]) for i in range(2)]
        z = msb("z", [128, HALVES, TOK])

        WLOADS = [
            (ident[:, :], a["c_ident"]), (center[:, :], a["c_center"]),
            (rope[:, :, :, :], a["c_rope"].rearrange("p (b k d) -> p b k d", b=2, k=4)),
            (w_in[:, :], a["W_in"]),
            (conv_w[:, :, :], a["conv_w"].rearrange("(h p) k -> p h k", p=128)),
            (conv_b[:, :], a["conv_b"].rearrange("(h p) -> p h", p=128)),
            (w_x[:, :, :], a["W_x"].rearrange("(h p) k -> p h k", p=128)),
            (w_dt[:, :], a["W_dt"]),
            (b_dt[:, :], a["b_dt"].rearrange("(h p) -> p h", p=128)),
            (a_neg[:, :, :], a["A_log"].rearrange("(h p) k -> p h k", p=128)),
            (skip_d[:, :], a["D"].rearrange("(h p) -> p h", p=128)),
            (w_out[:, :, :], a["W_out"].rearrange("(h p) k -> p h k", p=128)),
            (wqkv[:, :, :], a["wqkv"].rearrange("l p n -> p l n")),
            (wo[:, :, :, :], a["wo"].rearrange("l (k p) n -> p l k n", p=128)),
            (ln_g[:, :], a["ln_g"].rearrange("l p -> p l")),
            (ln_b[:, :], a["ln_b"].rearrange("l p -> p l")),
            (w1[:, :, :], a["w1"].rearrange("l p n -> p l n")),
            (b2[:, :], a["b2"].rearrange("l p -> p l")),
            (qks[:, :, 0, :], a["q_scale"].partition_broadcast(128)),
            (qks[:, :, 1, :], a["k_scale"].partition_broadcast(128)),
            (w2[:, 0, 0:2, :], a["w2"][0, 0:256, :].rearrange("(k p) n -> p k n", p=128)),
            (w2[:, 1, 0:2, :], a["w2"][1, 0:256, :].rearrange("(k p) n -> p k n", p=128)),
            (w2[0:HID - 256, :, 2, :], a["w2"][:, 256:HID, :].rearrange("l p n -> p l n")),
            (cond[:, :], a["c"]), (wmod[:, :], a["wmod"]),
        ]
        for s in range(2):
            for layer in range(DEPTH):
                at = s * HID
                WLOADS.append((b1[:, layer, s, 0:2],
                               a["b1"][layer, at:at + 256].rearrange("(j p) -> p j", p=128)))
                WLOADS.append((b1[0:HID - 256, layer, s, 2:3],
                               a["b1"][layer, at + 256:at + HID].rearrange("(p j) -> p j", j=1)))
        CASTS = [(sel[:, :, :], a["c_sel"].rearrange("p (n m) -> p n m", n=32)),
                 (mask[:, :, :], a["c_mask"].rearrange("p (t m) -> p t m", t=2)),
                 (identb[:, :], a["c_ident"])]
        ALL_W = 16 * len(WLOADS)
        pA, pB = psum[0], psum[1]
        bB, bC, pE, yp = psum[2:4], psum[4], psum[5], psum[6:8]

        (xT_done, xs_done, cen_done, sq_done, var_done, ln_done, rstd_done, hn_done, h_done,
         u_done, ub_done, res_done, sr_done, conv_step, cv_done, us_done, xdbl_done, dr_done,
         hi_done, rest_done, mid_done, split_done, dt_done, abs_done, exp_done, spl_done, pos_done,
         delta_done, du_done, bcB_done, bcC_done, dA_done, dBu_done, scan_done, cs_done, hc_done,
         y_done, yd_done, z_done, out_done, xn_done, x1_done, cen2_done, sq2_done, var2_done,
         ln2_done, rstd2_done, hn2_done, xf_done) = [event(n) for n in (
             "xT xs cen sq var ln rstd hn h u ub res sr conv cv us xdbl dr hi rest mid split dt abs "
             "exp spl pos delta du bcB bcC dA dBu scan cs hc y yd z out xn x1 cen2 sq2 var2 ln2 "
             "rstd2 hn2 xf").split()]

        block = ctx.enter_context(nc.Block())

        m_ctx.close()
        hf = sb("hf", [128, BATCH * SEQ])
        a_ctx = ExitStack()

        def asb(name, shape, dt=FP32):
            return a_ctx.enter_context(nc.sbuf_tensor(name, shape, dt))

        hT = [asb(f"hT{i}", [128, SEQ]) for i in range(2)]
        sqk = [asb(f"sqk{i}", [128, 2 * QKV]) for i in range(2)]
        ss = asb("ss", [128, 2 * HEADS])
        ssm = asb("ssm", [128, 2 * HEADS])
        ln_ss = asb("ln_ss", [128, 2 * HEADS])
        rn_est = asb("rn_est", [128, 2 * HEADS])
        rn_step = asb("rn_step", [128, 2 * HEADS])
        rn = [[asb(f"rn{i}{t}", [128, 2 * HEADS]) for t in range(2)] for i in range(2)]
        rot_a = [asb(f"rot_a{i}", [128, 2, QKV]) for i in range(2)]
        rot_b = [asb(f"rot_b{i}", [128, 2, QKV]) for i in range(2)]
        qT = [asb(f"qT{i}", [128, 4, SEQ]) for i in range(2)]
        kT = [asb(f"kT{i}", [128, 4, SEQ]) for i in range(2)]
        vs = [asb(f"vs{i}", [128, 3, HEADS, DH + 1]) for i in range(2)]
        mx = [asb(f"mx{i}", [128, 4]) for i in range(2)]
        nb = [asb(f"nb{i}", [128, 4]) for i in range(2)]
        pr = [asb(f"pr{i}", [128, 4, 128]) for i in range(2)]
        pT = [asb(f"pT{i}", [128, 4, 128]) for i in range(2)]
        rd = [asb(f"rd{i}", [128, 4]) for i in range(2)]
        on = [asb(f"on{i}", [128, QKV]) for i in range(2)]
        oT = [asb(f"oT{i}", [128, 4, SEQ]) for i in range(2)]
        hs = asb("hs", [128, SEQ])
        a_sq = asb("a_sq", [128, SEQ])
        a_rstd = asb("a_rstd", [128, SEQ])
        a_hn = asb("a_hn", [128, SEQ])
        front, tb, sc, op = psum[0:2], psum[2:4], psum[4:6], psum[6:8]
        (ht_done, qk_done, sqk_done, ss_done, ssm_done, lss_done, est_done, step_done, rn_done, rot_done, add_done, kn_done,
         tq_done, qT_done, kT_done, v_done, vs_done, s_done, mx_done, nb_done, p_done, tp_done,
         pT_done, o_done, rd_done, on_done, to_done, oT_done, wo_done, xr_done, hs_done, ac_done,
         asq_done, avar_done, aln_done, arstd_done, ahn_done, hf_done) = [
             event("a_" + n) for n in (
                 "ht qk sqk ss ssm lss est step rn rot add kn tq qT kT v vs s mx nb p tp pT o rd on to oT wo xr "
                 "hs ac asq avar aln arstd ahn hf").split()]
        a_ctx.close()

        f_ctx = ExitStack()

        def fsb(name, shape, dt=FP32):
            return f_ctx.enter_context(nc.sbuf_tensor(name, shape, dt))

        ge = [fsb(f"ge{i}", [128, TOK]) for i in range(2)]
        mid = [fsb(f"mid{i}", [128, TOK]) for i in range(3)]
        fo = fsb("fo", [128, TOK])
        so = [fsb(f"so{i}", [128, 4, DIM]) for i in range(2)]
        gp, ap_, rp, tp = psum[0:2], psum[2:4], psum[4], psum[5]
        (g_done, ge_done, mid_done_f, w2_done, xo_done, fo_done, fT_done, so_done) = [
            event("f_" + n) for n in "g ge mid w2 xo fo fT so".split()]
        f_ctx.close()

        def tokens(buf, pair):
            return buf[:, bass.ds(pair * TOK, TOK)]

        def seqs(buf):
            return buf.rearrange("p (b s) -> p b s", b=2)

        @block.sync
        def _(sp):
            for s in loop_sems:
                sp.sem_inc(s, CREDIT)
            with nc.allow_non_contiguous_dma(reason="short vectors put one element on a partition, once"):
                for dst, src in WLOADS:
                    sp.dma_start(dst, src).then_inc(s_w, 16)
            with sp.Fori(0, PAIRS // 2) as i:
                for par in range(2):
                    pair = 2 * i + par
                    sp.wait_ge(xT_done, ev(pair - 1))
                    sp.dma_start(xin[par][:, :, :],
                                 x_rows[bass.ds(pair * TOK, TOK), :].rearrange("(t p) d -> p t d", p=128)
                                 ).then_inc(s_x[par], 16)
            with sp.Fori(0, PAIRS // 2) as i:
                for par in range(2):
                    pair = 2 * i + par
                    sp.wait_ge(so_done, ev(pair + 1))
                    sp.dma_start(out_rows[bass.ds(pair * TOK, TOK), :].rearrange("(t p) d -> p t d", p=128),
                                 so[par][:, :, :]).then_inc(s_out[par], 16)
            for par in range(2):
                sp.wait_ge(s_out[par], ev(16 * (PAIRS // 2)))

        @block.gpsimd
        def _(pool):
            for dst, src in CASTS:
                pool.dma_start(dst, src).then_inc(s_cast, 16)
            pool.memset(mean_w[:, :], 1.0 / DIM)
            pool.memset(eps[:, :], EPS)
            pool.memset(rn_shift[:, :], 0.5 * SS_BITS * math.log(2.0))
            for k, scale in enumerate((QK_SCALE, 1.0)):
                pool.memset(newton_a[:, k * HEADS:(k + 1) * HEADS], -0.5 * scale)
                pool.memset(newton_b[:, k * HEADS:(k + 1) * HEADS], 1.5 * scale)
            pool.memset(ub[:, :, :, :], 0.0)
            pool.memset(dA[0][:, :, :, :], 0.0)
            pool.memset(dA[1][:, :, :, :], 0.0).then_inc(s_set_pool, 1)

            def mamba(pair, head):
                for n in range(STATE):
                    g = pair * STATE + n
                    if head and n == 4:
                        pool.wait_ge(xs_done, ev(pair + 2))
                    pool.wait_ge(scan_done, ev(g + 1))
                    pool.wait_ge(cs_done, ev(g + 1))
                    tile = hst[n % RING][:, :, :]
                    pool.tensor_tensor(tile, tile, cs[n % 2][:, :].unsqueeze(1).broadcast_to([128, HALVES, TOK]),
                                       ALU.mult).then_inc(hc_done, 1)
                    if head and n == 4:
                        pool.tensor_copy(tokens(x1, pair + 1), xs[:, :]).then_inc(x1_done, 1)

            pool.wait_ge(xs_done, ev(1))
            pool.tensor_copy(tokens(x1, 0), xs[:, :]).then_inc(x1_done, 1)
            mamba(0, True)
            with pool.Fori(1, PAIRS - 1) as pair:
                mamba(pair, True)
            mamba(PAIRS - 1, False)
            pool.wait_ge(xf_done, ev(PAIRS))
            for layer in range(DEPTH):
                if layer:
                    pool.wait_ge(xo_done, ev(PAIRS))
                for k in range(2):
                    pool.memset(hT[k][:, :], 0.0)
                    pool.memset(vs[k][:, :, :, :], 1.0)
                pool.memset(hs[:, :], 0.0).then_inc(s_set_pool, 1)
                with pool.Fori(0, BATCH // 2) as i:
                    for par in range(2):
                        f = 2 * i + (layer * BATCH + par)
                        for t in range(2):
                            e = f * 2 + t
                            for c in range(2):
                                pool.wait_ge(rot_done, ev(e * 2 + c + 1))
                                pool.tensor_tensor(rot_a[t][:, c, :], rot_a[t][:, c, :], rot_b[t][:, c, :],
                                                   ALU.add).then_inc(add_done, 1)
                            pool.wait_ge(est_done, ev(e + 1))
                            pool.wait_ge(rn_done, ev(e))
                            pool.tensor_tensor(rn_step[:, :], rn_est[:, :], rn_est[:, :],
                                               ALU.mult).then_inc(step_done, 1)
                            for n, other in enumerate((ssm, newton_a, newton_b)):
                                pool.wait_ge(step_done, ev(e * 4 + n + 1))
                                pool.tensor_tensor(rn_step[:, :], rn_step[:, :], other[:, :],
                                                   ALU.add if n == 2 else ALU.mult).then_inc(step_done, 1)
                            pool.wait_ge(step_done, ev(e * 4 + 4))
                            pool.wait_ge(p_done, ev(4 * f - 6 + 2 * t))
                            pool.wait_ge(kn_done, ev(e - 3))
                            pool.tensor_tensor(rn[par][t][:, :], rn_est[:, :], rn_step[:, :],
                                               ALU.mult).then_inc(rn_done, 1)
                            pool.wait_ge(add_done, ev(e * 2 + 2))
                            pool.wait_ge(rn_done, ev(e + 1))
                            k3 = rot_a[t][:, 1, :].rearrange("p (h d) -> p h d", h=HEADS)
                            pool.tensor_tensor(
                                k3, k3, rn[par][t][:, HEADS:].unsqueeze(2).broadcast_to([128, HEADS, DH]),
                                ALU.mult).then_inc(kn_done, 1)

        @block.scalar
        def _(act):
            act.wait_ge(s_w, ALL_W)
            act.wait_ge(s_mod, 1)
            act.activation(condT[:, :], psum[0][:, 0:BATCH], ACT.Silu).then_inc(s_set_act, 1)
            act.activation(a_neg[:, :, :], a_neg[:, :, :], ACT.Exp).then_inc(s_set_act, 1)
            act.preload_act_table_set("natural_log_exp_and_others")
            act.wait_ge(s_set_pool, 1)
            act.wait_ge(s_set_dve, SET_DVE)

            def state(pair, par, n):
                g = pair * STATE + n
                r = n % 2
                after(act, scan_done, g - 1)
                for k in range(HALVES):
                    last = act.activation(dA[r][:, k, :, 1:], seqs(delta[par][:, k, :])[:, :, 1:],
                                          ACT.Exp, scale=a_neg[:, k, n:n + 1])
                last.then_inc(dA_done, 1)
                act.wait_ge(bcC_done, ev(g + 1))
                after(act, hc_done, g - 1)
                act.activation(cs[r][:, :], bC[:, :], ACT.Copy).then_inc(cs_done, 1)

            def head_x(f):
                act.wait_ge(xT_done, ev(f + 1))
                after(act, x1_done, f)
                after(act, cen_done, f)
                act.activation(xs[:, :], pA[:, :], ACT.Copy).then_inc(xs_done, 1)

            def head_square(f):
                act.wait_ge(cen_done, ev(f + 1))
                act.activation(sq[:, :], pB[:, :], ACT.Square).then_inc(sq_done, 1)

            def head_rstd(f):
                act.wait_ge(var_done, ev(f + 1))
                after(act, hn_done, f)
                act.activation(rstd[:, :], pA[:, :], ACT.Ln, bias=eps[:, 0:1]).then_inc(ln_done, 1)
                act.wait_ge(ln_done, ev(f + 1))
                act.activation(rstd[:, :], rstd[:, :], ACT.Exp, scale=-0.5).then_inc(rstd_done, 1)

            def head_u(f):
                for k in range(HALVES):
                    act.wait_ge(u_done, ev(f * 2 + k + 1))
                    after(act, cv_done, f * 2 - 1 + k)
                    act.activation(ub[:, k, :, TAPS - 1:], seqs((pA, pB)[k][:, :]),
                                   ACT.Copy).then_inc(ub_done, 1)

            def head_silu(f, par):
                for k in range(HALVES):
                    act.wait_ge(res_done, ev(f * 2 + k + 1))
                    after(act, z_done, f - 1)
                    act.activation(sr[par][:, k, :], (pA, pB)[k][:, :], ACT.Silu).then_inc(sr_done, 1)
                for k in range(HALVES):
                    act.wait_ge(cv_done, ev(f * 2 + k + 1))
                    after(act, yd_done, f - 1)
                    act.activation(us[par][:, k, :], cv[:, k, :, :].rearrange("p b s -> p (b s)"),
                                   ACT.Silu).then_inc(us_done, 1)
                act.preload_act_table_set("natural_log_exp_and_others")

            def head_rank(f):
                act.wait_ge(xdbl_done, ev(f + 1))
                after(act, dt_done, 2 * f)
                act.activation(dr, pA[0:RANK, :], ACT.Copy).then_inc(dr_done, 1)

            def head_softplus(f):
                for k in range(HALVES):
                    e = f * 2 + k
                    act.wait_ge(dt_done, ev(e + 1))
                    after(act, spl_done, e)
                    act.activation(sp_abs[:, :], (pB, pA)[k][:, :], ACT.Abs,
                                   bias=b_dt[:, k:k + 1]).then_inc(abs_done, 1)
                    act.wait_ge(abs_done, ev(e + 1))
                    act.activation(sp_abs[:, :], sp_abs[:, :], ACT.Exp, scale=-1.0).then_inc(exp_done, 1)
                    act.wait_ge(exp_done, ev(e + 1))
                    after(act, delta_done, f)
                    act.activation(sp_ln[:, k, :], sp_abs[:, :], ACT.Ln, bias=1.0).then_inc(spl_done, 1)

            def tail_square(e):
                act.wait_ge(cen2_done, ev(e + 1))
                after(act, xf_done, e)
                act.activation(sq2[:, :], pE[:, :], ACT.Square).then_inc(sq2_done, 1)

            def tail_rstd(e):
                act.wait_ge(var2_done, ev(e + 1))
                after(act, hn2_done, e)
                act.activation(rstd2[:, :], pB[:, :], ACT.Ln, bias=eps[:, 0:1]).then_inc(ln2_done, 1)
                act.wait_ge(ln2_done, ev(e + 1))
                act.activation(rstd2[:, :], rstd2[:, :], ACT.Exp, scale=-0.5).then_inc(rstd2_done, 1)

            def mamba(pair, par, tail, head):
                act.wait_ge(delta_done, ev(pair + 1))
                for n in range(STATE):
                    state(pair, par, n)
                    if head and n == 1:
                        head_x(pair + 1)
                    if head and n == 2:
                        head_square(pair + 1)
                    if head and n == 3:
                        head_rstd(pair + 1)
                    if head and n == 6:
                        head_u(pair + 1)
                    if tail and n == 7:
                        tail_square(pair - 1)
                    if head and n == 9:
                        head_silu(pair + 1, 1 - par)
                    if head and n == 11:
                        head_rank(pair + 1)
                    if tail and n == 11:
                        tail_rstd(pair - 1)
                    if head and n == 13:
                        head_softplus(pair + 1)

            head_x(0)
            head_square(0)
            head_rstd(0)
            head_u(0)
            head_silu(0, 0)
            head_rank(0)
            head_softplus(0)
            mamba(0, 0, False, True)
            with act.Fori(0, PAIRS // 2 - 1) as i:
                for par in (1, 0):
                    mamba(2 * i + 2 - par, par, True, True)
            mamba(PAIRS - 1, 1, True, False)
            tail_square(PAIRS - 1)
            tail_rstd(PAIRS - 1)

            def squares(f, t):
                act.wait_ge(qk_done, ev(f * 2 + t + 1))
                after(act, ss_done, f * 2 + t - 1)
                for c in range(2):
                    last = act.activation(sqk[t][:, c * QKV:(c + 1) * QKV], front[c][:, :], ACT.Square)
                last.then_inc(sqk_done, 1)

            def norms(f, t):
                e = f * 2 + t
                act.wait_ge(ssm_done, ev(e + 1))
                after(act, est_done, e)
                act.activation(ln_ss[:, :], ssm[:, :], ACT.Ln, scale=2.0 ** SS_BITS).then_inc(lss_done, 1)
                act.wait_ge(lss_done, ev(e + 1))
                after(act, rn_done, e)
                act.activation(rn_est[:, :], ln_ss[:, :], ACT.Exp, scale=-0.5,
                               bias=rn_shift[:, 0:1]).then_inc(est_done, 1)

            def keep_T(kept, events, f, par, t, bank, nth):
                act.wait_ge(tq_done, ev(nth))
                after(act, s_done, 4 * (f - 1))
                act.activation(kept[par][:, :, t * 128:(t + 1) * 128],
                               tb[bank][:, :].rearrange("p (k c) -> p k c", k=4), ACT.Copy).then_inc(events, 1)

            def keep_v(f, par, j):
                act.wait_ge(v_done, ev(f * 3 + j + 1))
                after(act, o_done, 4 * (f - 1))
                act.activation(vs[par][:, j, :, 0:DH], front[j % 2][:, :].rearrange("p (h d) -> p h d", h=HEADS),
                               ACT.Copy).then_inc(vs_done, 1)

            def exps(b, par, t, hp):
                e = b * 4 + 2 * t + hp
                act.wait_ge(nb_done, ev(e + 1))
                after(act, tp_done, e - 1)
                for k in range(4):
                    h = 2 * k + hp
                    last = act.activation(pr[hp][:, k, :], sc[hp][:, k * 128:(k + 1) * 128], ACT.Exp,
                                          scale=rn[par][t][:, h:h + 1], bias=nb[hp][:, k:k + 1])
                last.then_inc(p_done, 1)

            def keep_oT(b, par, t):
                act.wait_ge(to_done, ev(b * 2 + t + 1))
                after(act, wo_done, b - 1)
                act.activation(oT[par][:, :, t * 128:(t + 1) * 128],
                               tb[t][:, :].rearrange("p (k c) -> p k c", k=4), ACT.Copy).then_inc(oT_done, 1)

            def norm_square(e):
                act.wait_ge(ac_done, ev(e + 1))
                after(act, avar_done, e)
                act.activation(a_sq[:, :], op[1][:, 0:SEQ], ACT.Square).then_inc(asq_done, 1)

            def norm_rstd(e):
                act.wait_ge(avar_done, ev(e + 1))
                after(act, ahn_done, e)
                act.activation(a_rstd[:, :], op[0][:, 0:SEQ], ACT.Ln, bias=eps[:, 0:1]).then_inc(aln_done, 1)
                act.wait_ge(aln_done, ev(e + 1))
                act.activation(a_rstd[:, :], a_rstd[:, :], ACT.Exp, scale=-0.5).then_inc(arstd_done, 1)

            def attend(b, par, tail, head):
                f = b + 1
                exps(b, par, 0, 0)
                if head:
                    squares(f, 0)
                if tail:
                    keep_oT(b - 1, 1 - par, 1)
                keep_T(kT, kT_done, b, par, 1, 0, 4 * b + 4)
                exps(b, par, 0, 1)
                if tail:
                    norm_square(b - 1)
                    norm_rstd(b - 1)
                exps(b, par, 1, 0)
                exps(b, par, 1, 1)
                if head:
                    norms(f, 0)
                    squares(f, 1)
                keep_oT(b, par, 0)
                if head:
                    keep_T(qT, qT_done, f, 1 - par, 0, 1, 4 * f + 1)
                    keep_T(kT, kT_done, f, 1 - par, 0, 0, 4 * f + 2)
                    keep_v(f, 1 - par, 0)
                    keep_v(f, 1 - par, 1)
                    norms(f, 1)
                    keep_v(f, 1 - par, 2)
                    keep_T(qT, qT_done, f, 1 - par, 1, 1, 4 * f + 3)

            for layer in range(DEPTH):
                first, end = layer * BATCH, (layer + 1) * BATCH
                act.wait_ge(s_set_pool, 2 + layer)
                squares(first, 0)
                norms(first, 0)
                squares(first, 1)
                norms(first, 1)
                for j in range(3):
                    keep_v(first, 0, j)
                keep_T(qT, qT_done, first, 0, 0, 1, 4 * first + 1)
                keep_T(kT, kT_done, first, 0, 0, 0, 4 * first + 2)
                keep_T(qT, qT_done, first, 0, 1, 1, 4 * first + 3)
                attend(first, 0, False, True)
                with act.Fori(0, BATCH // 2 - 1) as i:
                    for par in (1, 0):
                        attend(2 * i + (first + 2 - par), par, True, True)
                attend(end - 1, 1, True, False)
                keep_oT(end - 1, 1, 1)
                norm_square(end - 1)
                norm_rstd(end - 1)
                with act.Fori(0, PAIRS // 2) as i:
                    for par in range(2):
                        pair = 2 * i + par + layer * PAIRS
                        for j, (_, m) in enumerate(HID_BLOCKS):
                            e = pair * 3 + j
                            act.wait_ge(g_done, ev(e + 1))
                            act.wait_ge(mid_done_f, ev(e - 1))
                            act.activation(ge[j % 2][0:m, :], gp[j % 2][0:m, :], ACT.Gelu,
                                           bias=b1[0:m, layer, 1, j:j + 1]).then_inc(ge_done, 1)
                        if layer == DEPTH - 1:
                            q = 2 * i + par
                            act.wait_ge(fT_done, ev(q + 1))
                            act.wait_ge(s_out[par], ev(16 * i))
                            act.activation(so[par][:, :, :].rearrange("p t d -> p (t d)"), tp[:, :],
                                           ACT.Copy).then_inc(so_done, 1)
                act.preload_act_table_set("natural_log_exp_and_others")

        @block.vector
        def _(dve):
            dve.wait_ge(s_w, ALL_W)
            half = DH // 2
            for layer in range(DEPTH):
                for c in range(2):
                    scale_of = qks[:, layer, c, :]
                    dve.tensor_tensor(tables[:, layer, :, 2 * c, :], rope[:, :, 2 * c, :],
                                      scale_of.unsqueeze(1).broadcast_to([128, 2, DH]), ALU.mult)
                    for s in range(2):
                        o = 1 - s
                        dve.tensor_tensor(tables[:, layer, :, 2 * c + 1, s * half:(s + 1) * half],
                                          rope[:, :, 2 * c + 1, s * half:(s + 1) * half],
                                          scale_of[:, o * half:(o + 1) * half].unsqueeze(1)
                                          .broadcast_to([128, 2, half]), ALU.mult)
            dve.wait_ge(s_mod, 2)
            dve.tensor_copy(mod[:, :, :], psum[1][:, 0:6 * BATCH].rearrange("p (k b) -> p k b", k=6)
                            ).then_inc(s_set_dve, 1)
            dve.wait_ge(s_set_dve, 1)
            dve.wait_ge(s_set_act, 2)
            for n, k in enumerate((1, 4)):
                dve.tensor_scalar(mod[:, k, :], mod[:, k, :], 1.0, None, ALU.add).then_inc(s_set_dve, 1)
            for n, k in enumerate((2, 5)):
                dve.tensor_scalar(gate_abs[:, n, :], mod[:, k, :], -1.0, None, ALU.mult).then_inc(s_set_dve, 1)
                dve.tensor_scalar(gate_sign[:, n, :], mod[:, k, :], 0.0, 2.0, ALU.is_ge, ALU.mult)
            dve.wait_ge(s_set_dve, 5)
            for n, k in enumerate((2, 5)):
                dve.tensor_tensor(gate_abs[:, n, :], gate_abs[:, n, :], mod[:, k, :], ALU.max).then_inc(s_set_dve, 1)
            dve.wait_ge(s_set_dve, 7)
            dve.tensor_scalar(gate_abs[:, :, :], gate_abs[:, :, :], 0.25, None, ALU.max).then_inc(s_set_dve, 1)
            dve.wait_ge(s_set_dve, 8)
            dve.scalar_tensor_tensor(mod[:, 2:6:3, :], gate_sign[:, :, :], -1.0, gate_abs[:, :, :],
                                     ALU.add, ALU.mult).then_inc(s_set_dve, 1)
            dve.tensor_scalar(a_neg[:, :, :], a_neg[:, :, :], -1.0, None, ALU.mult).then_inc(s_set_dve, 1)
            dve.wait_ge(s_set_dve, SET_DVE)
            dve.wait_ge(s_set_pool, 1)

            def scalar_of(k, pair, j):
                return mod[:, k, bass.ds(pair * 2 + j, 1)]


            def head_norm(f):
                dve.wait_ge(rstd_done, ev(f + 1))
                after(dve, res_done, 2 * f)
                dve.tensor_tensor(h_mod[:, :], pB[:, :], rstd[:, :], ALU.mult).then_inc(hn_done, 1)
                dve.wait_ge(hn_done, ev(f + 1))
                for j in range(2):
                    cols = slice(j * SEQ, (j + 1) * SEQ)
                    last = dve.tensor_scalar(h_mod[:, cols], h_mod[:, cols], scalar_of(1, f, j),
                                             scalar_of(0, f, j), ALU.mult, ALU.add)
                last.then_inc(h_done, 1)

            def head_conv(f, k, tap):
                if tap == 0:
                    dve.wait_ge(ub_done, ev(f * 2 + k + 1))
                    after(dve, us_done, f * 2 - 1 + k)
                    dve.tensor_scalar(cv[:, k, :, :], ub[:, k, :, 0:SEQ], conv_w[:, k, 0:1],
                                      conv_b[:, k:k + 1], ALU.mult, ALU.add).then_inc(conv_step, 1)
                else:
                    dve.wait_ge(conv_step, ev((f * 2 + k) * (TAPS - 1) + tap))
                    last = dve.scalar_tensor_tensor(cv[:, k, :, :], ub[:, k, :, tap:tap + SEQ],
                                                    conv_w[:, k, tap:tap + 1], cv[:, k, :, :],
                                                    ALU.mult, ALU.add)
                    last.then_inc(cv_done if tap == TAPS - 1 else conv_step, 1)

            def head_split(f, par):
                dve.wait_ge(xdbl_done, ev(f + 1))
                after(dve, bcC_done, (f - 1) * STATE)
                after(dve, split_done, f)
                bc = pA[RANK:RANK + 2 * STATE, :]
                dve.tensor_copy(parts[par][0:32, :], bc).then_inc(hi_done, 1)
                dve.wait_ge(hi_done, ev(f + 1))
                dve.tensor_tensor(rest, bc, parts[par][0:32, :], ALU.subtract).then_inc(rest_done, 1)
                dve.wait_ge(rest_done, ev(f + 1))
                dve.tensor_copy(parts[par][64:96, :], rest).then_inc(mid_done, 1)
                dve.wait_ge(mid_done, ev(f + 1))
                dve.tensor_tensor(parts[par][32:64, :], rest, parts[par][64:96, :],
                                  ALU.subtract).then_inc(split_done, 1)

            def head_delta(f, par):
                after(dve, dA_done, (f - 1) * STATE)
                for k in range(HALVES):
                    dve.wait_ge(abs_done, ev(f * 2 + k + 1))
                    dve.tensor_scalar(delta[par][:, k, :], (pB, pA)[k][:, :], b_dt[:, k:k + 1], 0.0,
                                      ALU.add, ALU.max).then_inc(pos_done, 1)
                dve.wait_ge(pos_done, ev(f * 2 + 2))
                dve.wait_ge(spl_done, ev(f * 2 + 2))
                dve.tensor_tensor(delta[par][:, :, :], delta[par][:, :, :], sp_ln[:, :, :],
                                  ALU.add).then_inc(delta_done, 1)
                dve.wait_ge(delta_done, ev(f + 1))
                dve.tensor_tensor(du[par][:, :, :], delta[par][:, :, :], us[par][:, :, :],
                                  ALU.mult).then_inc(du_done, 1)

            def state(pair, par, n):
                g = pair * STATE + n
                r = n % 2
                dve.wait_ge(bcB_done, ev(g + 1))
                after(dve, y_done, g + 1 - RING)
                tile = hst[n % RING]
                dve.tensor_tensor(tile[:, :, :], du[par][:, :, :],
                                  bB[r][:, :].unsqueeze(1).broadcast_to([128, HALVES, TOK]),
                                  ALU.mult).then_inc(dBu_done, 1)
                dve.wait_ge(dBu_done, ev(g + 1))
                dve.wait_ge(dA_done, ev(g + 1))
                flat = tile[:, :, :].rearrange("p k s -> p (k s)")
                dve.tensor_tensor_scan(flat, dA[r][:, :, :, :].rearrange("p k b s -> p (k b s)"), flat,
                                       0.0, ALU.mult, ALU.add).then_inc(scan_done, 1)

            def tail_gate(e, par):
                dve.wait_ge(y_done, ev(e * STATE + STATE))
                after(dve, out_done, e)
                for k in range(HALVES):
                    last = dve.scalar_tensor_tensor(z[:, k, :], us[par][:, k, :], skip_d[:, k:k + 1],
                                                    yp[k][:, :], ALU.mult, ALU.add)
                last.then_inc(yd_done, 1)
                dve.wait_ge(yd_done, ev(e + 1))
                dve.tensor_tensor(z[:, :, :], z[:, :, :], sr[par][:, :, :], ALU.mult).then_inc(z_done, 1)

            def tail_residual(e):
                dve.wait_ge(out_done, ev(e + 1))
                dve.wait_ge(x1_done, ev(e + 1))
                for j in range(2):
                    cur = x1[:, bass.ds(e * TOK + j * SEQ, SEQ)]
                    last = dve.scalar_tensor_tensor(cur, pE[:, j * SEQ:(j + 1) * SEQ], scalar_of(2, e, j),
                                                    cur, ALU.mult, ALU.add)
                last.then_inc(xn_done, 1)

            def tail_norm(e):
                dve.wait_ge(rstd2_done, ev(e + 1))
                dve.tensor_tensor(sq2[:, :], pE[:, :], rstd2[:, :], ALU.mult).then_inc(hn2_done, 1)
                dve.wait_ge(hn2_done, ev(e + 1))
                for j in range(2):
                    last = dve.tensor_scalar(xf[:, bass.ds(e * TOK + j * SEQ, SEQ)],
                                             sq2[:, j * SEQ:(j + 1) * SEQ], scalar_of(4, e, j),
                                             scalar_of(3, e, j), ALU.mult, ALU.add)
                last.then_inc(xf_done, 1)

            def mamba(pair, par, tail, head):
                dve.wait_ge(du_done, ev(pair + 1))
                for n in range(STATE):
                    state(pair, par, n)
                    if tail and n == 2:
                        tail_gate(pair - 1, 1 - par)
                    if head and n == 4:
                        head_norm(pair + 1)
                    if tail and n == 5:
                        tail_residual(pair - 1)
                    if head and n in (7, 8):
                        for tap in range(TAPS):
                            head_conv(pair + 1, n - 7, tap)
                    if head and n == 11:
                        head_split(pair + 1, 1 - par)
                    if tail and n == 12:
                        tail_norm(pair - 1)
                    if head and n == 14:
                        head_delta(pair + 1, 1 - par)

            head_norm(0)
            for k in range(HALVES):
                for tap in range(TAPS):
                    head_conv(0, k, tap)
            head_split(0, 0)
            head_delta(0, 0)
            mamba(0, 0, False, True)
            with dve.Fori(0, PAIRS // 2 - 1) as i:
                for par in (1, 0):
                    mamba(2 * i + 2 - par, par, True, True)
            mamba(PAIRS - 1, 1, True, False)
            tail_gate(PAIRS - 1, 1)
            tail_residual(PAIRS - 1)
            tail_norm(PAIRS - 1)

            def shifted(dst, b):
                dve.tensor_scalar(dst[0:64, :], xf[0:64, bass.ds(b * SEQ, SEQ)], 1.0, None, ALU.mult)
                return dve.tensor_scalar(dst[64:128, 1:SEQ], xf[64:128, bass.ds(b * SEQ, SEQ - 1)],
                                         1.0, None, ALU.mult)

            def shift_in(f, par, first):
                after(dve, v_done, 3 * (f - 1))
                shifted(hT[par], f - first).then_inc(ht_done, 1)

            def rotate(f, layer, t, c):
                e = f * 2 + t
                dve.wait_ge(sqk_done, ev(e + 1))
                after(dve, tq_done, 2 * e - 2)
                after(dve, add_done, 2 * e - 2)
                src = front[c][:, :].rearrange("p (h d) -> p h d", h=HEADS)
                table = tables[:, layer, t, 2 * c, :].unsqueeze(1).broadcast_to([128, HEADS, DH])
                dve.tensor_tensor(rot_a[t][:, c, :].rearrange("p (h d) -> p h d", h=HEADS),
                                  src, table, ALU.mult)
                for s in range(2):
                    o = 1 - s
                    table = tables[:, layer, t, 2 * c + 1, s * half:(s + 1) * half]
                    last = dve.tensor_tensor(
                        rot_b[t][:, c, :].rearrange("p (h d) -> p h d", h=HEADS)[:, :, s * half:(s + 1) * half],
                        src[:, :, o * half:(o + 1) * half],
                        table.unsqueeze(1).broadcast_to([128, HEADS, half]), ALU.mult)
                last.then_inc(rot_done, 1)

            def norm_sums(f, t):
                e = f * 2 + t
                after(dve, ssm_done, e)
                dve.tensor_reduce(ss[:, :], sqk[t][:, :].rearrange("p (h d) -> p h d", d=DH),
                                  AX.X, ALU.add).then_inc(ss_done, 1)
                dve.wait_ge(ss_done, ev(e + 1))
                after(dve, rn_done, e)
                dve.tensor_scalar(ssm[:, :], ss[:, :], 1e-24, None, ALU.max).then_inc(ssm_done, 1)

            def maxima(b, par, t):
                for hp in range(2):
                    e = b * 4 + 2 * t + hp
                    dve.wait_ge(s_done, ev(e + 1))
                    after(dve, nb_done, e - 1)
                    dve.tensor_reduce(mx[hp][:, :], sc[hp][:, :].rearrange("p (k j) -> p k j", k=4),
                                      AX.X, ALU.max).then_inc(mx_done, 1)
                    dve.wait_ge(mx_done, ev(e + 1))
                    after(dve, p_done, e - 1)
                    dve.wait_ge(rn_done, ev(b * 2 + t + 1))
                    dve.scalar_tensor_tensor(nb[hp][:, :], mx[hp][:, :], -1.0,
                                             rn[par][t][:, hp:HEADS:2], ALU.mult, ALU.mult).then_inc(nb_done, 1)

            def keep_pT(b, t):
                for hp in range(2):
                    e = b * 4 + 2 * t + hp
                    dve.wait_ge(tp_done, ev(e + 1))
                    after(dve, o_done, e - 1)
                    dve.tensor_copy(pT[hp][:, :, :].rearrange("p k j -> p (k j)"),
                                    tb[hp][:, :]).then_inc(pT_done, 1)

            def normalise(b, t):
                for hp in range(2):
                    e = b * 4 + 2 * t + hp
                    o4 = op[hp][:, 0:4 * (DH + 1)].rearrange("p (k d) -> p k d", k=4)
                    dve.wait_ge(o_done, ev(e + 1))
                    after(dve, on_done, e - 1)
                    dve.reciprocal(rd[hp][:, :], o4[:, :, DH]).then_inc(rd_done, 1)
                    dve.wait_ge(rd_done, ev(e + 1))
                    after(dve, to_done, b * 2 + t - 1)
                    dve.tensor_tensor(
                        on[t][:, :].rearrange("p (k s d) -> p k s d", k=4, s=2)[:, :, hp, :],
                        o4[:, :, 0:DH], rd[hp][:, :].unsqueeze(2).broadcast_to([128, 4, DH]),
                        ALU.mult).then_inc(on_done, 1)

            def residual(e, first):
                dve.wait_ge(wo_done, ev(e + 1))
                cur = xf[:, bass.ds((e - first) * SEQ, SEQ)]
                dve.tensor_tensor(cur, op[0][:, 0:SEQ], cur, ALU.add).then_inc(xr_done, 1)
                dve.wait_ge(xr_done, ev(e + 1))
                after(dve, ac_done, e)
                shifted(hs, e - first).then_inc(hs_done, 1)

            def norm_out(e, first, layer):
                dve.wait_ge(arstd_done, ev(e + 1))
                after(dve, hf_done, e)
                dve.tensor_tensor(a_hn[:, :], op[1][:, 0:SEQ], a_rstd[:, :], ALU.mult).then_inc(ahn_done, 1)
                dve.wait_ge(ahn_done, ev(e + 1))
                dve.tensor_scalar(hf[:, bass.ds((e - first) * SEQ, SEQ)], a_hn[:, :], ln_g[:, layer:layer + 1],
                                  ln_b[:, layer:layer + 1], ALU.mult, ALU.add).then_inc(hf_done, 1)

            def attend(b, par, first, layer, tail, head):
                f = b + 1
                if head:
                    shift_in(f, 1 - par, first)
                maxima(b, par, 0)
                if head:
                    rotate(f, layer, 0, 0)
                    norm_sums(f, 0)
                if tail:
                    residual(b - 1, first)
                keep_pT(b, 0)
                if head:
                    rotate(f, layer, 0, 1)
                maxima(b, par, 1)
                if tail:
                    norm_out(b - 1, first, layer)
                normalise(b, 0)
                keep_pT(b, 1)
                if head:
                    rotate(f, layer, 1, 0)
                    rotate(f, layer, 1, 1)
                    norm_sums(f, 1)
                normalise(b, 1)

            dve.wait_ge(xf_done, ev(PAIRS))
            for layer in range(DEPTH):
                first, end = layer * BATCH, (layer + 1) * BATCH
                dve.wait_ge(s_set_pool, 2 + layer)
                if layer:
                    dve.wait_ge(xo_done, ev(PAIRS))
                shift_in(first, 0, first)
                for t in range(2):
                    rotate(first, layer, t, 0)
                    rotate(first, layer, t, 1)
                    norm_sums(first, t)
                attend(first, 0, first, layer, False, True)
                with dve.Fori(0, BATCH // 2 - 1) as i:
                    for par in (1, 0):
                        attend(2 * i + (first + 2 - par), par, first, layer, True, True)
                attend(end - 1, 1, first, layer, True, False)
                residual(end - 1, first)
                norm_out(end - 1, first, layer)
                with dve.Fori(0, PAIRS // 2) as i:
                    for par in range(2):
                        q = 2 * i + par
                        pair = q + layer * PAIRS
                        for j, (_, m) in enumerate(HID_BLOCKS):
                            e = pair * 3 + j
                            dve.wait_ge(ge_done, ev(e + 1))
                            dve.wait_ge(w2_done, ev(pair))
                            dve.scalar_tensor_tensor(mid[j][0:m, :], ap_[j % 2][0:m, :],
                                                     b1[0:m, layer, 0, j:j + 1], ge[j % 2][0:m, :],
                                                     ALU.add, ALU.mult).then_inc(mid_done_f, 1)
                        dve.wait_ge(w2_done, ev(pair + 1))
                        dve.scalar_tensor_tensor(tokens(xf, q), rp[:, :], b2[:, layer:layer + 1],
                                                 tokens(xf, q), ALU.add, ALU.add).then_inc(xo_done, 1)
                        if layer == DEPTH - 1:
                            dve.wait_ge(xo_done, ev(pair + 1))
                            dve.wait_ge(fT_done, ev(q))
                            for j in range(2):
                                at = bass.ds(q * TOK + j * SEQ, SEQ)
                                last = dve.scalar_tensor_tensor(fo[:, j * SEQ:(j + 1) * SEQ], xf[:, at],
                                                                scalar_of(5, q, j), x1[:, at],
                                                                ALU.mult, ALU.add)
                            last.then_inc(fo_done, 1)

        @block.tensor
        def _(pe):
            pe.wait_ge(s_w, ALL_W)
            pe.wait_ge(s_cast, 16 * len(CASTS))
            pe.transpose(psum[0][:, 0:BATCH], cond[:, :], ident[0:32, 0:32]).then_inc(s_mod, 1)
            pe.wait_ge(s_set_act, 1)
            for k in range(6):
                last = pe.matmul(psum[1][:, k * BATCH:(k + 1) * BATCH], wmod[:, k * DIM:(k + 1) * DIM],
                                 condT[:, :], start=True, stop=True)
            last.then_inc(s_mod, 1)
            pe.wait_ge(s_set_dve, SET_DVE)
            pe.wait_ge(s_set_pool, 1)


            def head_transpose(f, par, loads):
                pe.wait_ge(s_x[par], ev(16 * loads))
                after(pe, pos_done, 2 * f)
                for t in range(4):
                    last = pe.transpose(pA[:, t * 128:(t + 1) * 128], xin[par][:, t, :], ident[:, :])
                last.then_inc(xT_done, 1)

            def head_center(f):
                pe.wait_ge(xs_done, ev(f + 1))
                pe.matmul(pB[:, :], center[:, :], xs[:, :], start=True, stop=True).then_inc(cen_done, 1)

            def head_var(f):
                pe.wait_ge(sq_done, ev(f + 1))
                pe.matmul(pA[:, :], mean_w[:, :], sq[:, :], start=True, stop=True).then_inc(var_done, 1)

            def head_u(f):
                pe.wait_ge(h_done, ev(f + 1))
                for k in range(HALVES):
                    pe.matmul((pA, pB)[k][:, :], w_in[:, k * 128:(k + 1) * 128], h_mod[:, :],
                              start=True, stop=True).then_inc(u_done, 1)

            def head_res(f):
                for k in range(HALVES):
                    pe.wait_ge(ub_done, ev(f * 2 + k + 1))
                    pe.matmul((pA, pB)[k][:, :], w_in[:, INNER + k * 128:INNER + (k + 1) * 128],
                              h_mod[:, :], start=True, stop=True).then_inc(res_done, 1)

            def head_xdbl(f, par):
                pe.wait_ge(us_done, ev(f * 2 + 2))
                for k in range(HALVES):
                    last = pe.matmul(pA[0:RANK + 2 * STATE, :], w_x[:, k, :], us[par][:, k, :],
                                     start=(k == 0), stop=(k == HALVES - 1))
                last.then_inc(xdbl_done, 1)

            def head_dt(f):
                pe.wait_ge(dr_done, ev(f + 1))
                after(pe, ln2_done, f - 1)
                pe.matmul(pB[:, :], w_dt[:, 0:128], dr, start=True, stop=True).then_inc(dt_done, 1)
                pe.wait_ge(rest_done, ev(f + 1))
                pe.matmul(pA[:, :], w_dt[:, 128:256], dr, start=True, stop=True).then_inc(dt_done, 1)

            def tail_out(e):
                pe.wait_ge(z_done, ev(e + 1))
                after(pe, hn2_done, e)
                for k in range(HALVES):
                    last = pe.matmul(pE[:, :], w_out[:, k, :], z[:, k, :], start=(k == 0),
                                     stop=(k == HALVES - 1))
                last.then_inc(out_done, 1)

            def tail_center(e):
                pe.wait_ge(xn_done, ev(e + 1))
                pe.matmul(pE[:, :], center[:, :], tokens(x1, e), start=True, stop=True).then_inc(cen2_done, 1)

            def tail_var(e, head):
                pe.wait_ge(sr_done if head else pos_done, ev(2 * e + 6) if head else ev(2 * PAIRS))
                pe.wait_ge(sq2_done, ev(e + 1))
                pe.matmul(pB[:, :], mean_w[:, :], sq2[:, :], start=True, stop=True).then_inc(var2_done, 1)

            def broadcast(pair, par, n):
                g = pair * STATE + n
                r = n % 2
                after(pe, dBu_done, g - 1)
                pe.matmul(bB[r][:, :], sel[:, n, :], parts[par][:, :], start=True,
                          stop=True).then_inc(bcB_done, 1)
                after(pe, cs_done, g)
                pe.matmul(bC[:, :], sel[:, STATE + n, :], parts[par][:, :], start=True,
                          stop=True).then_inc(bcC_done, 1)

            def reduce_state(pair, n):
                if n == 0:
                    after(pe, yd_done, pair)
                pe.wait_ge(hc_done, ev(pair * STATE + n + 1))
                for k in range(HALVES):
                    last = pe.matmul(yp[k][:, :], ident[:, :], hst[n % RING][:, k, :],
                                     start=(n == 0), stop=(n == STATE - 1))
                last.then_inc(y_done, 1)

            def mamba(pair, par, tail, head, loads=None):
                pe.wait_ge(split_done, ev(pair + 1))
                broadcast(pair, par, 0)
                for n in range(STATE):
                    if n + 1 < STATE:
                        broadcast(pair, par, n + 1)
                    if head and n == 0:
                        head_transpose(pair + 1, 1 - par, loads)
                    if head and n == 1:
                        head_center(pair + 1)
                    if head and n == 2:
                        head_var(pair + 1)
                    if tail and n == 4:
                        tail_out(pair - 1)
                    if head and n == 5:
                        head_u(pair + 1)
                    if tail and n == 6:
                        tail_center(pair - 1)
                    if head and n == 7:
                        head_res(pair + 1)
                    if tail and n == 10:
                        tail_var(pair - 1, head)
                    if head and n == 10:
                        head_xdbl(pair + 1, 1 - par)
                    if head and n == 12:
                        head_dt(pair + 1)
                    if n >= LAG:
                        reduce_state(pair, n - LAG)
                    elif tail:
                        reduce_state(pair - 1, n - LAG + STATE)

            head_transpose(0, 0, 1)
            head_center(0)
            head_var(0)
            head_u(0)
            head_res(0)
            head_xdbl(0, 0)
            head_dt(0)
            mamba(0, 0, False, True, 1)
            with pe.Fori(0, PAIRS // 2 - 1) as i:
                for par in (1, 0):
                    mamba(2 * i + 2 - par, par, True, True, i + 2)
            mamba(PAIRS - 1, 1, True, False)
            for n in range(STATE - LAG, STATE):
                reduce_state(PAIRS - 1, n)
            tail_out(PAIRS - 1)
            tail_center(PAIRS - 1)
            tail_var(PAIRS - 1, False)

            def q_k(f, par, layer, t):
                pe.wait_ge(ht_done, ev(f + 1))
                for c in range(2):
                    if t:
                        pe.wait_ge(rot_done, ev(f * 4 + c + 1))
                    else:
                        after(pe, vs_done, 3 * f)
                    last = pe.matmul(front[c][:, :], hT[par][:, t * 128:(t + 1) * 128],
                                     wqkv[:, layer, c * QKV:(c + 1) * QKV], start=True, stop=True)
                last.then_inc(qk_done, 1)

            def v_rows(f, par, layer, j):
                if j == 2:
                    pe.wait_ge(vs_done, ev(f * 3 + 1))
                else:
                    pe.wait_ge(rot_done, ev(f * 4 + j + 3))
                pe.matmul(front[j % 2][:, :], hT[par][:, j * 64:j * 64 + 128],
                          wqkv[:, layer, 2 * QKV:3 * QKV], start=True, stop=True).then_inc(v_done, 1)

            def transpose_q(f, t, bank):
                pe.wait_ge(add_done, ev(f * 4 + 2 * t + 1))
                for k in range(4):
                    last = pe.transpose(tb[bank][:, k * 128:(k + 1) * 128],
                                        rot_a[t][:, 0, k * 128:(k + 1) * 128], ident[:, :])
                last.then_inc(tq_done, 1)

            def transpose_k(f, t, bank):
                pe.wait_ge(kn_done, ev(f * 2 + t + 1))
                for k in range(4):
                    last = pe.transpose(tb[bank][:, k * 128:(k + 1) * 128],
                                        rot_a[t][:, 1, k * 128:(k + 1) * 128], ident[:, :])
                last.then_inc(tq_done, 1)

            def scores(b, par, t, hp):
                e = b * 4 + 2 * t + hp
                rows = slice(64 * hp, 64 * hp + 64)
                after(pe, p_done, e - 1)
                pe.wait_ge(qT_done, ev(2 * b + 1 + t))
                pe.wait_ge(kT_done, ev(2 * b + 1 + t))
                pe.matmul(sc[hp][:, :], identb[:, :],
                          mask[:, t, :].unsqueeze(1).broadcast_to([128, 4, 128]),
                          start=True, stop=False, skip_group_check=True)
                for k in range(4):
                    cols = slice(k * 128, (k + 1) * 128)
                    if t == 0:
                        last = pe.matmul(sc[hp][:, cols], qT[par][rows, k, 0:128], kT[par][rows, k, 0:128],
                                         start=False, stop=True, skip_group_check=True)
                    else:
                        for w in range(2):
                            last = pe.matmul(sc[hp][64 * w:64 * w + 64, cols],
                                             qT[par][rows, k, 128 + 64 * w:192 + 64 * w],
                                             kT[par][rows, k, 64 + 64 * w:192 + 64 * w],
                                             start=False, stop=True, skip_group_check=True)
                last.then_inc(s_done, 1)

            def transpose_p(b, t, hp):
                e = b * 4 + 2 * t + hp
                pe.wait_ge(p_done, ev(e + 1))
                for k in range(4):
                    last = pe.transpose(tb[hp][:, k * 128:(k + 1) * 128], pr[hp][:, k, :], ident[:, :])
                last.then_inc(tp_done, 1)

            def values(b, par, t, hp):
                e = b * 4 + 2 * t + hp
                pe.wait_ge(pT_done, ev(e + 1))
                if t == 0:
                    after(pe, ahn_done, b)
                    pe.wait_ge(vs_done, ev(b * 3 + 3))
                after(pe, on_done, e - 1)
                for k in range(4):
                    h = 2 * k + hp
                    cols = slice(k * (DH + 1), (k + 1) * (DH + 1))
                    if t == 0:
                        last = pe.matmul(op[hp][:, cols], pT[hp][:, k, :], vs[par][:, 0, h, :],
                                         start=True, stop=True)
                    else:
                        for w in range(2):
                            last = pe.matmul(op[hp][64 * w:64 * w + 64, cols],
                                             pT[hp][:, k, 64 * w:64 * w + 64],
                                             vs[par][:, 1 + w, h, :], start=True, stop=True)
                last.then_inc(o_done, 1)

            def transpose_o(b, t):
                pe.wait_ge(on_done, ev(b * 4 + 2 * t + 2))
                for k in range(4):
                    last = pe.transpose(tb[t][:, k * 128:(k + 1) * 128],
                                        on[t][:, k * 128:(k + 1) * 128], ident[:, :])
                last.then_inc(to_done, 1)

            def project(e, par, layer):
                pe.wait_ge(on_done, ev(4 * e + 4))
                pe.wait_ge(oT_done, ev(e * 2 + 2))
                for k in range(4):
                    last = pe.matmul(op[0][:, 0:SEQ], wo[:, layer, k, :], oT[par][:, k, :],
                                     start=(k == 0), stop=(k == 3))
                last.then_inc(wo_done, 1)

            def norm_center(e):
                pe.wait_ge(hs_done, ev(e + 1))
                pe.matmul(op[1][:, 0:SEQ], center[:, :], hs[:, :], start=True, stop=True).then_inc(ac_done, 1)

            def norm_var(e):
                pe.wait_ge(asq_done, ev(e + 1))
                pe.matmul(op[0][:, 0:SEQ], mean_w[:, :], a_sq[:, :], start=True, stop=True).then_inc(avar_done, 1)

            def attend(b, par, layer, tail, head):
                f = b + 1
                scores(b, par, 0, 0)
                scores(b, par, 0, 1)
                if head:
                    q_k(f, 1 - par, layer, 0)
                if tail:
                    pe.wait_ge(qT_done, ev(2 * b + 2))
                    transpose_o(b - 1, 1)
                pe.wait_ge(kT_done, ev(2 * b + 1))
                transpose_k(b, 1, 0)
                if tail:
                    project(b - 1, 1 - par, layer)
                pe.wait_ge(kT_done, ev(2 * b + 2))
                transpose_p(b, 0, 0)
                if tail:
                    pe.wait_ge(oT_done, ev(2 * b))
                transpose_p(b, 0, 1)
                scores(b, par, 1, 0)
                if tail:
                    norm_center(b - 1)
                scores(b, par, 1, 1)
                if tail:
                    norm_var(b - 1)
                if head:
                    q_k(f, 1 - par, layer, 1)
                values(b, par, 0, 0)
                pe.wait_ge(pT_done, ev(4 * b + 1))
                transpose_p(b, 1, 0)
                values(b, par, 0, 1)
                pe.wait_ge(pT_done, ev(4 * b + 2))
                transpose_p(b, 1, 1)
                pe.wait_ge(pT_done, ev(4 * b + 3))
                transpose_o(b, 0)
                if head:
                    pe.wait_ge(pT_done, ev(4 * b + 4))
                    transpose_q(f, 0, 1)
                values(b, par, 1, 0)
                values(b, par, 1, 1)
                if head:
                    v_rows(f, 1 - par, layer, 0)
                    pe.wait_ge(oT_done, ev(2 * b + 1))
                    transpose_k(f, 0, 0)
                    v_rows(f, 1 - par, layer, 1)
                    pe.wait_ge(qT_done, ev(2 * f + 1))
                    transpose_q(f, 1, 1)
                    v_rows(f, 1 - par, layer, 2)

            for layer in range(DEPTH):
                first, end = layer * BATCH, (layer + 1) * BATCH
                pe.wait_ge(s_set_pool, 2 + layer)
                q_k(first, 0, layer, 0)
                q_k(first, 0, layer, 1)
                for j in range(3):
                    v_rows(first, 0, layer, j)
                after(pe, oT_done, 2 * first)
                transpose_q(first, 0, 1)
                transpose_k(first, 0, 0)
                pe.wait_ge(qT_done, ev(2 * first + 1))
                transpose_q(first, 1, 1)
                attend(first, 0, layer, False, True)
                with pe.Fori(0, BATCH // 2 - 1) as i:
                    for par in (1, 0):
                        attend(2 * i + (first + 2 - par), par, layer, True, True)
                attend(end - 1, 1, layer, True, False)
                pe.wait_ge(pT_done, ev(4 * end))
                transpose_o(end - 1, 1)
                project(end - 1, 1, layer)
                norm_center(end - 1)
                norm_var(end - 1)
                pe.wait_ge(hf_done, ev((layer + 1) * BATCH))
                with pe.Fori(0, PAIRS // 2) as i:
                    for par in range(2):
                        q = 2 * i + par
                        pair = q + layer * PAIRS
                        for j, (at, m) in enumerate(HID_BLOCKS):
                            e = pair * 3 + j
                            pe.wait_ge(mid_done_f, ev(e - 1))
                            pe.matmul(gp[j % 2][0:m, :], w1[:, layer, HID + at:HID + at + m],
                                      tokens(hf, q), start=True, stop=True)
                            pe.matmul(ap_[j % 2][0:m, :], w1[:, layer, at:at + m], tokens(hf, q),
                                      start=True, stop=True).then_inc(g_done, 1)
                        pe.wait_ge(xo_done, ev(pair))
                        for j, (at, m) in enumerate(HID_BLOCKS):
                            pe.wait_ge(mid_done_f, ev(pair * 3 + j + 1))
                            last = pe.matmul(rp[:, :], w2[0:m, layer, j, :], mid[j][0:m, :],
                                             start=(j == 0), stop=(j == 2))
                        last.then_inc(w2_done, 1)
                        if layer == DEPTH - 1:
                            pe.wait_ge(fo_done, ev(q + 1))
                            pe.wait_ge(so_done, ev(q))
                            for t in range(4):
                                last = pe.transpose(tp[:, t * 128:(t + 1) * 128],
                                                    fo[:, t * 128:(t + 1) * 128], ident[:, :])
                            last.then_inc(fT_done, 1)


_NAMES = {
    "L0_attn_x": "x", "L0_attn_W_in": "W_in", "L0_attn_conv_w": "conv_w", "L0_attn_conv_b": "conv_b",
    "L0_attn_W_x": "W_x", "L0_attn_W_dt": "W_dt", "L0_attn_b_dt": "b_dt", "L0_attn_A_log": "A_log",
    "L0_attn_D": "D", "L0_attn_W_out": "W_out", "L0_ffn_wqkv": "wqkv", "L0_ffn_q_scale": "q_scale",
    "L0_ffn_k_scale": "k_scale", "L0_ffn_wo": "wo", "L0_ffn_ln_g": "ln_g", "L0_ffn_ln_b": "ln_b",
    "L0_ffn_w1": "w1", "L0_ffn_b1": "b1", "L0_ffn_w2": "w2", "L0_ffn_b2": "b2", "L0_c": "c",
    "L0_wmod": "wmod",
}


def kernel(**inputs):
    import numpy as _np
    import concourse.bacc as _bacc
    from concourse import mybir as _mybir
    from concourse.bass_utils import run_bass_kernel_spmd as _run

    nc = _bacc.Bacc("TRN2", target_bir_lowering=False, num_devices=1)
    arrays, args = {}, {}
    given = {short: _np.ascontiguousarray(inputs[name]) for name, short in _NAMES.items()}
    given.update(shape_constants())
    for short, a in given.items():
        arrays[f"in_{short}"] = a
        args[short] = nc.dram_tensor(f"in_{short}", a.shape, _mybir.dt.from_np(a.dtype),
                                     kind="ExternalInput").ap()
    out = nc.dram_tensor("out_0", (BATCH, SEQ, DIM), _mybir.dt.float32, kind="ExternalOutput").ap()
    block_kernel(nc, args, out)
    r = _run(nc, [arrays], core_ids=[0])
    return r.results[0]["out_0"]
```

```python
import math

import concourse.bass as bass
import numpy as np
from concourse import mybir
from contextlib import ExitStack

FP32 = mybir.dt.float32
BF16 = mybir.dt.bfloat16
ALU = mybir.AluOpType
ACT = mybir.ActivationFunctionType
AX = mybir.AxisListType

BATCH, SEQ, DIM = 32, 256, 128
INNER = 256
HALVES = INNER // 128
STATE = 16
TAPS = 4
RING = 4
LAG = 2
RANK = 64
DEPTH = 2
HEADS, DH = 8, 64
WINDOW = 64
QKV = HEADS * DH
HID = 341
HID_BLOCKS = [(0, 128), (128, 128), (256, HID - 256)]
TOK = 512
PAIRS = BATCH // 2
QK_SCALE = 8.0
MASKED = -1.0e30
EPS = 1e-5
SS_BITS = 18

CREDIT = 8


def shape_constants():
    ident = np.eye(128, dtype=np.float32)
    center = (ident - np.float32(1.0 / 128)).astype(np.float32)
    sel = np.zeros((96, 32, 128), np.float32)
    for n in range(32):
        for part in range(3):
            sel[32 * part + n, n, :] = 1.0
    i = np.arange(128)[:, None]
    j = np.arange(128)[None, :]
    near = i - j
    far = WINDOW + (i % WINDOW) - j
    mask = np.stack([np.where((d >= 0) & (d <= WINDOW), 0.0, MASKED) for d in (near, far)], 1)
    half = np.arange(0, DH, 2, dtype=np.float32)
    inv = (np.float32(1.0) / np.float32(10000.0) ** (half / np.float32(DH))).astype(np.float32)
    t = np.arange(SEQ, dtype=np.float32)
    freqs = t[:, None] * inv[None, :]
    freqs = np.concatenate([freqs, freqs], -1).astype(np.float32)
    base = ((half + np.float32(0.4 * DH)) / np.float32(1.4 * DH)).astype(np.float32)
    power = ((t - SEQ // 2) / np.float32(WINDOW // 2)).astype(np.float32)
    scale = (base[None, :] ** power[:, None]).astype(np.float32)
    scale = np.concatenate([scale, scale], -1)
    sign = np.where(np.arange(DH) < DH // 2, -1.0, 1.0).astype(np.float32)
    cos, sin = np.cos(freqs), np.sin(freqs) * sign
    rope = np.stack([cos * scale, sin * scale, cos / scale, sin / scale], 1).astype(np.float32)
    rope = rope.reshape(2, 128, 4, DH).transpose(1, 0, 2, 3)
    return {
        "c_ident": ident, "c_center": center, "c_sel": sel.reshape(96, 32 * 128),
        "c_mask": mask.astype(np.float32).reshape(128, 256),
        "c_rope": np.ascontiguousarray(rope).reshape(128, 2 * 4 * DH),
    }


def ev(count):
    return count + CREDIT


def after(eng, sem, count):
    if not isinstance(count, int) or count > 0:
        eng.wait_ge(sem, ev(count))


def block_kernel(nc, a, out):
    ctx = ExitStack()
    with ctx:
        def sb(name, shape, dt=FP32):
            return ctx.enter_context(nc.sbuf_tensor(name, shape, dt))

        def sem(name):
            return ctx.enter_context(nc.semaphore(name))

        loop_sems = []

        def event(name):
            loop_sems.append(sem(name))
            return loop_sems[-1]

        ident = sb("ident", [128, 128])
        identb = sb("identb", [128, 128], BF16)
        center = sb("center", [128, 128])
        mean_w = sb("mean_w", [128, 128])
        mask = sb("mask", [128, 2, 128], BF16)
        tables = sb("tables", [128, DEPTH, 2, 4, DH])
        conv_w = sb("conv_w", [128, HALVES, TAPS])
        conv_b = sb("conv_b", [128, HALVES])
        b_dt = sb("b_dt", [128, HALVES])
        a_neg = sb("a_neg", [128, HALVES, STATE])
        skip_d = sb("skip_d", [128, HALVES])
        wqkv = sb("wqkv", [128, DEPTH, 3 * QKV])
        wo = sb("wo", [128, DEPTH, 4, DIM])
        ln_g = sb("ln_g", [128, DEPTH])
        ln_b = sb("ln_b", [128, DEPTH])
        w1 = sb("w1", [128, DEPTH, 2 * HID])
        b1 = sb("b1", [128, DEPTH, 2, 3])
        w2 = sb("w2", [128, DEPTH, 3, DIM])
        b2 = sb("b2", [128, DEPTH])
        eps = sb("eps", [128, 1])
        rn_shift = sb("rn_shift", [128, 1])
        newton_a = sb("newton_a", [128, 2 * HEADS])
        newton_b = sb("newton_b", [128, 2 * HEADS])
        mod = sb("mod", [128, 6, BATCH])

        x1 = sb("x1", [128, BATCH * SEQ])
        xf = sb("xf", [128, BATCH * SEQ])

        psum = [ctx.enter_context(nc.psum_tensor(f"bank{i}", [128, 512], FP32)) for i in range(8)]

        s_first = sem("s_first")
        s_w = sem("s_w")
        s_cast = sem("s_cast")
        s_mod = sem("s_mod")
        s_set_act = sem("s_set_act")
        s_set_dve = sem("s_set_dve")
        s_set_pool = sem("s_set_pool")
        s_x = [event("s_x0"), event("s_x1")]
        s_out = [event("s_out0"), event("s_out1")]

        MOD_DVE, SET_DVE = 9, 10
        x_rows = a["x"].rearrange("b s d -> (b s) d")
        out_rows = out.rearrange("b s d -> (b s) d")

        with ExitStack() as s_ctx:
            def ssb(name, shape):
                return s_ctx.enter_context(nc.sbuf_tensor(name, shape, FP32))

            rope = ssb("rope", [128, 2, 4, DH])
            qks = ssb("qks", [128, DEPTH, 2, DH])
            cond = ssb("cond", [32, DIM])
            wmod = ssb("wmod", [128, 6 * DIM])
            condT = ssb("condT", [128, BATCH])
            gate_abs = ssb("gate_abs", [128, 2, BATCH])
            gate_sign = ssb("gate_sign", [128, 2, BATCH])
        m_ctx = ExitStack()

        def msb(name, shape, dt=FP32):
            return m_ctx.enter_context(nc.sbuf_tensor(name, shape, dt))

        us = [msb(f"us{i}", [128, HALVES, TOK]) for i in range(2)]
        sr = [msb(f"sr{i}", [128, HALVES, TOK]) for i in range(2)]
        xin = [msb(f"xin{i}", [128, 4, DIM]) for i in range(2)]
        xs = msb("xs", [128, TOK])
        sq, sq2 = msb("sq", [128, TOK]), msb("sq2", [128, TOK])
        rstd, rstd2 = msb("rstd", [128, TOK]), msb("rstd2", [128, TOK])
        h_mod = msb("h_mod", [128, TOK])
        sel = msb("sel", [96, 32, 128], BF16)
        w_in = msb("w_in", [128, 2 * INNER])
        w_x = msb("w_x", [128, HALVES, RANK + 2 * STATE])
        w_dt = msb("w_dt", [RANK, INNER])
        w_out = msb("w_out", [128, HALVES, DIM])
        ub = msb("ub", [128, HALVES, 2, TAPS - 1 + SEQ])
        cv = msb("cv", [128, HALVES, 2, SEQ])
        dr_rest = msb("dr_rest", [96, TOK])
        dr, rest = dr_rest[0:RANK, :], dr_rest[64:96, :]
        parts = [msb(f"parts{i}", [96, TOK], BF16) for i in range(2)]
        sp_abs = msb("sp_abs", [128, TOK])
        sp_ln = msb("sp_ln", [128, HALVES, TOK])
        delta = [msb(f"delta{i}", [128, HALVES, TOK]) for i in range(2)]
        du = [msb(f"du{i}", [128, HALVES, TOK]) for i in range(2)]
        dA = [msb(f"dA{i}", [128, HALVES, 2, SEQ]) for i in range(2)]
        hst = [msb(f"hst{i}", [128, HALVES, TOK]) for i in range(RING)]
        cs = [msb(f"cs{i}", [128, TOK]) for i in range(2)]
        z = msb("z", [128, HALVES, TOK])

        FIRST = [
            (ident[:, :], a["c_ident"]), (cond[:, :], a["c"]), (wmod[:, :], a["wmod"]),
            (center[:, :], a["c_center"]), (w_in[:, :], a["W_in"]),
        ]
        WLOADS = [
            (rope[:, :, :, :], a["c_rope"].rearrange("p (b k d) -> p b k d", b=2, k=4)),
            (conv_w[:, :, :], a["conv_w"].rearrange("(h p) k -> p h k", p=128)),
            (conv_b[:, :], a["conv_b"].rearrange("(h p) -> p h", p=128)),
            (w_x[:, :, :], a["W_x"].rearrange("(h p) k -> p h k", p=128)),
            (w_dt[:, :], a["W_dt"]),
            (b_dt[:, :], a["b_dt"].rearrange("(h p) -> p h", p=128)),
            (a_neg[:, :, :], a["A_log"].rearrange("(h p) k -> p h k", p=128)),
            (skip_d[:, :], a["D"].rearrange("(h p) -> p h", p=128)),
            (w_out[:, :, :], a["W_out"].rearrange("(h p) k -> p h k", p=128)),
            (wqkv[:, :, :], a["wqkv"].rearrange("l p n -> p l n")),
            (wo[:, :, :, :], a["wo"].rearrange("l (k p) n -> p l k n", p=128)),
            (ln_g[:, :], a["ln_g"].rearrange("l p -> p l")),
            (ln_b[:, :], a["ln_b"].rearrange("l p -> p l")),
            (w1[:, :, :], a["w1"].rearrange("l p n -> p l n")),
            (b2[:, :], a["b2"].rearrange("l p -> p l")),
            (qks[:, :, 0, :], a["q_scale"].partition_broadcast(128)),
            (qks[:, :, 1, :], a["k_scale"].partition_broadcast(128)),
            (w2[:, 0, 0:2, :], a["w2"][0, 0:256, :].rearrange("(k p) n -> p k n", p=128)),
            (w2[:, 1, 0:2, :], a["w2"][1, 0:256, :].rearrange("(k p) n -> p k n", p=128)),
            (w2[0:HID - 256, :, 2, :], a["w2"][:, 256:HID, :].rearrange("l p n -> p l n")),
        ]
        for s in range(2):
            for layer in range(DEPTH):
                at = s * HID
                WLOADS.append((b1[:, layer, s, 0:2],
                               a["b1"][layer, at:at + 256].rearrange("(j p) -> p j", p=128)))
                WLOADS.append((b1[0:HID - 256, layer, s, 2:3],
                               a["b1"][layer, at + 256:at + HID].rearrange("(p j) -> p j", j=1)))
        CASTS = [(sel[:, :, :], a["c_sel"].rearrange("p (n m) -> p n m", n=32)),
                 (mask[:, :, :], a["c_mask"].rearrange("p (t m) -> p t m", t=2)),
                 (identb[:, :], a["c_ident"])]
        ALL_FIRST, ALL_W = 16 * len(FIRST), 16 * len(WLOADS)
        pA, pB = psum[0], psum[1]
        bB, bC, pE, yp = psum[2:4], psum[4], psum[5], psum[6:8]

        (xT_done, xs_done, cen_done, sq_done, var_done, ln_done, rstd_done, hn_done, h_done,
         u_done, ub_done, res_done, sr_done, cv0_done, conv_step, cv_done, us_done, xdbl_done, dr_done,
         hi_done, rest_done, mid_done, split_done, dt_done, abs_done, exp_done, spl_done, pos_done,
         delta_done, du_done, bcB_done, bcC_done, dA_done, dBu_done, scan_done, cs_done, hc_done,
         y_done, yd_done, z_done, out_done, xn_done, x1_done, cen2_done, sq2_done, var2_done,
         ln2_done, rstd2_done, hn2_done, xf_done) = [event(n) for n in (
             "xT xs cen sq var ln rstd hn h u ub res sr cv0 conv cv us xdbl dr hi rest mid split dt abs "
             "exp spl pos delta du bcB bcC dA dBu scan cs hc y yd z out xn x1 cen2 sq2 var2 ln2 "
             "rstd2 hn2 xf").split()]

        block = ctx.enter_context(nc.Block())

        m_ctx.close()
        hf = sb("hf", [128, BATCH * SEQ])
        hT = [sb(f"hT{i}", [128, SEQ]) for i in range(2)]
        hs = sb("hs", [128, SEQ])
        vs = [sb(f"vs{i}", [128, 3, HEADS, DH + 1]) for i in range(2)]
        a_ctx = ExitStack()

        def asb(name, shape, dt=FP32):
            return a_ctx.enter_context(nc.sbuf_tensor(name, shape, dt))

        sqk = [asb(f"sqk{i}", [128, 2 * QKV]) for i in range(2)]
        ss = asb("ss", [128, 2 * HEADS])
        ssm = asb("ssm", [128, 2 * HEADS])
        ln_ss = asb("ln_ss", [128, 2 * HEADS])
        rn_est = asb("rn_est", [128, 2 * HEADS])
        rn_step = asb("rn_step", [128, 2 * HEADS])
        rn = [[asb(f"rn{i}{t}", [128, 2 * HEADS]) for t in range(2)] for i in range(2)]
        rot_a = [asb(f"rot_a{i}", [128, 2, QKV]) for i in range(2)]
        rot_b = [asb(f"rot_b{i}", [128, 2, QKV]) for i in range(2)]
        qT = [asb(f"qT{i}", [128, 4, SEQ]) for i in range(2)]
        kT = [asb(f"kT{i}", [128, 4, SEQ]) for i in range(2)]
        mx = [asb(f"mx{i}", [128, 4]) for i in range(2)]
        nb = [asb(f"nb{i}", [128, 4]) for i in range(2)]
        pr = [asb(f"pr{i}", [128, 4, 128]) for i in range(2)]
        pT = [asb(f"pT{i}", [128, 4, 128]) for i in range(2)]
        rd = [asb(f"rd{i}", [128, 4]) for i in range(2)]
        on = [asb(f"on{i}", [128, QKV]) for i in range(2)]
        oT = [asb(f"oT{i}", [128, 4, SEQ]) for i in range(2)]
        a_sq = asb("a_sq", [128, SEQ])
        a_rstd = asb("a_rstd", [128, SEQ])
        a_hn = asb("a_hn", [128, SEQ])
        front, tb, sc, op = psum[0:2], psum[2:4], psum[4:6], psum[6:8]
        (ht_done, qk_done, sqk_done, ss_done, ssm_done, lss_done, est_done, step_done, rn_done, rot_done, add_done, kn_done,
         tq_done, qT_done, kT_done, v_done, vs_done, s_done, mx_done, nb_done, p_done, tp_done,
         pT_done, o_done, rd_done, on_done, to_done, oT_done, wo_done, xr_done, hs_done, ac_done,
         asq_done, avar_done, aln_done, arstd_done, ahn_done, hf_done) = [
             event("a_" + n) for n in (
                 "ht qk sqk ss ssm lss est step rn rot add kn tq qT kT v vs s mx nb p tp pT o rd on to oT wo xr "
                 "hs ac asq avar aln arstd ahn hf").split()]
        a_ctx.close()

        f_ctx = ExitStack()

        def fsb(name, shape, dt=FP32):
            return f_ctx.enter_context(nc.sbuf_tensor(name, shape, dt))

        ge = [fsb(f"ge{i}", [128, TOK]) for i in range(2)]
        mid = [fsb(f"mid{i}", [128, TOK]) for i in range(3)]
        fo = fsb("fo", [128, TOK])
        so = [fsb(f"so{i}", [128, 4, DIM]) for i in range(2)]
        gp, ap_, rp, tp = psum[0:2], psum[2:4], psum[4:6], psum[6]
        (g_done, ge_done, mid_done_f, w2_done, xo_done, fo_done, fT_done, so_done) = [
            event("f_" + n) for n in "g ge mid w2 xo fo fT so".split()]
        f_ctx.close()

        def tokens(buf, pair):
            return buf[:, bass.ds(pair * TOK, TOK)]

        def seqs(buf):
            return buf.rearrange("p (b s) -> p b s", b=2)

        @block.sync
        def _(sp):
            for s in loop_sems:
                sp.sem_inc(s, CREDIT)
            def load_x(pair, par):
                sp.dma_start(xin[par][:, :, :],
                             x_rows[bass.ds(pair * TOK, TOK), :].rearrange("(t p) d -> p t d", p=128)
                             ).then_inc(s_x[par], 16)

            for dst, src in FIRST:
                sp.dma_start(dst, src).then_inc(s_first, 16)
            for par in range(2):
                load_x(par, par)
            with nc.allow_non_contiguous_dma(reason="short vectors put one element on a partition, once"):
                for dst, src in WLOADS:
                    sp.dma_start(dst, src).then_inc(s_w, 16)
            with sp.Fori(1, PAIRS // 2) as i:
                for par in range(2):
                    sp.wait_ge(xT_done, ev(2 * i + (par - 1)))
                    load_x(2 * i + par, par)
            with sp.Fori(0, PAIRS // 2) as i:
                for par in range(2):
                    pair = 2 * i + par
                    sp.wait_ge(so_done, ev(pair + 1))
                    sp.dma_start(out_rows[bass.ds(pair * TOK, TOK), :].rearrange("(t p) d -> p t d", p=128),
                                 so[par][:, :, :]).then_inc(s_out[par], 16)
            for par in range(2):
                sp.wait_ge(s_out[par], ev(16 * (PAIRS // 2)))

        @block.gpsimd
        def _(pool):
            for dst, src in CASTS:
                pool.dma_start(dst, src).then_inc(s_cast, 16)
            pool.memset(mean_w[:, :], 1.0 / DIM)
            pool.memset(eps[:, :], EPS)
            pool.memset(rn_shift[:, :], 0.5 * SS_BITS * math.log(2.0))
            for k, scale in enumerate((QK_SCALE, 1.0)):
                pool.memset(newton_a[:, k * HEADS:(k + 1) * HEADS], -0.5 * scale)
                pool.memset(newton_b[:, k * HEADS:(k + 1) * HEADS], 1.5 * scale)
            pool.memset(ub[:, :, :, :], 0.0)
            pool.memset(dA[0][:, :, :, :], 0.0)
            pool.memset(dA[1][:, :, :, :], 0.0).then_inc(s_set_pool, 1)

            def head_delta(f, par, k):
                pool.wait_ge(pos_done, ev(f * 2 + k + 1))
                pool.wait_ge(spl_done, ev(f * 2 + k + 1))
                pool.tensor_tensor(delta[par][:, k, :], delta[par][:, k, :], sp_ln[:, k, :],
                                   ALU.add).then_inc(delta_done, 1)

            def tail_gate(e, par):
                pool.wait_ge(yd_done, ev(e + 1))
                pool.tensor_tensor(z[:, :, :], z[:, :, :], sr[par][:, :, :], ALU.mult).then_inc(z_done, 1)

            def head_keep(f):
                pool.wait_ge(xs_done, ev(f + 1))
                pool.tensor_copy(tokens(x1, f), xs[:, :]).then_inc(x1_done, 1)

            def mamba(pair, par, tail, head):
                for n in range(STATE):
                    g = pair * STATE + n
                    if head and n in (12, 13):
                        head_delta(pair + 1, 1 - par, n - 12)
                    pool.wait_ge(scan_done, ev(g + 1))
                    pool.wait_ge(cs_done, ev(g + 1))
                    tile = hst[n % RING][:, :, :]
                    pool.tensor_tensor(tile, tile, cs[n % 2][:, :].unsqueeze(1).broadcast_to([128, HALVES, TOK]),
                                       ALU.mult).then_inc(hc_done, 1)
                    if tail and n == 2:
                        tail_gate(pair - 1, 1 - par)
                    if head and n == 5:
                        head_keep(pair + 1)

            head_keep(0)
            for k in range(HALVES):
                head_delta(0, 0, k)
            mamba(0, 0, False, True)
            with pool.Fori(0, PAIRS // 2 - 1) as i:
                for par in (1, 0):
                    mamba(2 * i + 2 - par, par, True, True)
            mamba(PAIRS - 1, 1, True, False)
            tail_gate(PAIRS - 1, 1)
            pool.wait_ge(xf_done, ev(PAIRS))
            for k in range(2):
                pool.memset(hT[k][:, 0:1], 0.0)
                pool.memset(vs[k][:, :, :, DH:DH + 1], 1.0)
            pool.memset(hs[:, 0:1], 0.0).then_inc(s_set_pool, 1)
            for layer in range(DEPTH):
                with pool.Fori(0, BATCH // 2) as i:
                    for par in range(2):
                        f = 2 * i + (layer * BATCH + par)
                        for t in range(2):
                            e = f * 2 + t
                            for c in range(2):
                                pool.wait_ge(rot_done, ev(e * 2 + c + 1))
                                pool.tensor_tensor(rot_a[t][:, c, :], rot_a[t][:, c, :], rot_b[t][:, c, :],
                                                   ALU.add).then_inc(add_done, 1)
                            pool.wait_ge(est_done, ev(e + 1))
                            pool.wait_ge(rn_done, ev(e))
                            pool.tensor_tensor(rn_step[:, :], rn_est[:, :], rn_est[:, :],
                                               ALU.mult).then_inc(step_done, 1)
                            for n, other in enumerate((ssm, newton_a, newton_b)):
                                pool.wait_ge(step_done, ev(e * 4 + n + 1))
                                pool.tensor_tensor(rn_step[:, :], rn_step[:, :], other[:, :],
                                                   ALU.add if n == 2 else ALU.mult).then_inc(step_done, 1)
                            pool.wait_ge(step_done, ev(e * 4 + 4))
                            pool.wait_ge(p_done, ev(4 * f - 6 + 2 * t))
                            pool.wait_ge(kn_done, ev(e - 3))
                            pool.tensor_tensor(rn[par][t][:, :], rn_est[:, :], rn_step[:, :],
                                               ALU.mult).then_inc(rn_done, 1)
                            pool.wait_ge(add_done, ev(e * 2 + 2))
                            pool.wait_ge(rn_done, ev(e + 1))
                            k3 = rot_a[t][:, 1, :].rearrange("p (h d) -> p h d", h=HEADS)
                            pool.tensor_tensor(
                                k3, k3, rn[par][t][:, HEADS:].unsqueeze(2).broadcast_to([128, HEADS, DH]),
                                ALU.mult).then_inc(kn_done, 1)

        @block.scalar
        def _(act):
            act.wait_ge(s_mod, 1)
            act.activation(condT[:, :], psum[0][:, 0:BATCH], ACT.Silu).then_inc(s_set_act, 1)
            act.preload_act_table_set("natural_log_exp_and_others")
            act.wait_ge(s_set_pool, 1)

            def state(pair, par, n):
                g = pair * STATE + n
                r = n % 2
                after(act, scan_done, g - 1)
                for k in range(HALVES):
                    last = act.activation(dA[r][:, k, :, 1:], seqs(delta[par][:, k, :])[:, :, 1:],
                                          ACT.Exp, scale=a_neg[:, k, n:n + 1])
                last.then_inc(dA_done, 1)
                act.wait_ge(bcC_done, ev(g + 1))
                after(act, hc_done, g - 1)
                act.activation(cs[r][:, :], bC[:, :], ACT.Copy).then_inc(cs_done, 1)

            def head_x(f):
                act.wait_ge(xT_done, ev(f + 1))
                after(act, x1_done, f)
                after(act, cen_done, f)
                act.activation(xs[:, :], pA[:, :], ACT.Copy).then_inc(xs_done, 1)

            def head_square(f):
                act.wait_ge(cen_done, ev(f + 1))
                act.activation(sq[:, :], pB[:, :], ACT.Square).then_inc(sq_done, 1)

            def head_rstd(f):
                act.wait_ge(var_done, ev(f + 1))
                after(act, hn_done, f)
                act.activation(rstd[:, :], pA[:, :], ACT.Ln, bias=eps[:, 0:1]).then_inc(ln_done, 1)
                act.wait_ge(ln_done, ev(f + 1))
                act.activation(rstd[:, :], rstd[:, :], ACT.Exp, scale=-0.5).then_inc(rstd_done, 1)

            def head_u(f):
                for k in range(HALVES):
                    act.wait_ge(u_done, ev(f * 2 + k + 1))
                    after(act, cv_done, f * 2 - 1 + k)
                    act.activation(ub[:, k, :, TAPS - 1:], seqs((pA, pB)[k][:, :]),
                                   ACT.Copy).then_inc(ub_done, 1)

            def head_tap(f):
                for k in range(HALVES):
                    act.wait_ge(ub_done, ev(f * 2 + k + 1))
                    act.activation(cv[:, k, :, :], ub[:, k, :, 0:SEQ], ACT.Identity,
                                   scale=conv_w[:, k, 0:1], bias=conv_b[:, k:k + 1]).then_inc(cv0_done, 1)

            def head_silu(f, par):
                for k in range(HALVES):
                    act.wait_ge(res_done, ev(f * 2 + k + 1))
                    after(act, z_done, f - 1)
                    act.activation(sr[par][:, k, :], (pA, pB)[k][:, :], ACT.Silu).then_inc(sr_done, 1)
                for k in range(HALVES):
                    act.wait_ge(cv_done, ev(f * 2 + k + 1))
                    after(act, yd_done, f - 1)
                    act.activation(us[par][:, k, :], cv[:, k, :, :].rearrange("p b s -> p (b s)"),
                                   ACT.Silu).then_inc(us_done, 1)
                act.preload_act_table_set("natural_log_exp_and_others")

            def head_rank(f, par):
                act.wait_ge(xdbl_done, ev(f + 1))
                after(act, dt_done, 2 * f)
                act.activation(dr, pA[0:RANK, :], ACT.Copy).then_inc(dr_done, 1)
                after(act, bcC_done, (f - 1) * STATE)
                act.activation(parts[par][0:32, :], pA[RANK:RANK + 2 * STATE, :], ACT.Copy).then_inc(hi_done, 1)

            def head_softplus(f, par, k):
                e = f * 2 + k
                after(act, dA_done, (f - 1) * STATE)
                after(act, du_done, f - 1)
                act.wait_ge(dt_done, ev(e + 1))
                after(act, spl_done, e)
                act.activation(sp_abs[:, :], (pB, pA)[k][:, :], ACT.Abs,
                               bias=b_dt[:, k:k + 1]).then_inc(abs_done, 1)
                act.activation(delta[par][:, k, :], (pB, pA)[k][:, :], ACT.Relu,
                               bias=b_dt[:, k:k + 1]).then_inc(pos_done, 1)
                act.wait_ge(abs_done, ev(e + 1))
                act.activation(sp_abs[:, :], sp_abs[:, :], ACT.Exp, scale=-1.0).then_inc(exp_done, 1)
                act.wait_ge(exp_done, ev(e + 1))
                after(act, delta_done, f * 2)
                act.activation(sp_ln[:, k, :], sp_abs[:, :], ACT.Ln, bias=1.0).then_inc(spl_done, 1)

            def tail_square(e):
                act.wait_ge(cen2_done, ev(e + 1))
                after(act, xf_done, e)
                act.activation(sq2[:, :], pE[:, :], ACT.Square).then_inc(sq2_done, 1)

            def tail_rstd(e):
                act.wait_ge(var2_done, ev(e + 1))
                after(act, hn2_done, e)
                act.activation(rstd2[:, :], pB[:, :], ACT.Ln, bias=eps[:, 0:1]).then_inc(ln2_done, 1)
                act.wait_ge(ln2_done, ev(e + 1))
                act.activation(rstd2[:, :], rstd2[:, :], ACT.Exp, scale=-0.5).then_inc(rstd2_done, 1)

            def mamba(pair, par, tail, head):
                act.wait_ge(delta_done, ev(pair * 2 + 2))
                for n in range(STATE):
                    state(pair, par, n)
                    if head and n == 1:
                        head_x(pair + 1)
                    if head and n == 2:
                        head_square(pair + 1)
                    if head and n == 3:
                        head_rstd(pair + 1)
                    if head and n == 5:
                        head_u(pair + 1)
                        head_tap(pair + 1)
                    if head and n == 7:
                        head_silu(pair + 1, 1 - par)
                    if tail and n == 8:
                        tail_square(pair - 1)
                    if head and n == 10:
                        head_rank(pair + 1, 1 - par)
                    if tail and n == 10:
                        tail_rstd(pair - 1)
                    if head and n in (11, 12):
                        head_softplus(pair + 1, 1 - par, n - 11)

            head_x(0)
            head_square(0)
            head_rstd(0)
            head_u(0)
            act.wait_ge(s_w, ALL_W)
            act.activation(a_neg[:, :, :], a_neg[:, :, :], ACT.Exp).then_inc(s_set_act, 1)
            head_tap(0)
            act.wait_ge(s_set_dve, SET_DVE)
            head_silu(0, 0)
            head_rank(0, 0)
            for k in range(HALVES):
                head_softplus(0, 0, k)
            mamba(0, 0, False, True)
            with act.Fori(0, PAIRS // 2 - 1) as i:
                for par in (1, 0):
                    mamba(2 * i + 2 - par, par, True, True)
            mamba(PAIRS - 1, 1, True, False)
            tail_square(PAIRS - 1)
            tail_rstd(PAIRS - 1)

            def squares(f, t):
                act.wait_ge(qk_done, ev(f * 2 + t + 1))
                after(act, ss_done, f * 2 + t - 1)
                for c in range(2):
                    last = act.activation(sqk[t][:, c * QKV:(c + 1) * QKV], front[c][:, :], ACT.Square)
                last.then_inc(sqk_done, 1)

            def norms(f, t):
                e = f * 2 + t
                act.wait_ge(ssm_done, ev(e + 1))
                after(act, est_done, e)
                act.activation(ln_ss[:, :], ssm[:, :], ACT.Ln, scale=2.0 ** SS_BITS).then_inc(lss_done, 1)
                act.wait_ge(lss_done, ev(e + 1))
                after(act, rn_done, e)
                act.activation(rn_est[:, :], ln_ss[:, :], ACT.Exp, scale=-0.5,
                               bias=rn_shift[:, 0:1]).then_inc(est_done, 1)

            def keep_T(kept, events, f, par, t, bank, nth):
                act.wait_ge(tq_done, ev(nth))
                after(act, s_done, 4 * (f - 1))
                act.activation(kept[par][:, :, t * 128:(t + 1) * 128],
                               tb[bank][:, :].rearrange("p (k c) -> p k c", k=4), ACT.Copy).then_inc(events, 1)

            def keep_v(f, par, t):
                act.wait_ge(v_done, ev(f * 2 + t + 1))
                after(act, o_done, 4 * (f - 1))
                v_tile = front[t][:, :].rearrange("p (h d) -> p h d", h=HEADS)
                near, there = slice(64 - 64 * t, 128 - 64 * t), slice(64 * t, 64 * t + 64)
                act.activation(vs[par][there, 1, :, 0:DH], v_tile[near, :, :], ACT.Copy)
                act.activation(vs[par][:, 2 * t, :, 0:DH], v_tile, ACT.Copy).then_inc(vs_done, 1)

            def exps(b, par, t, hp):
                e = b * 4 + 2 * t + hp
                act.wait_ge(nb_done, ev(e + 1))
                after(act, tp_done, e - 1)
                for k in range(4):
                    h = 2 * k + hp
                    last = act.activation(pr[hp][:, k, :], sc[hp][:, k * 128:(k + 1) * 128], ACT.Exp,
                                          scale=rn[par][t][:, h:h + 1], bias=nb[hp][:, k:k + 1])
                last.then_inc(p_done, 1)

            def keep_oT(b, par, t):
                act.wait_ge(to_done, ev(b * 2 + t + 1))
                after(act, wo_done, b - 1)
                act.activation(oT[par][:, :, t * 128:(t + 1) * 128],
                               tb[t][:, :].rearrange("p (k c) -> p k c", k=4), ACT.Copy).then_inc(oT_done, 1)

            def norm_square(e):
                act.wait_ge(ac_done, ev(e + 1))
                after(act, avar_done, e)
                act.activation(a_sq[:, :], op[1][:, 0:SEQ], ACT.Square).then_inc(asq_done, 1)

            def norm_rstd(e):
                act.wait_ge(avar_done, ev(e + 1))
                after(act, ahn_done, e)
                act.activation(a_rstd[:, :], op[0][:, 0:SEQ], ACT.Ln, bias=eps[:, 0:1]).then_inc(aln_done, 1)
                act.wait_ge(aln_done, ev(e + 1))
                act.activation(a_rstd[:, :], a_rstd[:, :], ACT.Exp, scale=-0.5).then_inc(arstd_done, 1)

            def attend(b, par, tail, head):
                f = b + 1
                exps(b, par, 0, 0)
                if tail:
                    keep_oT(b - 1, 1 - par, 1)
                if head:
                    squares(f, 0)
                keep_T(kT, kT_done, b, par, 1, 0, 4 * b + 4)
                exps(b, par, 0, 1)
                if tail:
                    norm_square(b - 1)
                    norm_rstd(b - 1)
                exps(b, par, 1, 0)
                exps(b, par, 1, 1)
                if head:
                    norms(f, 0)
                    squares(f, 1)
                keep_oT(b, par, 0)
                if head:
                    keep_T(qT, qT_done, f, 1 - par, 0, 1, 4 * f + 1)
                    keep_T(kT, kT_done, f, 1 - par, 0, 0, 4 * f + 2)
                    keep_v(f, 1 - par, 0)
                    keep_v(f, 1 - par, 1)
                    norms(f, 1)
                    keep_T(qT, qT_done, f, 1 - par, 1, 1, 4 * f + 3)

            def keep_out(q, par):
                act.wait_ge(fT_done, ev(q + 1))
                act.wait_ge(s_out[par], ev(8 * (q - par)))
                act.activation(so[par][:, :, :].rearrange("p t d -> p (t d)"), tp[:, :],
                               ACT.Copy).then_inc(so_done, 1)

            def feed_forward(q, par, layer, out_before):
                pair = q + layer * PAIRS
                for j, (_, m) in enumerate(HID_BLOCKS):
                    e = pair * 3 + j
                    r = (par + j) % 2
                    act.wait_ge(g_done, ev(e + 1))
                    after(act, mid_done_f, e - 1)
                    act.activation(ge[r][0:m, :], gp[r][0:m, :], ACT.Gelu,
                                   bias=b1[0:m, layer, 1, j:j + 1]).then_inc(ge_done, 1)
                if out_before:
                    keep_out(q - 1, 1 - par)

            for layer in range(DEPTH):
                first, end = layer * BATCH, (layer + 1) * BATCH
                act.wait_ge(s_set_pool, 2)
                squares(first, 0)
                norms(first, 0)
                squares(first, 1)
                norms(first, 1)
                for t in range(2):
                    keep_v(first, 0, t)
                keep_T(qT, qT_done, first, 0, 0, 1, 4 * first + 1)
                keep_T(kT, kT_done, first, 0, 0, 0, 4 * first + 2)
                keep_T(qT, qT_done, first, 0, 1, 1, 4 * first + 3)
                attend(first, 0, False, True)
                with act.Fori(0, BATCH // 2 - 1) as i:
                    for par in (1, 0):
                        attend(2 * i + (first + 2 - par), par, True, True)
                attend(end - 1, 1, True, False)
                keep_oT(end - 1, 1, 1)
                norm_square(end - 1)
                norm_rstd(end - 1)
                act.preload_act_table_set("gelu_and_others")
                last_layer = layer == DEPTH - 1
                feed_forward(0, 0, layer, False)
                with act.Fori(0, PAIRS // 2 - 1) as i:
                    for par in (1, 0):
                        feed_forward(2 * i + 2 - par, par, layer, last_layer)
                feed_forward(PAIRS - 1, 1, layer, last_layer)
                if last_layer:
                    keep_out(PAIRS - 1, 1)
                act.preload_act_table_set("natural_log_exp_and_others")

        @block.vector
        def _(dve):
            dve.wait_ge(s_mod, 2)
            dve.tensor_copy(mod[:, :, :], psum[1][:, 0:6 * BATCH].rearrange("p (k b) -> p k b", k=6)
                            ).then_inc(s_set_dve, 1)
            dve.wait_ge(s_set_dve, 1)
            for n, k in enumerate((1, 4)):
                dve.tensor_scalar(mod[:, k, :], mod[:, k, :], 1.0, None, ALU.add).then_inc(s_set_dve, 1)
            for n, k in enumerate((2, 5)):
                dve.tensor_scalar(gate_abs[:, n, :], mod[:, k, :], -1.0, None, ALU.mult).then_inc(s_set_dve, 1)
                dve.tensor_scalar(gate_sign[:, n, :], mod[:, k, :], 0.0, 2.0, ALU.is_ge, ALU.mult)
            dve.wait_ge(s_set_dve, 5)
            for n, k in enumerate((2, 5)):
                dve.tensor_tensor(gate_abs[:, n, :], gate_abs[:, n, :], mod[:, k, :], ALU.max).then_inc(s_set_dve, 1)
            dve.wait_ge(s_set_dve, 7)
            dve.tensor_scalar(gate_abs[:, :, :], gate_abs[:, :, :], 0.25, None, ALU.max).then_inc(s_set_dve, 1)
            dve.wait_ge(s_set_dve, 8)
            dve.scalar_tensor_tensor(mod[:, 2:6:3, :], gate_sign[:, :, :], -1.0, gate_abs[:, :, :],
                                     ALU.add, ALU.mult).then_inc(s_set_dve, 1)
            dve.wait_ge(s_set_dve, MOD_DVE)
            dve.wait_ge(s_set_pool, 1)

            half = DH // 2

            def scalar_of(k, pair, j):
                return mod[:, k, bass.ds(pair * 2 + j, 1)]


            def head_norm(f):
                dve.wait_ge(rstd_done, ev(f + 1))
                after(dve, res_done, 2 * f)
                dve.tensor_tensor(h_mod[:, :], pB[:, :], rstd[:, :], ALU.mult).then_inc(hn_done, 1)
                dve.wait_ge(hn_done, ev(f + 1))
                for j in range(2):
                    cols = slice(j * SEQ, (j + 1) * SEQ)
                    last = dve.tensor_scalar(h_mod[:, cols], h_mod[:, cols], scalar_of(1, f, j),
                                             scalar_of(0, f, j), ALU.mult, ALU.add)
                last.then_inc(h_done, 1)

            def head_conv(f, k, tap):
                if tap == 1:
                    dve.wait_ge(cv0_done, ev(f * 2 + k + 1))
                else:
                    dve.wait_ge(conv_step, ev((f * 2 + k) * (TAPS - 2) + tap - 1))
                last = dve.scalar_tensor_tensor(cv[:, k, :, :], ub[:, k, :, tap:tap + SEQ],
                                                conv_w[:, k, tap:tap + 1], cv[:, k, :, :],
                                                ALU.mult, ALU.add)
                last.then_inc(cv_done if tap == TAPS - 1 else conv_step, 1)

            def head_split(f, par):
                bc = pA[RANK:RANK + 2 * STATE, :]
                dve.wait_ge(hi_done, ev(f + 1))
                dve.tensor_tensor(rest, bc, parts[par][0:32, :], ALU.subtract).then_inc(rest_done, 1)
                dve.wait_ge(rest_done, ev(f + 1))
                dve.tensor_copy(parts[par][64:96, :], rest).then_inc(mid_done, 1)
                dve.wait_ge(mid_done, ev(f + 1))
                dve.tensor_tensor(parts[par][32:64, :], rest, parts[par][64:96, :],
                                  ALU.subtract).then_inc(split_done, 1)

            def head_du(f, par):
                dve.wait_ge(delta_done, ev(f * 2 + 2))
                after(dve, us_done, f * 2 + 2)
                dve.tensor_tensor(du[par][:, :, :], delta[par][:, :, :], us[par][:, :, :],
                                  ALU.mult).then_inc(du_done, 1)

            def state(pair, par, n):
                g = pair * STATE + n
                r = n % 2
                dve.wait_ge(bcB_done, ev(g + 1))
                after(dve, y_done, g + 1 - RING)
                tile = hst[n % RING]
                dve.tensor_tensor(tile[:, :, :], du[par][:, :, :],
                                  bB[r][:, :].unsqueeze(1).broadcast_to([128, HALVES, TOK]),
                                  ALU.mult).then_inc(dBu_done, 1)
                dve.wait_ge(dBu_done, ev(g + 1))
                dve.wait_ge(dA_done, ev(g + 1))
                flat = tile[:, :, :].rearrange("p k s -> p (k s)")
                dve.tensor_tensor_scan(flat, dA[r][:, :, :, :].rearrange("p k b s -> p (k b s)"), flat,
                                       0.0, ALU.mult, ALU.add).then_inc(scan_done, 1)

            def tail_gate(e, par):
                dve.wait_ge(y_done, ev(e * STATE + STATE))
                after(dve, out_done, e)
                for k in range(HALVES):
                    last = dve.scalar_tensor_tensor(z[:, k, :], us[par][:, k, :], skip_d[:, k:k + 1],
                                                    yp[k][:, :], ALU.mult, ALU.add)
                last.then_inc(yd_done, 1)

            def tail_residual(e):
                dve.wait_ge(out_done, ev(e + 1))
                dve.wait_ge(x1_done, ev(e + 1))
                for j in range(2):
                    cur = x1[:, bass.ds(e * TOK + j * SEQ, SEQ)]
                    last = dve.scalar_tensor_tensor(cur, pE[:, j * SEQ:(j + 1) * SEQ], scalar_of(2, e, j),
                                                    cur, ALU.mult, ALU.add)
                last.then_inc(xn_done, 1)

            def tail_norm(e):
                dve.wait_ge(rstd2_done, ev(e + 1))
                dve.tensor_tensor(sq2[:, :], pE[:, :], rstd2[:, :], ALU.mult).then_inc(hn2_done, 1)
                dve.wait_ge(hn2_done, ev(e + 1))
                for j in range(2):
                    last = dve.tensor_scalar(xf[:, bass.ds(e * TOK + j * SEQ, SEQ)],
                                             sq2[:, j * SEQ:(j + 1) * SEQ], scalar_of(4, e, j),
                                             scalar_of(3, e, j), ALU.mult, ALU.add)
                last.then_inc(xf_done, 1)

            def mamba(pair, par, tail, head):
                dve.wait_ge(du_done, ev(pair + 1))
                for n in range(STATE):
                    state(pair, par, n)
                    if tail and n == 2:
                        tail_gate(pair - 1, 1 - par)
                    if head and n == 3:
                        head_norm(pair + 1)
                    if head and n in (5, 6):
                        for tap in range(1, TAPS):
                            head_conv(pair + 1, n - 5, tap)
                    if tail and n == 4:
                        tail_residual(pair - 1)
                    if head and n == 10:
                        head_split(pair + 1, 1 - par)
                    if tail and n == 11:
                        tail_norm(pair - 1)
                    if head and n == 14:
                        head_du(pair + 1, 1 - par)

            head_norm(0)
            dve.wait_ge(s_w, ALL_W)
            for layer in range(DEPTH):
                for c in range(2):
                    scale_of = qks[:, layer, c, :]
                    dve.tensor_tensor(tables[:, layer, :, 2 * c, :], rope[:, :, 2 * c, :],
                                      scale_of.unsqueeze(1).broadcast_to([128, 2, DH]), ALU.mult)
                    for s in range(2):
                        o = 1 - s
                        dve.tensor_tensor(tables[:, layer, :, 2 * c + 1, s * half:(s + 1) * half],
                                          rope[:, :, 2 * c + 1, s * half:(s + 1) * half],
                                          scale_of[:, o * half:(o + 1) * half].unsqueeze(1)
                                          .broadcast_to([128, 2, half]), ALU.mult)
            dve.wait_ge(s_set_act, 2)
            dve.tensor_scalar(a_neg[:, :, :], a_neg[:, :, :], -1.0, None, ALU.mult).then_inc(s_set_dve, 1)
            dve.wait_ge(s_set_dve, SET_DVE)
            for k in range(HALVES):
                for tap in range(1, TAPS):
                    head_conv(0, k, tap)
            head_split(0, 0)
            head_du(0, 0)
            mamba(0, 0, False, True)
            with dve.Fori(0, PAIRS // 2 - 1) as i:
                for par in (1, 0):
                    mamba(2 * i + 2 - par, par, True, True)
            mamba(PAIRS - 1, 1, True, False)
            tail_gate(PAIRS - 1, 1)
            tail_residual(PAIRS - 1)
            tail_norm(PAIRS - 1)

            def shifted(dst, b):
                dve.tensor_scalar(dst[0:64, :], xf[0:64, bass.ds(b * SEQ, SEQ)], 1.0, None, ALU.mult)
                return dve.tensor_scalar(dst[64:128, 1:SEQ], xf[64:128, bass.ds(b * SEQ, SEQ - 1)],
                                         1.0, None, ALU.mult)

            def shift_in(f, par, first):
                after(dve, v_done, 2 * (f - 1))
                shifted(hT[par], f - first).then_inc(ht_done, 1)

            def rotate(f, layer, t, c):
                e = f * 2 + t
                dve.wait_ge(sqk_done, ev(e + 1))
                after(dve, tq_done, 2 * e - 2)
                after(dve, add_done, 2 * e - 2)
                src = front[c][:, :].rearrange("p (h d) -> p h d", h=HEADS)
                table = tables[:, layer, t, 2 * c, :].unsqueeze(1).broadcast_to([128, HEADS, DH])
                dve.tensor_tensor(rot_a[t][:, c, :].rearrange("p (h d) -> p h d", h=HEADS),
                                  src, table, ALU.mult)
                for s in range(2):
                    o = 1 - s
                    table = tables[:, layer, t, 2 * c + 1, s * half:(s + 1) * half]
                    last = dve.tensor_tensor(
                        rot_b[t][:, c, :].rearrange("p (h d) -> p h d", h=HEADS)[:, :, s * half:(s + 1) * half],
                        src[:, :, o * half:(o + 1) * half],
                        table.unsqueeze(1).broadcast_to([128, HEADS, half]), ALU.mult)
                last.then_inc(rot_done, 1)

            def norm_sums(f, t):
                e = f * 2 + t
                after(dve, ssm_done, e)
                dve.tensor_reduce(ss[:, :], sqk[t][:, :].rearrange("p (h d) -> p h d", d=DH),
                                  AX.X, ALU.add).then_inc(ss_done, 1)
                dve.wait_ge(ss_done, ev(e + 1))
                after(dve, rn_done, e)
                dve.tensor_scalar(ssm[:, :], ss[:, :], 1e-24, None, ALU.max).then_inc(ssm_done, 1)

            def maxima(b, par, t, hp):
                e = b * 4 + 2 * t + hp
                dve.wait_ge(s_done, ev(e + 1))
                after(dve, nb_done, e - 1)
                dve.tensor_reduce(mx[hp][:, :], sc[hp][:, :].rearrange("p (k j) -> p k j", k=4),
                                  AX.X, ALU.max).then_inc(mx_done, 1)
                dve.wait_ge(mx_done, ev(e + 1))
                after(dve, p_done, e - 1)
                dve.wait_ge(rn_done, ev(b * 2 + t + 1))
                dve.scalar_tensor_tensor(nb[hp][:, :], mx[hp][:, :], -1.0,
                                         rn[par][t][:, hp:HEADS:2], ALU.mult, ALU.mult).then_inc(nb_done, 1)

            def keep_pT(b, t, hp):
                e = b * 4 + 2 * t + hp
                dve.wait_ge(tp_done, ev(e + 1))
                after(dve, o_done, e - 1)
                dve.tensor_copy(pT[hp][:, :, :].rearrange("p k j -> p (k j)"),
                                tb[hp][:, :]).then_inc(pT_done, 1)

            def normalise(b, t, hp):
                e = b * 4 + 2 * t + hp
                o4 = op[hp][:, 0:4 * (DH + 1)].rearrange("p (k d) -> p k d", k=4)
                dve.wait_ge(o_done, ev(e + 1))
                after(dve, on_done, e - 1)
                dve.reciprocal(rd[hp][:, :], o4[:, :, DH]).then_inc(rd_done, 1)
                dve.wait_ge(rd_done, ev(e + 1))
                after(dve, to_done, b * 2 + t - 1)
                dve.tensor_tensor(
                    on[t][:, :].rearrange("p (k s d) -> p k s d", k=4, s=2)[:, :, hp, :],
                    o4[:, :, 0:DH], rd[hp][:, :].unsqueeze(2).broadcast_to([128, 4, DH]),
                    ALU.mult).then_inc(on_done, 1)

            def residual(e, first):
                dve.wait_ge(wo_done, ev(e + 1))
                cur = xf[:, bass.ds((e - first) * SEQ, SEQ)]
                dve.tensor_tensor(cur, op[0][:, 0:SEQ], cur, ALU.add).then_inc(xr_done, 1)
                dve.wait_ge(xr_done, ev(e + 1))
                after(dve, ac_done, e)
                shifted(hs, e - first).then_inc(hs_done, 1)

            def norm_out(e, first, layer):
                dve.wait_ge(arstd_done, ev(e + 1))
                after(dve, hf_done, e)
                dve.tensor_tensor(a_hn[:, :], op[1][:, 0:SEQ], a_rstd[:, :], ALU.mult).then_inc(ahn_done, 1)
                dve.wait_ge(ahn_done, ev(e + 1))
                dve.tensor_scalar(hf[:, bass.ds((e - first) * SEQ, SEQ)], a_hn[:, :], ln_g[:, layer:layer + 1],
                                  ln_b[:, layer:layer + 1], ALU.mult, ALU.add).then_inc(hf_done, 1)

            def attend(b, par, first, layer, tail, head):
                f = b + 1
                if head:
                    shift_in(f, 1 - par, first)
                maxima(b, par, 0, 0)
                maxima(b, par, 0, 1)
                if head:
                    rotate(f, layer, 0, 0)
                if tail:
                    residual(b - 1, first)
                if head:
                    norm_sums(f, 0)
                keep_pT(b, 0, 0)
                keep_pT(b, 0, 1)
                maxima(b, par, 1, 0)
                if head:
                    rotate(f, layer, 0, 1)
                if tail:
                    norm_out(b - 1, first, layer)
                maxima(b, par, 1, 1)
                normalise(b, 0, 0)
                keep_pT(b, 1, 0)
                normalise(b, 0, 1)
                keep_pT(b, 1, 1)
                if head:
                    rotate(f, layer, 1, 0)
                    rotate(f, layer, 1, 1)
                    norm_sums(f, 1)
                normalise(b, 1, 0)
                normalise(b, 1, 1)

            def residual_out(q, par, layer):
                pair = q + layer * PAIRS
                dve.wait_ge(w2_done, ev(pair * 3 + 3))
                dve.scalar_tensor_tensor(tokens(xf, q), rp[par][:, :], b2[:, layer:layer + 1],
                                         tokens(xf, q), ALU.add, ALU.add).then_inc(xo_done, 1)
                if layer == DEPTH - 1:
                    dve.wait_ge(xo_done, ev(pair + 1))
                    after(dve, fT_done, q)
                    for j in range(2):
                        at = bass.ds(q * TOK + j * SEQ, SEQ)
                        last = dve.scalar_tensor_tensor(fo[:, j * SEQ:(j + 1) * SEQ], xf[:, at],
                                                        scalar_of(5, q, j), x1[:, at],
                                                        ALU.mult, ALU.add)
                    last.then_inc(fo_done, 1)

            def feed_forward(q, par, layer, before):
                for j, (_, m) in enumerate(HID_BLOCKS):
                    e = (q + layer * PAIRS) * 3 + j
                    r = (par + j) % 2
                    dve.wait_ge(ge_done, ev(e + 1))
                    after(dve, w2_done, e - 2)
                    dve.scalar_tensor_tensor(mid[j][0:m, :], ap_[r][0:m, :],
                                             b1[0:m, layer, 0, j:j + 1], ge[r][0:m, :],
                                             ALU.add, ALU.mult).then_inc(mid_done_f, 1)
                    if before and j == 1:
                        residual_out(q - 1, 1 - par, layer)

            dve.wait_ge(xf_done, ev(PAIRS))
            for layer in range(DEPTH):
                first, end = layer * BATCH, (layer + 1) * BATCH
                dve.wait_ge(s_set_pool, 2)
                if layer:
                    dve.wait_ge(xo_done, ev(PAIRS))
                shift_in(first, 0, first)
                for t in range(2):
                    rotate(first, layer, t, 0)
                    rotate(first, layer, t, 1)
                    norm_sums(first, t)
                attend(first, 0, first, layer, False, True)
                with dve.Fori(0, BATCH // 2 - 1) as i:
                    for par in (1, 0):
                        attend(2 * i + (first + 2 - par), par, first, layer, True, True)
                attend(end - 1, 1, first, layer, True, False)
                residual(end - 1, first)
                norm_out(end - 1, first, layer)
                feed_forward(0, 0, layer, False)
                with dve.Fori(0, PAIRS // 2 - 1) as i:
                    for par in (1, 0):
                        feed_forward(2 * i + 2 - par, par, layer, True)
                feed_forward(PAIRS - 1, 1, layer, True)
                residual_out(PAIRS - 1, 1, layer)

        @block.tensor
        def _(pe):
            pe.wait_ge(s_first, ALL_FIRST)
            pe.transpose(psum[0][:, 0:BATCH], cond[:, :], ident[0:32, 0:32]).then_inc(s_mod, 1)
            pe.wait_ge(s_set_act, 1)
            for k in range(6):
                last = pe.matmul(psum[1][:, k * BATCH:(k + 1) * BATCH], wmod[:, k * DIM:(k + 1) * DIM],
                                 condT[:, :], start=True, stop=True)
            last.then_inc(s_mod, 1)
            pe.wait_ge(s_set_dve, MOD_DVE)
            pe.wait_ge(s_set_pool, 1)


            def head_transpose(f, par, loads):
                pe.wait_ge(s_x[par], ev(16 * loads))
                after(pe, pos_done, 2 * f)
                for t in range(4):
                    last = pe.transpose(pA[:, t * 128:(t + 1) * 128], xin[par][:, t, :], ident[:, :])
                last.then_inc(xT_done, 1)

            def head_center(f):
                pe.wait_ge(xs_done, ev(f + 1))
                pe.matmul(pB[:, :], center[:, :], xs[:, :], start=True, stop=True).then_inc(cen_done, 1)

            def head_var(f):
                pe.wait_ge(sq_done, ev(f + 1))
                pe.matmul(pA[:, :], mean_w[:, :], sq[:, :], start=True, stop=True).then_inc(var_done, 1)

            def head_u(f):
                pe.wait_ge(h_done, ev(f + 1))
                for k in range(HALVES):
                    pe.matmul((pA, pB)[k][:, :], w_in[:, k * 128:(k + 1) * 128], h_mod[:, :],
                              start=True, stop=True).then_inc(u_done, 1)

            def head_res(f):
                for k in range(HALVES):
                    pe.wait_ge(ub_done, ev(f * 2 + k + 1))
                    pe.matmul((pA, pB)[k][:, :], w_in[:, INNER + k * 128:INNER + (k + 1) * 128],
                              h_mod[:, :], start=True, stop=True).then_inc(res_done, 1)

            def head_xdbl(f, par):
                pe.wait_ge(us_done, ev(f * 2 + 2))
                for k in range(HALVES):
                    last = pe.matmul(pA[0:RANK + 2 * STATE, :], w_x[:, k, :], us[par][:, k, :],
                                     start=(k == 0), stop=(k == HALVES - 1))
                last.then_inc(xdbl_done, 1)

            def head_dt(f):
                pe.wait_ge(dr_done, ev(f + 1))
                after(pe, ln2_done, f - 1)
                pe.matmul(pB[:, :], w_dt[:, 0:128], dr, start=True, stop=True).then_inc(dt_done, 1)
                pe.wait_ge(rest_done, ev(f + 1))
                pe.matmul(pA[:, :], w_dt[:, 128:256], dr, start=True, stop=True).then_inc(dt_done, 1)

            def tail_out(e):
                pe.wait_ge(z_done, ev(e + 1))
                after(pe, hn2_done, e)
                for k in range(HALVES):
                    last = pe.matmul(pE[:, :], w_out[:, k, :], z[:, k, :], start=(k == 0),
                                     stop=(k == HALVES - 1))
                last.then_inc(out_done, 1)

            def tail_center(e):
                pe.wait_ge(xn_done, ev(e + 1))
                pe.matmul(pE[:, :], center[:, :], tokens(x1, e), start=True, stop=True).then_inc(cen2_done, 1)

            def tail_var(e, head):
                pe.wait_ge(sr_done if head else pos_done, ev(2 * e + 6) if head else ev(2 * PAIRS))
                pe.wait_ge(sq2_done, ev(e + 1))
                pe.matmul(pB[:, :], mean_w[:, :], sq2[:, :], start=True, stop=True).then_inc(var2_done, 1)

            def broadcast(pair, par, n):
                g = pair * STATE + n
                r = n % 2
                after(pe, dBu_done, g - 1)
                pe.matmul(bB[r][:, :], sel[:, n, :], parts[par][:, :], start=True,
                          stop=True).then_inc(bcB_done, 1)
                after(pe, cs_done, g)
                pe.matmul(bC[:, :], sel[:, STATE + n, :], parts[par][:, :], start=True,
                          stop=True).then_inc(bcC_done, 1)

            def reduce_state(pair, n):
                if n == 0:
                    after(pe, yd_done, pair)
                pe.wait_ge(hc_done, ev(pair * STATE + n + 1))
                for k in range(HALVES):
                    last = pe.matmul(yp[k][:, :], ident[:, :], hst[n % RING][:, k, :],
                                     start=(n == 0), stop=(n == STATE - 1))
                last.then_inc(y_done, 1)

            def mamba(pair, par, tail, head, loads=None):
                pe.wait_ge(split_done, ev(pair + 1))
                broadcast(pair, par, 0)
                for n in range(STATE):
                    if n + 1 < STATE:
                        broadcast(pair, par, n + 1)
                    if head and n == 0:
                        head_transpose(pair + 1, 1 - par, loads)
                    if head and n == 1:
                        head_center(pair + 1)
                    if head and n == 2:
                        head_var(pair + 1)
                    if tail and n == 4:
                        tail_out(pair - 1)
                    if head and n == 4:
                        head_u(pair + 1)
                    if head and n == 6:
                        head_res(pair + 1)
                    if tail and n == 7:
                        tail_center(pair - 1)
                    if head and n == 9:
                        head_xdbl(pair + 1, 1 - par)
                    if tail and n == 9:
                        tail_var(pair - 1, head)
                    if head and n == 10:
                        head_dt(pair + 1)
                    if n >= LAG:
                        reduce_state(pair, n - LAG)
                    elif tail:
                        reduce_state(pair - 1, n - LAG + STATE)

            head_transpose(0, 0, 1)
            head_center(0)
            head_var(0)
            head_u(0)
            head_res(0)
            pe.wait_ge(s_w, ALL_W)
            head_xdbl(0, 0)
            head_dt(0)
            pe.wait_ge(s_cast, 16 * len(CASTS))
            mamba(0, 0, False, True, 1)
            with pe.Fori(0, PAIRS // 2 - 1) as i:
                for par in (1, 0):
                    mamba(2 * i + 2 - par, par, True, True, i + 2)
            mamba(PAIRS - 1, 1, True, False)
            for n in range(STATE - LAG, STATE):
                reduce_state(PAIRS - 1, n)
            tail_out(PAIRS - 1)
            tail_center(PAIRS - 1)
            tail_var(PAIRS - 1, False)

            def q_k(f, par, layer, t):
                pe.wait_ge(ht_done, ev(f + 1))
                for c in range(2):
                    if t:
                        pe.wait_ge(rot_done, ev(f * 4 + c + 1))
                    else:
                        after(pe, vs_done, 2 * f)
                    last = pe.matmul(front[c][:, :], hT[par][:, t * 128:(t + 1) * 128],
                                     wqkv[:, layer, c * QKV:(c + 1) * QKV], start=True, stop=True)
                last.then_inc(qk_done, 1)

            def v_rows(f, par, layer, t):
                pe.wait_ge(rot_done, ev(f * 4 + t + 3))
                pe.matmul(front[t][:, :], hT[par][:, t * 128:(t + 1) * 128],
                          wqkv[:, layer, 2 * QKV:3 * QKV], start=True, stop=True).then_inc(v_done, 1)

            def transpose_q(f, t, bank):
                pe.wait_ge(add_done, ev(f * 4 + 2 * t + 1))
                for k in range(4):
                    last = pe.transpose(tb[bank][:, k * 128:(k + 1) * 128],
                                        rot_a[t][:, 0, k * 128:(k + 1) * 128], ident[:, :])
                last.then_inc(tq_done, 1)

            def transpose_k(f, t, bank):
                pe.wait_ge(kn_done, ev(f * 2 + t + 1))
                for k in range(4):
                    last = pe.transpose(tb[bank][:, k * 128:(k + 1) * 128],
                                        rot_a[t][:, 1, k * 128:(k + 1) * 128], ident[:, :])
                last.then_inc(tq_done, 1)

            def scores(b, par, t, hp):
                e = b * 4 + 2 * t + hp
                rows = slice(64 * hp, 64 * hp + 64)
                after(pe, p_done, e - 1)
                pe.wait_ge(qT_done, ev(2 * b + 1 + t))
                pe.wait_ge(kT_done, ev(2 * b + 1 + t))
                pe.matmul(sc[hp][:, :], identb[:, :],
                          mask[:, t, :].unsqueeze(1).broadcast_to([128, 4, 128]),
                          start=True, stop=False, skip_group_check=True)
                for k in range(4):
                    cols = slice(k * 128, (k + 1) * 128)
                    if t == 0:
                        last = pe.matmul(sc[hp][:, cols], qT[par][rows, k, 0:128], kT[par][rows, k, 0:128],
                                         start=False, stop=True, skip_group_check=True)
                    else:
                        for w in range(2):
                            last = pe.matmul(sc[hp][64 * w:64 * w + 64, cols],
                                             qT[par][rows, k, 128 + 64 * w:192 + 64 * w],
                                             kT[par][rows, k, 64 + 64 * w:192 + 64 * w],
                                             start=False, stop=True, skip_group_check=True)
                last.then_inc(s_done, 1)

            def transpose_p(b, t, hp):
                e = b * 4 + 2 * t + hp
                pe.wait_ge(p_done, ev(e + 1))
                for k in range(4):
                    last = pe.transpose(tb[hp][:, k * 128:(k + 1) * 128], pr[hp][:, k, :], ident[:, :])
                last.then_inc(tp_done, 1)

            def values(b, par, t, hp):
                e = b * 4 + 2 * t + hp
                pe.wait_ge(pT_done, ev(e + 1))
                if t == 0:
                    after(pe, ahn_done, b)
                    pe.wait_ge(vs_done, ev(b * 2 + 2))
                after(pe, on_done, e - 1)
                for k in range(4):
                    h = 2 * k + hp
                    cols = slice(k * (DH + 1), (k + 1) * (DH + 1))
                    if t == 0:
                        last = pe.matmul(op[hp][:, cols], pT[hp][:, k, :], vs[par][:, 0, h, :],
                                         start=True, stop=True)
                    else:
                        for w in range(2):
                            last = pe.matmul(op[hp][64 * w:64 * w + 64, cols],
                                             pT[hp][:, k, 64 * w:64 * w + 64],
                                             vs[par][:, 1 + w, h, :], start=True, stop=True)
                last.then_inc(o_done, 1)

            def transpose_o(b, t):
                pe.wait_ge(on_done, ev(b * 4 + 2 * t + 2))
                for k in range(4):
                    last = pe.transpose(tb[t][:, k * 128:(k + 1) * 128],
                                        on[t][:, k * 128:(k + 1) * 128], ident[:, :])
                last.then_inc(to_done, 1)

            def project(e, par, layer):
                pe.wait_ge(on_done, ev(4 * e + 4))
                pe.wait_ge(oT_done, ev(e * 2 + 2))
                for k in range(4):
                    last = pe.matmul(op[0][:, 0:SEQ], wo[:, layer, k, :], oT[par][:, k, :],
                                     start=(k == 0), stop=(k == 3))
                last.then_inc(wo_done, 1)

            def norm_center(e):
                pe.wait_ge(hs_done, ev(e + 1))
                pe.matmul(op[1][:, 0:SEQ], center[:, :], hs[:, :], start=True, stop=True).then_inc(ac_done, 1)

            def norm_var(e):
                pe.wait_ge(asq_done, ev(e + 1))
                pe.matmul(op[0][:, 0:SEQ], mean_w[:, :], a_sq[:, :], start=True, stop=True).then_inc(avar_done, 1)

            def attend(b, par, layer, tail, head):
                f = b + 1
                scores(b, par, 0, 0)
                scores(b, par, 0, 1)
                if tail:
                    pe.wait_ge(qT_done, ev(2 * b + 2))
                    transpose_o(b - 1, 1)
                if head:
                    q_k(f, 1 - par, layer, 0)
                pe.wait_ge(kT_done, ev(2 * b + 1))
                transpose_k(b, 1, 0)
                if tail:
                    project(b - 1, 1 - par, layer)
                pe.wait_ge(kT_done, ev(2 * b + 2))
                transpose_p(b, 0, 0)
                if tail:
                    pe.wait_ge(oT_done, ev(2 * b))
                transpose_p(b, 0, 1)
                if tail:
                    norm_center(b - 1)
                scores(b, par, 1, 0)
                if tail:
                    norm_var(b - 1)
                scores(b, par, 1, 1)
                if head:
                    q_k(f, 1 - par, layer, 1)
                values(b, par, 0, 0)
                pe.wait_ge(pT_done, ev(4 * b + 1))
                transpose_p(b, 1, 0)
                values(b, par, 0, 1)
                pe.wait_ge(pT_done, ev(4 * b + 2))
                transpose_p(b, 1, 1)
                pe.wait_ge(pT_done, ev(4 * b + 3))
                transpose_o(b, 0)
                if head:
                    pe.wait_ge(pT_done, ev(4 * b + 4))
                    transpose_q(f, 0, 1)
                values(b, par, 1, 0)
                values(b, par, 1, 1)
                if head:
                    v_rows(f, 1 - par, layer, 0)
                    pe.wait_ge(oT_done, ev(2 * b + 1))
                    transpose_k(f, 0, 0)
                    v_rows(f, 1 - par, layer, 1)
                    pe.wait_ge(qT_done, ev(2 * f + 1))
                    transpose_q(f, 1, 1)

            def gate_rows(q, par, layer, j):
                e = (q + layer * PAIRS) * 3 + j
                at, m = HID_BLOCKS[j]
                r = (par + j) % 2
                after(pe, mid_done_f, e - 1)
                pe.matmul(gp[r][0:m, :], w1[:, layer, HID + at:HID + at + m], tokens(hf, q),
                          start=True, stop=True)
                pe.matmul(ap_[r][0:m, :], w1[:, layer, at:at + m], tokens(hf, q),
                          start=True, stop=True).then_inc(g_done, 1)

            def down(q, par, layer, j):
                pair = q + layer * PAIRS
                m = HID_BLOCKS[j][1]
                pe.wait_ge(mid_done_f, ev(pair * 3 + j + 1))
                if j == 0:
                    after(pe, xo_done, pair - 1)
                pe.matmul(rp[par][:, :], w2[0:m, layer, j, :], mid[j][0:m, :],
                          start=(j == 0), stop=(j == 2)).then_inc(w2_done, 1)

            def turn_out(q):
                pe.wait_ge(fo_done, ev(q + 1))
                after(pe, so_done, q)
                for t in range(4):
                    last = pe.transpose(tp[:, t * 128:(t + 1) * 128],
                                        fo[:, t * 128:(t + 1) * 128], ident[:, :])
                last.then_inc(fT_done, 1)

            def feed_forward(q, par, layer, before):
                gate_rows(q, par, layer, 0)
                gate_rows(q, par, layer, 1)
                if before:
                    down(q - 1, 1 - par, layer, 2)
                gate_rows(q, par, layer, 2)
                down(q, par, layer, 0)
                down(q, par, layer, 1)
                if before and layer == DEPTH - 1:
                    turn_out(q - 1)

            for layer in range(DEPTH):
                first, end = layer * BATCH, (layer + 1) * BATCH
                pe.wait_ge(s_set_pool, 2)
                q_k(first, 0, layer, 0)
                q_k(first, 0, layer, 1)
                for t in range(2):
                    v_rows(first, 0, layer, t)
                after(pe, oT_done, 2 * first)
                transpose_q(first, 0, 1)
                transpose_k(first, 0, 0)
                pe.wait_ge(qT_done, ev(2 * first + 1))
                transpose_q(first, 1, 1)
                attend(first, 0, layer, False, True)
                with pe.Fori(0, BATCH // 2 - 1) as i:
                    for par in (1, 0):
                        attend(2 * i + (first + 2 - par), par, layer, True, True)
                attend(end - 1, 1, layer, True, False)
                pe.wait_ge(pT_done, ev(4 * end))
                transpose_o(end - 1, 1)
                project(end - 1, 1, layer)
                norm_center(end - 1)
                norm_var(end - 1)
                pe.wait_ge(hf_done, ev((layer + 1) * BATCH))
                feed_forward(0, 0, layer, False)
                with pe.Fori(0, PAIRS // 2 - 1) as i:
                    for par in (1, 0):
                        feed_forward(2 * i + 2 - par, par, layer, True)
                feed_forward(PAIRS - 1, 1, layer, True)
                down(PAIRS - 1, 1, layer, 2)
                if layer == DEPTH - 1:
                    turn_out(PAIRS - 1)


_NAMES = {
    "L0_attn_x": "x", "L0_attn_W_in": "W_in", "L0_attn_conv_w": "conv_w", "L0_attn_conv_b": "conv_b",
    "L0_attn_W_x": "W_x", "L0_attn_W_dt": "W_dt", "L0_attn_b_dt": "b_dt", "L0_attn_A_log": "A_log",
    "L0_attn_D": "D", "L0_attn_W_out": "W_out", "L0_ffn_wqkv": "wqkv", "L0_ffn_q_scale": "q_scale",
    "L0_ffn_k_scale": "k_scale", "L0_ffn_wo": "wo", "L0_ffn_ln_g": "ln_g", "L0_ffn_ln_b": "ln_b",
    "L0_ffn_w1": "w1", "L0_ffn_b1": "b1", "L0_ffn_w2": "w2", "L0_ffn_b2": "b2", "L0_c": "c",
    "L0_wmod": "wmod",
}


def kernel(**inputs):
    import numpy as _np
    import concourse.bacc as _bacc
    from concourse import mybir as _mybir
    from concourse.bass_utils import run_bass_kernel_spmd as _run

    nc = _bacc.Bacc("TRN2", target_bir_lowering=False, num_devices=1)
    arrays, args = {}, {}
    given = {short: _np.ascontiguousarray(inputs[name]) for name, short in _NAMES.items()}
    given.update(shape_constants())
    for short, a in given.items():
        arrays[f"in_{short}"] = a
        args[short] = nc.dram_tensor(f"in_{short}", a.shape, _mybir.dt.from_np(a.dtype),
                                     kind="ExternalInput").ap()
    out = nc.dram_tensor("out_0", (BATCH, SEQ, DIM), _mybir.dt.float32, kind="ExternalOutput").ap()
    block_kernel(nc, args, out)
    r = _run(nc, [arrays], core_ids=[0])
    return r.results[0]["out_0"]
```
